# Optimizing a Trainium2 kernel written in Bass

```python
import numpy as np
import jax
import jax.numpy as jnp

def _softmax(x, axis=-1):
    return jax.nn.softmax(x, axis=axis)

def _gelu(x):
    return jax.nn.gelu(x, approximate=True)

def _silu(x):
    return jax.nn.silu(x)

def _sigmoid(x):
    return jax.nn.sigmoid(x)

def _layernorm(x, axis=-1, eps=1e-05):
    m = jnp.mean(x, axis=axis, keepdims=True)
    v = jnp.var(x, axis=axis, keepdims=True)
    return (x - m) / jnp.sqrt(v + eps)

def _scatter_add(tgt, idx, src, axis=0):
    return tgt.at[idx].add(src)

def _segment_sum(src, seg, n):
    return jax.ops.segment_sum(src, seg, n)
kernel_name = 'mk_macaron_d1_jaxref_r8_b923ff'

def setup_inputs(seed: int=0):
    np.random.seed(seed)
    _w = jnp.asarray

    def _L0_attn_setup():
        import jax, jax.numpy as jnp
        import numpy as np
        D_MODEL = 128
        D_STATE = 128
        D_CONV = 4
        EXPAND = 2
        HEADDIM = 64
        D_INNER = EXPAND * D_MODEL
        NHEADS = D_INNER // HEADDIM
        CONV_DIM = D_INNER + 2 * D_STATE
        D_IN_PROJ = 2 * D_INNER + 2 * D_STATE + NHEADS
        CHUNK = 64
        BATCH, SEQ = (2, 512)
        EPS = 1e-06

        def rmsnorm(x, w):
            return x * jax.lax.rsqrt(jnp.mean(x * x, axis=-1, keepdims=True) + EPS) * w

        def segsum(a):
            cs = jnp.cumsum(a, axis=-1)
            ss = cs[..., :, None] - cs[..., None, :]
            T = a.shape[-1]
            mask = jnp.tril(jnp.ones((T, T), dtype=bool))
            return jnp.where(mask, ss, -jnp.inf)

        def ssd(x, A, B, C, chunk):
            b, l, h, p = x.shape
            c = l // chunk
            x = x.reshape(b, c, chunk, h, p)
            A = A.reshape(b, c, chunk, h).transpose(0, 3, 1, 2)
            B = B.reshape(b, c, chunk, -1)
            C = C.reshape(b, c, chunk, -1)
            A_cs = jnp.cumsum(A, axis=-1)
            L = jnp.exp(segsum(A))
            Y_diag = jnp.einsum('bcln,bcsn,bhcls,bcshp->bclhp', C, B, L, x)
            decay_states = jnp.exp(A_cs[..., -1:] - A_cs)
            states = jnp.einsum('bcln,bhcl,bclhp->bchpn', B, decay_states, x)
            A_chunk = jnp.pad(A_cs[..., -1], ((0, 0), (0, 0), (1, 0)))
            decay_chunk = jnp.exp(segsum(A_chunk))
            states_cat = jnp.concatenate([jnp.zeros_like(states[:, :1]), states], axis=1)
            new_states = jnp.einsum('bhzc,bchpn->bzhpn', decay_chunk, states_cat)
            prev_states = new_states[:, :-1]
            state_decay = jnp.exp(A_cs)
            Y_off = jnp.einsum('bcln,bchpn,bhcl->bclhp', C, prev_states, state_decay)
            return (Y_diag + Y_off).reshape(b, l, h, p)

        def mamba2(u, in_proj_w, conv_w, conv_b, dt_bias, A_log, D_param, ssm_norm_w, out_proj_w):
            b, l, _ = u.shape
            zxbcdt = jnp.einsum('bld,ed->ble', u, in_proj_w)
            z = zxbcdt[..., :D_INNER]
            xBC = zxbcdt[..., D_INNER:D_INNER + CONV_DIM]
            dt = zxbcdt[..., D_INNER + CONV_DIM:]
            xpad = jnp.pad(xBC, ((0, 0), (D_CONV - 1, 0), (0, 0)))
            xc = conv_b
            conv = sum((conv_w[:, k] * xpad[:, k:k + l, :] for k in range(D_CONV))) + conv_b
            xBC = jax.nn.silu(conv)
            x = xBC[..., :D_INNER]
            Bm = xBC[..., D_INNER:D_INNER + D_STATE]
            Cm = xBC[..., D_INNER + D_STATE:]
            dt = jax.nn.softplus(dt + dt_bias)
            A = -jnp.exp(A_log)
            xh = x.reshape(b, l, NHEADS, HEADDIM)
            y = ssd(xh * dt[..., None], A * dt, Bm, Cm, CHUNK)
            y = y + D_param[None, None, :, None] * xh
            y = y.reshape(b, l, D_INNER)
            y = rmsnorm(y * jax.nn.silu(z), ssm_norm_w)
            return jnp.einsum('ble,de->bld', y, out_proj_w)
        key = jax.random.key(seed)
        ks = jax.random.split(key, 12)
        s = 0.02
        return {'x': jax.random.normal(ks[0], (BATCH, SEQ, D_MODEL), jnp.float32), 'prenorm_w': jnp.ones((D_MODEL,), jnp.float32), 'postnorm_w': jnp.ones((D_MODEL,), jnp.float32), 'in_proj_w': jax.random.normal(ks[1], (D_IN_PROJ, D_MODEL), jnp.float32) * s, 'conv_w': jax.random.normal(ks[2], (CONV_DIM, D_CONV), jnp.float32) * 0.1, 'conv_b': jnp.zeros((CONV_DIM,), jnp.float32), 'dt_bias': jnp.log(jnp.expm1(jax.random.uniform(ks[3], (NHEADS,), jnp.float32, 0.001, 0.1))), 'A_log': jnp.log(jax.random.uniform(ks[4], (NHEADS,), jnp.float32, 1.0, 16.0)), 'D_param': jnp.ones((NHEADS,), jnp.float32), 'ssm_norm_w': jnp.ones((D_INNER,), jnp.float32), 'out_proj_w': jax.random.normal(ks[5], (D_MODEL, D_INNER), jnp.float32) * s, 'gate_w': jax.random.normal(ks[6], (4 * D_MODEL, D_MODEL), jnp.float32) * s, 'up_w': jax.random.normal(ks[7], (4 * D_MODEL, D_MODEL), jnp.float32) * s, 'down_w': jax.random.normal(ks[8], (D_MODEL, 4 * D_MODEL), jnp.float32) * s}
    _L0_attn_in = _L0_attn_setup()

    def _L0_ffn_setup():
        import jax, jax.numpy as jnp
        import numpy as np
        N_EMBD = 128
        N_EXPERTS = 8
        TOP_K = 2
        B, T = (4, 256)
        key = jax.random.key(seed)
        ks = jax.random.split(key, 8)
        C, E, H = (N_EMBD, N_EXPERTS, 4 * N_EMBD)
        s_in = 1.0 / np.sqrt(C)
        s_hid = 1.0 / np.sqrt(H)
        x = jax.random.normal(ks[0], (B, T, C), dtype=jnp.float32)
        W1 = jax.random.uniform(ks[1], (E, C, H), minval=-s_in, maxval=s_in, dtype=jnp.float32)
        b1 = jax.random.uniform(ks[2], (E, H), minval=-s_in, maxval=s_in, dtype=jnp.float32)
        W2 = jax.random.uniform(ks[3], (E, H, C), minval=-s_hid, maxval=s_hid, dtype=jnp.float32)
        b2 = jax.random.uniform(ks[4], (E, C), minval=-s_hid, maxval=s_hid, dtype=jnp.float32)
        Wg = jax.random.uniform(ks[5], (C, E), minval=-s_in, maxval=s_in, dtype=jnp.float32)
        bg = jax.random.uniform(ks[6], (E,), minval=-s_in, maxval=s_in, dtype=jnp.float32)
        return {'x': x, 'W1': W1, 'b1': b1, 'W2': W2, 'b2': b2, 'Wg': Wg, 'bg': bg}
    _L0_ffn_in = _L0_ffn_setup()
    _d = {'L0_attn_x': _L0_attn_in['x'], 'L0_attn_prenorm_w': _L0_attn_in['prenorm_w'], 'L0_attn_postnorm_w': _L0_attn_in['postnorm_w'], 'L0_attn_in_proj_w': _L0_attn_in['in_proj_w'], 'L0_attn_conv_w': _L0_attn_in['conv_w'], 'L0_attn_conv_b': _L0_attn_in['conv_b'], 'L0_attn_dt_bias': _L0_attn_in['dt_bias'], 'L0_attn_A_log': _L0_attn_in['A_log'], 'L0_attn_D_param': _L0_attn_in['D_param'], 'L0_attn_ssm_norm_w': _L0_attn_in['ssm_norm_w'], 'L0_attn_out_proj_w': _L0_attn_in['out_proj_w'], 'L0_attn_gate_w': _L0_attn_in['gate_w'], 'L0_attn_up_w': _L0_attn_in['up_w'], 'L0_attn_down_w': _L0_attn_in['down_w'], 'L0_ffn_W1': _L0_ffn_in['W1'], 'L0_ffn_b1': _L0_ffn_in['b1'], 'L0_ffn_W2': _L0_ffn_in['W2'], 'L0_ffn_b2': _L0_ffn_in['b2'], 'L0_ffn_Wg': _L0_ffn_in['Wg'], 'L0_ffn_bg': _L0_ffn_in['bg']}
    _x0 = _d['L0_attn_x']
    _d['L0_attn_x'] = jax.random.normal(jax.random.fold_in(jax.random.key(seed), 1), (8, 1024, 128), dtype=_x0.dtype)
    del _x0
    return _d

def reference(L0_attn_x, L0_attn_prenorm_w, L0_attn_postnorm_w, L0_attn_in_proj_w, L0_attn_conv_w, L0_attn_conv_b, L0_attn_dt_bias, L0_attn_A_log, L0_attn_D_param, L0_attn_ssm_norm_w, L0_attn_out_proj_w, L0_attn_gate_w, L0_attn_up_w, L0_attn_down_w, L0_ffn_W1, L0_ffn_b1, L0_ffn_W2, L0_ffn_b2, L0_ffn_Wg, L0_ffn_bg):

    def _L0_attn_ref(x, prenorm_w, postnorm_w, in_proj_w, conv_w, conv_b, dt_bias, A_log, D_param, ssm_norm_w, out_proj_w, gate_w, up_w, down_w):
        import jax, jax.numpy as jnp
        import numpy as np
        D_MODEL = 128
        D_STATE = 128
        D_CONV = 4
        EXPAND = 2
        HEADDIM = 64
        D_INNER = EXPAND * D_MODEL
        NHEADS = D_INNER // HEADDIM
        CONV_DIM = D_INNER + 2 * D_STATE
        D_IN_PROJ = 2 * D_INNER + 2 * D_STATE + NHEADS
        CHUNK = 64
        BATCH, SEQ = (2, 512)
        EPS = 1e-06

        def rmsnorm(x, w):
            return x * jax.lax.rsqrt(jnp.mean(x * x, axis=-1, keepdims=True) + EPS) * w

        def segsum(a):
            cs = jnp.cumsum(a, axis=-1)
            ss = cs[..., :, None] - cs[..., None, :]
            T = a.shape[-1]
            mask = jnp.tril(jnp.ones((T, T), dtype=bool))
            return jnp.where(mask, ss, -jnp.inf)

        def ssd(x, A, B, C, chunk):
            b, l, h, p = x.shape
            c = l // chunk
            x = x.reshape(b, c, chunk, h, p)
            A = A.reshape(b, c, chunk, h).transpose(0, 3, 1, 2)
            B = B.reshape(b, c, chunk, -1)
            C = C.reshape(b, c, chunk, -1)
            A_cs = jnp.cumsum(A, axis=-1)
            L = jnp.exp(segsum(A))
            Y_diag = jnp.einsum('bcln,bcsn,bhcls,bcshp->bclhp', C, B, L, x)
            decay_states = jnp.exp(A_cs[..., -1:] - A_cs)
            states = jnp.einsum('bcln,bhcl,bclhp->bchpn', B, decay_states, x)
            A_chunk = jnp.pad(A_cs[..., -1], ((0, 0), (0, 0), (1, 0)))
            decay_chunk = jnp.exp(segsum(A_chunk))
            states_cat = jnp.concatenate([jnp.zeros_like(states[:, :1]), states], axis=1)
            new_states = jnp.einsum('bhzc,bchpn->bzhpn', decay_chunk, states_cat)
            prev_states = new_states[:, :-1]
            state_decay = jnp.exp(A_cs)
            Y_off = jnp.einsum('bcln,bchpn,bhcl->bclhp', C, prev_states, state_decay)
            return (Y_diag + Y_off).reshape(b, l, h, p)

        def mamba2(u, in_proj_w, conv_w, conv_b, dt_bias, A_log, D_param, ssm_norm_w, out_proj_w):
            b, l, _ = u.shape
            zxbcdt = jnp.einsum('bld,ed->ble', u, in_proj_w)
            z = zxbcdt[..., :D_INNER]
            xBC = zxbcdt[..., D_INNER:D_INNER + CONV_DIM]
            dt = zxbcdt[..., D_INNER + CONV_DIM:]
            xpad = jnp.pad(xBC, ((0, 0), (D_CONV - 1, 0), (0, 0)))
            xc = conv_b
            conv = sum((conv_w[:, k] * xpad[:, k:k + l, :] for k in range(D_CONV))) + conv_b
            xBC = jax.nn.silu(conv)
            x = xBC[..., :D_INNER]
            Bm = xBC[..., D_INNER:D_INNER + D_STATE]
            Cm = xBC[..., D_INNER + D_STATE:]
            dt = jax.nn.softplus(dt + dt_bias)
            A = -jnp.exp(A_log)
            xh = x.reshape(b, l, NHEADS, HEADDIM)
            y = ssd(xh * dt[..., None], A * dt, Bm, Cm, CHUNK)
            y = y + D_param[None, None, :, None] * xh
            y = y.reshape(b, l, D_INNER)
            y = rmsnorm(y * jax.nn.silu(z), ssm_norm_w)
            return jnp.einsum('ble,de->bld', y, out_proj_w)
        h = mamba2(rmsnorm(x, prenorm_w), in_proj_w, conv_w, conv_b, dt_bias, A_log, D_param, ssm_norm_w, out_proj_w) + x
        hn = rmsnorm(h, postnorm_w)
        mlp = jnp.einsum('blf,df->bld', jax.nn.silu(jnp.einsum('bld,fd->blf', hn, gate_w)) * jnp.einsum('bld,fd->blf', hn, up_w), down_w)
        return mlp + h

    def _L0_ffn_ref(x, W1, b1, W2, b2, Wg, bg):
        import jax, jax.numpy as jnp
        import numpy as np
        N_EMBD = 128
        N_EXPERTS = 8
        TOP_K = 2
        B, T = (4, 256)
        gate_scores = jax.nn.softmax(jnp.einsum('btc,ce->bte', x, Wg) + bg, axis=-1)
        h = jax.nn.relu(jnp.einsum('btc,ech->bteh', x, W1) + b1)
        expert_out = jnp.einsum('bteh,ehc->btec', h, W2) + b2
        topk_scores, topk_idx = jax.lax.top_k(gate_scores, TOP_K)
        top_probs = jax.nn.softmax(topk_scores, axis=-1)
        sel = jnp.take_along_axis(expert_out, topk_idx[..., None], axis=2)
        out = jnp.sum(sel * top_probs[..., None], axis=2)
        return out
    x = L0_attn_x
    x = x + 0.5 * _L0_ffn_ref(_layernorm(x, axis=-1), L0_ffn_W1, L0_ffn_b1, L0_ffn_W2, L0_ffn_b2, L0_ffn_Wg, L0_ffn_bg)
    x = x + _L0_attn_ref(_layernorm(x, axis=-1), L0_attn_prenorm_w, L0_attn_postnorm_w, L0_attn_in_proj_w, L0_attn_conv_w, L0_attn_conv_b, L0_attn_dt_bias, L0_attn_A_log, L0_attn_D_param, L0_attn_ssm_norm_w, L0_attn_out_proj_w, L0_attn_gate_w, L0_attn_up_w, L0_attn_down_w)
    x = x + 0.5 * _L0_ffn_ref(_layernorm(x, axis=-1), L0_ffn_W1, L0_ffn_b1, L0_ffn_W2, L0_ffn_b2, L0_ffn_Wg, L0_ffn_bg)
    return x

_drawn_inputs = setup_inputs


def setup_inputs(seed=0):
    import zlib

    import numpy as np

    out = dict(_drawn_inputs(seed))
    spreads = {'L0_attn_prenorm_w': (1.0, 0.2),
     'L0_attn_postnorm_w': (1.0, 0.6),
     'L0_attn_conv_b': (0.0, 0.1),
     'L0_attn_D_param': (1.0, 0.6),
     'L0_attn_ssm_norm_w': (1.0, 0.2)}
    factors = {'L0_attn_dt_bias': 8.0,
     'L0_attn_A_log': 8.0,
     'L0_attn_gate_w': 8.0,
     'L0_attn_up_w': 8.0,
     'L0_attn_down_w': 8.0,
     'L0_ffn_b1': 5.084,
     'L0_ffn_b2': 4.307}
    for name, (base, spread) in spreads.items():
        noise = np.random.default_rng([zlib.crc32(name.encode()), seed]).standard_normal(out[name].shape)
        drawn = base * np.exp(spread * noise) if base else spread * noise
        out[name] = jnp.asarray(drawn.astype(out[name].dtype))
    for name, factor in factors.items():
        out[name] = (out[name] * factor).astype(out[name].dtype)
    return out
```

```python
from contextlib import ExitStack

import concourse.bass as bass
from concourse import mybir

F32 = mybir.dt.float32
I32 = mybir.dt.int32
ALU = mybir.AluOpType
EngineType = mybir.EngineType
ACT = mybir.ActivationFunctionType
AX = mybir.AxisListType.X
ds = bass.ds

P = 128
SEQS, SEQ = 8, 1024
TILES = SEQS * SEQ // P
NE, HID = 8, 512
HB = HID // P
GROUPS = 2
GT = TILES // GROUPS
SLOTS = 256
TR = 4
GTILES = 8
NT = (2 * GT * P + NE * (SLOTS - 1)) // SLOTS
HEADS, HD = 4, 64
QT = 4
QUADS = TILES // QT
CONV_DVE, CONV_POOL, CONV_ORDER = (2, 0, 1), (3,), (2, 0, 3, 1)
NEG = -1.0e30
MAGIC = float(0x5F3759DF)
POOL_PER, DVE_PER = 97, 64
LN_EPS, RMS_EPS = 1e-5, 1e-6

C_ID, C_TRI, C_LOW, C_UP, C_ONE, C_MIN, C_E8, C_J = 0, 128, 256, 384, 512, 640, 768, 776
C_END = 776 + 40
SM = {}
_at = 0
for _n, _w in (("wg", 8), ("bg", 8), ("dtb", 4), ("alog", 4), ("dpar", 4), ("convw", 16), ("convb", 4),
               ("pre", 1), ("post", 1), ("ssm", 2)):
    SM[_n] = (_at, _at + _w)
    _at += _w
SM_END = _at
WM = {}
_at = 0
for _n, _w in (("wx", 512), ("wz", 260), ("wout", 256), ("gate", 512), ("up", 512), ("down", 512)):
    WM[_n] = (_at, _at + _w)
    _at += _w
WM_END = _at


class Steps:

    def __init__(self, eng, sem, tick=None):
        self.eng, self.sem, self.tick, self.base, self.n = eng, sem, tick, 0, 0

    def mark(self, ins):
        ins.then_inc(self.sem, 1)
        self.n += 1

    def link(self, ins):
        self.mark(ins)
        self.eng.wait_ge(self.sem, self.base + self.n)
        if self.tick is not None:
            self.eng.sem_inc(self.tick, 1)

    def enter(self, i, per):
        self.start, self.per = self.base + self.n, per
        self.base, self.n = self.start + i * per, 0

    def leave(self, turns):
        assert self.n == self.per, (self.n, self.per)
        self.base, self.n = self.start + turns * self.per, 0


def wait(eng, sem, value):
    if isinstance(value, int) and value <= 0:
        return
    eng.wait_ge(sem, value)


def bc(ap, n):
    return ap.unsqueeze(2).to_broadcast([ap.shape[0], ap.shape[1], n])


def rep(ap, n):
    return ap.unsqueeze(1).to_broadcast([ap.shape[0], n, ap.shape[1]])


def macaron(nc, x, cst, small, wmam, w1p, w2p, b2p, out):
    ctx = ExitStack()
    with ctx:
        def sb(name, shape, dt=F32):
            return ctx.enter_context(nc.sbuf_tensor(name, shape, dt))

        def ps(name):
            return ctx.enter_context(nc.psum_tensor(name, [P, 512], F32))

        def sem(name):
            return ctx.enter_context(nc.semaphore(name))

        xs = [nc.dram_tensor(f"xs{g}", (NT * SLOTS, P), F32, kind="Internal").ap() for g in range(GROUPS)]
        ys = [nc.dram_tensor(f"ys{g}", (NT * SLOTS, P), F32, kind="Internal").ap() for g in range(GROUPS)]
        x_v = x.rearrange("b (t p) c -> p (b t) c", p=P)
        out_v = out.rearrange("b (t p) c -> p (b t) c", p=P)

        X = sb("X", [P, TILES, P])
        CST = sb("CST", [P, C_END])
        SMALL = sb("SMALL", [P, SM_END])
        WMAM = sb("WMAM", [P, WM_END])
        W1 = sb("W1", [P, NE, HID + HB])
        W2 = sb("W2", [P, NE, HB, P])
        B2 = sb("B2", [P, NE, P])
        IDENT, TRI, LOW, UP, ONE, MINM = (CST[:, c:c + P] for c in (C_ID, C_TRI, C_LOW, C_UP, C_ONE, C_MIN))
        E8, JJ = CST[:, C_E8:C_E8 + NE], CST[:, C_J:C_J + NT]

        def sm(name):
            return SMALL[:, SM[name][0]:SM[name][1]]

        def wm(name):
            return WMAM[:, WM[name][0]:WM[name][1]]

        arena = sb("arena", [P, 30000])
        used = {"f": 0, "m": 0}

        def at(which, shape):
            n = 1
            for s in shape:
                n *= s
            a = arena[:, used[which]:used[which] + n]
            used[which] += n
            assert used[which] <= 30000
            if len(shape) == 2:
                a = a.rearrange("p (a b) -> p a b", a=shape[0])
            if len(shape) == 3:
                a = a.rearrange("p (a b c) -> p a b c", a=shape[0], b=shape[1])
            return a

        XN = at("f", [TILES, P])
        xq = [at("f", [4, P]) for _ in range(2)]
        xnT = [at("f", [4 * P]) for _ in range(2)]
        w1c = [at("f", [HID + HB]) for _ in range(2)]
        xt = [at("f", [2, P]) for _ in range(TR)]
        xT = [at("f", [SLOTS]) for _ in range(2)]
        Hh = [at("f", [HB, SLOTS]) for _ in range(2)]
        Yb = [at("f", [2, P]) for _ in range(TR)]
        R = [at("f", [GT, NE]) for _ in range(8)]
        GB = [at("f", [GT, 2, P]), XN.rearrange("p (a b) c -> p a b c", b=2)]

        st6 = sb("st6", [P, TILES, 6])
        mean = sb("mean", [P, TILES])
        rs2 = sb("rs2", [P, 2, TILES])
        va2 = sb("va2", [P, 2, TILES])
        nw = sb("nw", [P, 2 * TILES])
        rb = sb("rb", [P, 12, GT])
        tb = sb("tb", [P, 8, NE])
        wtop = [sb(f"wtop{g}", [P, 2, GT]) for g in range(GROUPS)]
        pos = [sb(f"pos{g}", [P, 2, GT], I32) for g in range(GROUPS)]
        jb = sb("jb", [P, NT, NE])
        jf = sb("jf", [P, NT])
        eid = [sb(f"eid{g}", [P, NT], I32) for g in range(GROUPS)]
        zeros = sb("zeros", [P, P])

        XR = [at("m", [4, 3 + QT * P]) for _ in range(2)]
        CV = at("m", [4, QT * P])
        TAP = at("m", [QT * P])
        XC = [at("m", [4, QT * P]) for _ in range(2)]
        U = [at("m", [QT, P]) for _ in range(2)]
        UN = at("m", [QT, P])
        UT = at("m", [QT * P])
        SZ = [at("m", [QT, 256]) for _ in range(2)]
        SLH = [at("m", [HEADS, P]) for _ in range(2)]
        RM = [at("m", [HEADS, P]) for _ in range(2)]
        EX = [at("m", [HEADS, P]) for _ in range(2)]
        MT = [at("m", [HEADS, P]) for _ in range(2)]
        XT = [at("m", [512]) for _ in range(2)]
        XD = [at("m", [256]) for _ in range(2)]
        XW = [at("m", [256]) for _ in range(2)]
        DX = [at("m", [256]) for _ in range(2)]
        S = at("m", [256])
        YY = at("m", [256])
        GY = [at("m", [256]) for _ in range(2)]
        GTr = [at("m", [256]) for _ in range(2)]
        JK = at("m", [256])
        JH = at("m", [P])
        HH = [at("m", [QT, P]) for _ in range(2)]
        HN = at("m", [QT, P])
        HT = at("m", [QT * P])
        SG = [at("m", [QT * P]) for _ in range(2)]
        AT = at("m", [4, QT * P])
        XH = at("m", [QT, P])
        DTR = [at("m", [16]) for _ in range(2)]
        V = at("m", [16])
        VA = at("m", [16])
        EE = at("m", [16])
        RD = at("m", [16])
        SS_ = at("m", [16])
        S2 = at("m", [16])
        PO = at("m", [16])
        DT = [at("m", [16]) for _ in range(2)]
        DA = [at("m", [16]) for _ in range(2)]
        C3 = at("m", [48])
        E3 = [at("m", [48]) for _ in range(2)]
        DTW = [at("m", [16]) for _ in range(2)]
        SQ = [at("m", [4]) for _ in range(2)]
        NV = [at("m", [4]) for _ in range(2)]
        NY = [at("m", [4]) for _ in range(2)]
        NW = [at("m", [4]) for _ in range(2)]
        ANEG = at("m", [4])

        BANK = [ps(f"bank{i}") for i in range(8)]
        psT, psA, psB, psX, psR, psY0, psS, psO = BANK
        psY = [psY0, psB]
        psTr = [BANK[0], BANK[1]]
        psL = BANK[2]
        psC = BANK[3]
        psHid = [[BANK[2], BANK[3]], [BANK[4], BANK[5]]]
        psOut = [BANK[6], BANK[7]]

        s_cst, s_small, s_wmam, s_w1, s_x, s_out = (sem(n) for n in ("s_cst", "s_small", "s_wmam", "s_w1", "s_x", "s_out"))
        s_zero = sem("s_zero")
        zero_ready = sem("zero_ready")
        pool_tick = sem("pool_tick")
        o_dve, o_pool = sem("o_dve"), sem("o_pool")
        xn_ready, xn_transposed, xnt_ready, xn_kept, logits_done = (
            sem(n) for n in ("xn_ready", "xn_transposed", "xnt_ready", "xn_kept", "logits_done"))
        shifted, exped, chosen, counted, placed, gap_ready, gap_exped, tiles_known = (
            sem(n) for n in ("shifted", "exped", "chosen", "counted", "placed", "gap_ready", "gap_exped", "tiles_known"))
        scattered = [sem(f"scattered{c}") for c in range(2 * GROUPS)]
        slots_in = [sem(f"slots_in{i}") for i in range(TR)]
        slots_out = [sem(f"slots_out{i}") for i in range(TR)]
        slots_turned, slots_ready, w1_ready, hidden_done, relu_act, relu_dve, rows_done, rows_ready = (
            sem(n) for n in ("slots_turned", "slots_ready", "w1_ready", "hidden_done", "relu_act", "relu_dve",
                             "rows_done", "rows_ready"))
        gathered = [[sem(f"gathered{g}_{i}") for i in range(GT // GTILES)] for g in range(GROUPS)]
        combined = sem("combined")
        (m_un, m_unT, m_ut, m_ip, m_xr, m_z, m_sz, m_cvd, m_cvp, m_xc, m_va, m_ee, m_rd, m_da, m_col, m_c3, m_e3,
         m_sl, m_tx, m_r, m_xt, m_rm, m_ex, m_xd, m_mt, m_y, m_st, m_s, m_dx, m_gy, m_gt, m_gc, m_o, m_sq, m_seed,
         m_nw, m_h, m_hn, m_hT, m_ht, m_ga, m_up, m_sg, m_at, m_dn, m_xh, m_fx, m_set, m_sqh, m_alog) = (
            sem("m_" + n) for n in
            ("un unT ut ip xr z sz cvd cvp xc va ee rd da col c3 e3 sl tx r xt rm ex xd mt y st s dx gy gt gc o sq seed"
             " nw h hn hT ht ga up sg at dn xh fx set sqh alog").split())

        block = ctx.enter_context(nc.Block())
        def load_ids(engine, g, j, n):
            return nc.values_load_multi_w_load_instructions(eid[g][0:1, ds(j, n)], engines=[engine],
                                                            min_val=0, max_val=NE - 1)[1]

        CALLS = [(f, g) for f in range(2) for g in range(GROUPS)]
        DMAS = 16
        TURNS = (NT - 3) // TR
        of_ring = [(NT - i + TR - 1) // TR for i in range(TR)]

        @block.sync
        def _(sp):
            sp.dma_start(CST[:, :], cst).then_inc(s_cst, DMAS)
            sp.dma_start(SMALL[:, :], small).then_inc(s_small, DMAS)
            for g in range(GROUPS):
                sp.dma_start(X[:, g * GT:(g + 1) * GT, :], x_v[:, g * GT:(g + 1) * GT, :]).then_inc(s_x, DMAS)
                sp.wait_ge(s_x, DMAS * (g + 1))
            sp.dma_start(W1[:, :, :], w1p).then_inc(s_w1, DMAS)
            sp.dma_start(W2[:, :, :, :], w2p).then_inc(s_w1, DMAS)
            sp.dma_start(B2[:, :, :], b2p).then_inc(s_w1, DMAS)
            sp.wait_ge(zero_ready, 1)
            for g in range(GROUPS):
                sp.dma_start(xs[g].rearrange("(p a) c -> p a c", p=P), rep(zeros[:, :], NT * SLOTS // P)
                             ).then_inc(s_zero, DMAS)
            sp.dma_start(WMAM[:, :], wmam).then_inc(s_wmam, DMAS)

            def slots_load(c, g, j, par):
                wait(sp, slots_turned, c * NT + j - TR + 1)
                sp.dma_start(xt[par], xs[g][ds(j * SLOTS, SLOTS), :].rearrange("(a p) c -> p a c", p=P)
                             ).then_inc(slots_in[par], DMAS)

            def slots_store(c, g, j, par):
                sp.wait_ge(rows_ready, c * NT + j + 1)
                sp.dma_start(ys[g][ds(j * SLOTS, SLOTS), :].rearrange("(a p) c -> p a c", p=P), Yb[par]
                             ).then_inc(slots_out[par], DMAS)

            for c, (f, g) in enumerate(CALLS):
                sp.wait_ge(scattered[c], DMAS * 2 * GT)
                if f == 1 and g == 0:
                    sp.wait_ge(m_fx, QUADS)
                for u in range(TR):
                    slots_load(c, g, u, u)
                with sp.Fori(0, TURNS - 1) as jj:
                    for u in range(TR):
                        slots_load(c, g, TR * jj + u + TR, u)
                        slots_store(c, g, TR * jj + u, u)
                for j in range(TR * (TURNS - 1), NT):
                    if j + TR < NT:
                        slots_load(c, g, j + TR, j % TR)
                    slots_store(c, g, j, j % TR)
                if g == GROUPS - 1 and f == 1:
                    for t in range(0, TILES, GTILES):
                        sp.wait_ge(combined, TILES + t + GTILES)
                        sp.dma_start(out_v[:, t:t + GTILES, :], X[:, t:t + GTILES, :]).then_inc(s_out, DMAS)
            sp.wait_ge(s_out, DMAS * TILES // GTILES)

        @block.gpsimd
        def _(pool):
            own = Steps(pool, o_pool, pool_tick)
            pool.memset(zeros[:, :], 0.0).then_inc(zero_ready, 1)

            def scatter(c, g):
                pool.wait_ge(placed, c + 1)
                pool.wait_ge(xn_kept, (c + 1) * GT // 4)
                pool.wait_ge(s_zero, DMAS * GROUPS)
                for t in range(GT):
                    for w in range(2):
                        pool.indirect_dma_start(
                            out=xs[g], out_offset=bass.IndirectOffsetOnAxis(ap=pos[g][:, w, t:t + 1], axis=0),
                            in_=XN[:, g * GT + t, :], in_offset=None).then_inc(scattered[c], DMAS)

            def gather(c, g):
                for u in range(TR):
                    pool.wait_ge(slots_out[u], DMAS * of_ring[u] * (c + 1))
                if g == GROUPS - 1:
                    pool.wait_ge(scattered[c], DMAS * 2 * GT)
                    pool.wait_ge(scattered[c - 1], DMAS * 2 * GT)
                for t in range(GT):
                    for w in range(2):
                        pool.indirect_dma_start(
                            out=GB[g][:, t, w, :], out_offset=None, in_=ys[g],
                            in_offset=bass.IndirectOffsetOnAxis(ap=pos[g][:, w, t:t + 1], axis=0)
                        ).then_inc(gathered[g][t // GTILES], DMAS)

            def hold(sem, value):
                if isinstance(value, int) and value <= 0:
                    return
                pool.wait_ge(sem, value)
                pool.sem_inc(pool_tick, 1)

            def softplus_a(k, u):
                hold(m_sz, QT * k + QT)
                hold(m_da, k)
                own.link(pool.tensor_tensor(V.rearrange("p (a b) -> p a b", a=QT),
                                            DTR[u].rearrange("p (a b) -> p a b", a=QT), rep(sm("dtb"), QT), ALU.add))
                own.link(pool.tensor_scalar(VA, V, 0.0, None, ALU.min))
                own.link(pool.tensor_scalar(V, V, 0.0, None, ALU.max))
                pool.tensor_tensor(VA, VA, V, ALU.subtract).then_inc(m_va, 1)

            def softplus_b(k, u):
                hold(m_rd, k + 1)
                own.link(pool.tensor_tensor(SS_, EE, RD, ALU.mult))
                own.link(pool.tensor_tensor(S2, SS_, SS_, ALU.mult))
                own.link(pool.tensor_scalar(PO, S2, 2.0 / 15, 2.0 / 13, ALU.mult, ALU.add))
                for d in (11, 9, 7, 5, 3, 1):
                    own.link(pool.tensor_tensor(PO, PO, S2, ALU.mult))
                    own.link(pool.tensor_scalar(PO, PO, 1.0, 2.0 / d, ALU.mult, ALU.add))
                own.link(pool.tensor_tensor(PO, PO, SS_, ALU.mult))
                own.link(pool.tensor_tensor(DT[u], PO, V, ALU.add))
                pool.tensor_tensor(DA[u].rearrange("p (a b) -> p a b", a=QT),
                                   DT[u].rearrange("p (a b) -> p a b", a=QT), rep(ANEG, QT), ALU.mult
                                   ).then_inc(m_da, 1)

            def newton(n, u):
                hold(m_seed, n)
                for it in range(3):
                    own.link(pool.tensor_tensor(NW[u], NY[u], NY[u], ALU.mult))
                    own.link(pool.tensor_tensor(NW[u], NW[u], NV[u], ALU.mult))
                    own.link(pool.tensor_scalar(NW[u], NW[u], -0.5, 1.5, ALU.mult, ALU.add))
                    last = pool.tensor_tensor(NY[u], NY[u], NW[u], ALU.mult)
                    if it < 2:
                        own.link(last)
                last.then_inc(m_nw, 1)

            def scan(k, u, prep):
                for i in range(QT):
                    I = QT * k + i
                    if i == 0:
                        hold(m_da, k + 1)
                    hold(m_r, I - 1)
                    pool.tensor_tensor(SLH[i % 2], rep(LOW, HEADS), bc(DA[u][:, 4 * i:4 * i + 4], P), ALU.mult
                                       ).then_inc(m_sl, 1)
                    if prep and i == 0:
                        softplus_a(k + 1, 1 - u)
                    if prep and i == QT - 1:
                        softplus_b(k + 1, 1 - u)
                    hold(m_xt, I + 1)
                    hold(m_gy, I - 1)
                    pool.tensor_tensor(DX[i % 2].rearrange("p (h d) -> p h d", h=HEADS),
                                       XT[i % 2][:, 0:256].rearrange("p (h d) -> p h d", h=HEADS),
                                       bc(sm("dpar"), HD), ALU.mult).then_inc(m_dx, 1)
                newton(2 * k + 1, 0)

            def conv(k, u):
                for b in CONV_POOL:
                    hold(m_xr, QT * k + b + 1)
                    hold(m_xc, QT * k)
                    if u == 1:
                        own.link(pool.tensor_copy(XR[1][:, b, 0:3], XR[0][:, b, QT * P:QT * P + 3]))
                    w = sm("convw")[:, 4 * b:4 * b + 4]
                    own.link(pool.tensor_scalar(CV[:, b, :], XR[u][:, b, 0:512], w[:, 0:1], None, ALU.mult))
                    for t in (1, 2, 3):
                        own.link(pool.tensor_scalar(TAP, XR[u][:, b, t:t + 512], w[:, t:t + 1], None, ALU.mult))
                        last = pool.tensor_tensor(CV[:, b, :], CV[:, b, :], TAP, ALU.add)
                        if t < 3:
                            own.link(last)
                    last.then_inc(m_cvp, 1)

            def residual(k, u):
                hold(m_h, k + 1)
                hold(m_fx, k)
                pool.tensor_tensor(XH, X[:, ds(QT * k, QT), :], HH[u], ALU.add).then_inc(m_xh, 1)

            def norm_h(k, u):
                newton(2 * k + 2, 1)
                hold(m_nw, 2 * k + 2)
                hold(m_hT, k)
                for i in range(QT):
                    last = pool.tensor_scalar(HN[:, i, :], HH[u][:, i, :], NY[1][:, i:i + 1], None, ALU.mult)
                last.then_inc(m_hn, 1)

            for f in range(2):
                for g in range(GROUPS):
                    scatter(2 * f + g, g)
                for g in range(GROUPS):
                    gather(2 * f + g, g)
                if f == 0:
                    pool.wait_ge(m_set, 1)
                    conv(0, 0)
                    softplus_a(0, 0)
                    softplus_b(0, 0)
                    scan(0, 0, True)
                    conv(1, 1)
                    norm_h(0, 0)
                    with pool.Fori(0, QUADS // 2 - 1) as b:
                        own.enter(b, POOL_PER)
                        for u in (1, 0):
                            k = 2 * b + (2 - u)
                            scan(k, u, True)
                            residual(k - 1, 1 - u)
                            conv(k + 1, 1 - u)
                            norm_h(k, u)
                        own.leave(QUADS // 2 - 1)
                    scan(QUADS - 1, 1, False)
                    residual(QUADS - 2, 0)
                    norm_h(QUADS - 1, 1)
                    residual(QUADS - 1, 1)

        @block.scalar
        def _(act):
            def route(c, g):
                q0 = c * GT // 4
                with act.Fori(0, GT // 8) as mm:
                    for u in range(2):
                        m = 2 * mm + u
                        act.wait_ge(xn_transposed, q0 + m + 1)
                        act.wait_ge(logits_done, q0 + 2 * mm)
                        act.activation(xnT[u], psTr[u][:, :], ACT.Copy).then_inc(xnt_ready, 1)
                        act.activation(XN[:, ds(g * GT + 4 * m, 4), :], xq[u], ACT.Copy).then_inc(xn_kept, 1)
                act.wait_ge(shifted, c + 1)
                act.activation(R[1], R[0], ACT.Exp).then_inc(exped, 1)
                act.wait_ge(gap_ready, c + 1)
                act.activation(rb[:, 6, :], rb[:, 5, :], ACT.Exp).then_inc(gap_exped, 1)

            def slots_T(c, j, par):
                act.wait_ge(slots_turned, c * NT + j + 1)
                wait(act, hidden_done, c * NT + j - 1)
                act.activation(xT[par], psTr[par][:, 0:256], ACT.Copy).then_inc(slots_ready, 1)

            def relu(c, j, par):
                act.wait_ge(hidden_done, c * NT + j + 1)
                for h in range(2):
                    last = act.activation(Hh[par][:, h, :], psHid[par][h // 2][:, (h % 2) * 256:(h % 2) * 256 + 256],
                                          ACT.Relu, bias=w1c[par][:, HID + h:HID + h + 1])
                last.then_inc(relu_act, 1)

            def experts(c):
                slots_T(c, 0, 0)
                with act.Fori(0, (NT - 1) // 2) as jj:
                    for u in range(2):
                        j = 2 * jj + u
                        relu(c, j, u)
                        slots_T(c, j + 1, 1 - u)
                relu(c, NT - 1, 0)

            def project(k, u):
                act.wait_ge(m_unT, k + 1)
                wait(act, m_z, QT * k)
                act.activation(UT, psT[:, :], ACT.Copy, scale=sm("pre")).then_inc(m_ut, 1)
                for b in range(4):
                    act.wait_ge(m_ip, QT * k + b + 1)
                    wait(act, m_cvd, len(CONV_DVE) * (k if u == 0 else k - 1))
                    wait(act, m_cvp, len(CONV_POOL) * (k if u == 0 else k - 1))
                    act.activation(XR[u][:, b, 3:515], (psA, psB)[b % 2][:, :], ACT.Copy).then_inc(m_xr, 1)
                for i in range(QT):
                    act.wait_ge(m_z, QT * k + i + 1)
                    wait(act, m_gy, QT * (k - 1))
                    act.activation(DTR[u][:, 4 * i:4 * i + 4], (psA, psB)[i % 2][:, 256:260], ACT.Copy)
                    act.activation(SZ[u][:, i, :], (psA, psB)[i % 2][:, 0:256], ACT.Silu).then_inc(m_sz, 1)

            def scan(k, u, prep):
                for i in range(QT):
                    I = QT * k + i
                    act.wait_ge(m_tx, I + 1)
                    wait(act, m_st, I - 1)
                    wait(act, m_dx, I - 1)
                    wait(act, m_xd, I - 1)
                    wait(act, m_mt, I - 1)
                    act.activation(XT[i % 2], psX[:, :], ACT.Copy).then_inc(m_xt, 1)
                    act.wait_ge(m_rm, I + 1)
                    act.activation(EX[i % 2], RM[i % 2], ACT.Exp).then_inc(m_ex, 1)
                    if prep and i == 1:
                        exp_a(k + 1)
                    if i >= 1:
                        square(k, i - 1)
                square(k, QT - 1)
                if prep:
                    exp_b(k + 1, 1 - u)

            def square(k, i):
                I = QT * k + i
                act.wait_ge(m_gy, I + 1)
                wait(act, m_sq, I)
                if i == 0:
                    wait(act, m_seed, 2 * k - 1)
                act.activation(JK, GY[i % 2], ACT.Square, accum_out=SQ[0][:, i:i + 1]).then_inc(m_sq, 1)
                act.wait_ge(m_gt, I + 1)
                wait(act, m_o, I - 1)
                act.activation(GTr[i % 2], psT[:, (i % 2) * 256:(i % 2) * 256 + 256], ACT.Copy).then_inc(m_gc, 1)

            def exp_a(k):
                act.wait_ge(m_va, k + 1)
                act.activation(EE, VA, ACT.Exp).then_inc(m_ee, 1)

            def exp_b(k, u):
                act.wait_ge(m_c3, k + 1)
                act.activation(E3[u], C3, ACT.Exp).then_inc(m_e3, 1)

            def mlp(k, u):
                act.wait_ge(m_hT, k + 1)
                wait(act, m_up, QT * k)
                act.activation(HT, psT[:, :], ACT.Copy, scale=sm("post")).then_inc(m_ht, 1)
                for b in range(4):
                    act.wait_ge(m_ga, QT * k + b + 1)
                    if b >= 2:
                        act.wait_ge(m_at, QT * k + b - 1)
                    act.activation(SG[b % 2], psA[:, :], ACT.Silu).then_inc(m_sg, 1)

            def square_h(k, u):
                act.wait_ge(m_h, k + 1)
                wait(act, m_seed, 2 * k)
                for i in range(QT):
                    wait(act, m_sqh, QT * k + i)
                    act.activation(JH, HH[u][:, i, :], ACT.Square, accum_out=SQ[1][:, i:i + 1]).then_inc(m_sqh, 1)

            def conv_silu(k, u):
                for b in CONV_ORDER:
                    if b in CONV_DVE:
                        act.wait_ge(m_cvd, len(CONV_DVE) * k + CONV_DVE.index(b) + 1)
                    else:
                        act.wait_ge(m_cvp, len(CONV_POOL) * k + CONV_POOL.index(b) + 1)
                    wait(act, m_y, QT * (k - 1))
                    act.activation(XC[u][:, b, :], CV[:, b, :], ACT.Silu, bias=sm("convb")[:, b:b + 1]).then_inc(m_xc, 1)

            for f in range(2):
                for g in range(GROUPS):
                    route(2 * f + g, g)
                for g in range(GROUPS):
                    experts(2 * f + g)
                if f == 0:
                    act.wait_ge(s_small, DMAS)
                    act.wait_ge(combined, TILES)
                    act.activation(ANEG, sm("alog"), ACT.Exp).then_inc(m_alog, 1)
                    project(0, 0)
                    conv_silu(0, 0)
                    exp_a(0)
                    exp_b(0, 0)
                    project(1, 1)
                    scan(0, 0, True)
                    square_h(0, 0)
                    conv_silu(1, 1)
                    with act.Fori(0, QUADS // 2 - 1) as b:
                        for u in (1, 0):
                            k = 2 * b + (2 - u)
                            project(k + 1, 1 - u)
                            scan(k, u, True)
                            mlp(k - 1, 1 - u)
                            square_h(k, u)
                            conv_silu(k + 1, 1 - u)
                    k = QUADS - 1
                    scan(k, 1, False)
                    mlp(k - 1, 0)
                    square_h(k, 1)
                    mlp(k, 1)

        @block.tensor
        def _(pe):
            pe.wait_ge(s_cst, DMAS)
            pe.wait_ge(s_small, DMAS)

            def route(c):
                q0 = c * GT // 4
                with pe.Fori(0, GT // 8) as mm:
                    for u in range(2):
                        m = 2 * mm + u
                        pe.wait_ge(xn_ready, q0 + m + 1)
                        for i in range(4):
                            last = pe.transpose(psTr[u][:, i * P:(i + 1) * P], xq[u][:, i, :], IDENT)
                        last.then_inc(xn_transposed, 1)
                        pe.wait_ge(xnt_ready, q0 + m + 1)
                        for i in range(4):
                            last = pe.matmul(psL[:, ds((4 * m + i) * NE, NE)], xnT[u][:, i * P:(i + 1) * P], sm("wg"),
                                             start=True, stop=True)
                        last.then_inc(logits_done, 1)
                pe.wait_ge(chosen, c + 1)
                oh = R[4].rearrange("p a b -> p (a b)")
                pe.matmul(psC[:, 0:256], UP, oh, start=True, stop=True)
                pe.matmul(psC[:, 256:512], ONE, oh, start=True, stop=True).then_inc(counted, 1)

            def turn(c, j, jj, r):
                par = r % 2
                pe.wait_ge(slots_in[r], DMAS * (of_ring[r] * c + jj + 1))
                for a in range(2):
                    last = pe.transpose(psTr[par][:, a * P:(a + 1) * P], xt[r][:, a, :], IDENT)
                last.then_inc(slots_turned, 1)

            def up_proj(c, j, par):
                pe.wait_ge(slots_ready, c * NT + j + 1)
                pe.wait_ge(w1_ready, c * NT + j + 1)
                for h in range(HB):
                    last = pe.matmul(psHid[par][h // 2][:, (h % 2) * 256:(h % 2) * 256 + 256],
                                     w1c[par][:, h * P:(h + 1) * P], xT[par], start=True, stop=True)
                last.then_inc(hidden_done, 1)

            def down_proj(c, e, j, par):
                pe.wait_ge(relu_act, c * NT + j + 1)
                pe.wait_ge(relu_dve, c * NT + j + 1)
                for a in range(2):
                    for h in range(HB):
                        last = pe.matmul(psOut[par][:, a * P:(a + 1) * P],
                                         Hh[par][:, h, a * P:(a + 1) * P], W2[:, ds(e, 1), h, :],
                                         start=(h == 0), stop=(h == HB - 1))
                last.then_inc(rows_done, 1)
                wait(pe, rows_ready, c * NT + j)

            def experts(c, g):
                pe.wait_ge(tiles_known, c + 1)
                turn(c, 0, 0, 0)
                up_proj(c, 0, 0)
                turn(c, 1, 0, 1)
                with pe.Fori(0, TURNS) as jj:
                    e = load_ids(EngineType.PE, g, TR * jj, TR)
                    for u in range(TR):
                        j = TR * jj + u
                        up_proj(c, j + 1, (u + 1) % 2)
                        turn(c, j + 2, jj + (u + 2) // TR, (u + 2) % TR)
                        down_proj(c, e[u], j, u % 2)
                e = load_ids(EngineType.PE, g, NT - 3, 3)
                up_proj(c, NT - 2, (NT - 2) % 2)
                turn(c, NT - 1, (NT - 1) // TR, (NT - 1) % TR)
                down_proj(c, e[0], NT - 3, (NT - 3) % 2)
                up_proj(c, NT - 1, (NT - 1) % 2)
                down_proj(c, e[1], NT - 2, (NT - 2) % 2)
                down_proj(c, e[2], NT - 1, (NT - 1) % 2)

            def project(k, u):
                pe.wait_ge(m_un, k + 1)
                for i in range(QT):
                    last = pe.transpose(psT[:, i * P:(i + 1) * P], UN[:, i, :], IDENT)
                last.then_inc(m_unT, 1)
                pe.wait_ge(m_ut, k + 1)
                wait(pe, m_sz, QT * k)
                for b in range(4):
                    if b >= 2:
                        pe.wait_ge(m_xr, QT * k + b - 1)
                    pe.matmul((psA, psB)[b % 2][:, :], wm("wx")[:, b * P:(b + 1) * P], UT, start=True, stop=True
                              ).then_inc(m_ip, 1)
                for i in range(QT):
                    if i < 2:
                        pe.wait_ge(m_xr, QT * k + 3 + i)
                    else:
                        pe.wait_ge(m_sz, QT * k + i - 1)
                    pe.matmul((psA, psB)[i % 2][:, 0:260], UT[:, i * P:(i + 1) * P], wm("wz"), start=True, stop=True
                              ).then_inc(m_z, 1)

            def sums(k, u, after):
                pe.wait_ge(m_da, k + 1)
                wait(pe, m_s, after)
                pe.matmul(psS[:, 256:272], TRI, DA[u], start=True, stop=True)
                pe.matmul(psS[:, 272:288], ONE, DA[u], start=True, stop=True).then_inc(m_col, 1)

            def chunk_a(k, u, i):
                I = QT * k + i
                if i == 0:
                    pe.wait_ge(m_xc, QT * k + QT)
                    wait(pe, m_fx, k - 1)
                wait(pe, m_xt, I)
                for b in range(3):
                    last = pe.transpose(psX[:, b * P:(b + 1) * P], XC[u][:, b, i * P:(i + 1) * P], IDENT)
                pe.matmul(psX[:, 384:512], XC[u][:, 2, i * P:(i + 1) * P],
                          XC[u][:, 3, i * P:(i + 1) * P], start=True, stop=True).then_inc(m_tx, 1)
                pe.wait_ge(m_sl, I + 1)
                wait(pe, m_rm, I)
                for h in range(HEADS):
                    last = pe.matmul(psR[:, h * P:(h + 1) * P], SLH[i % 2][:, h, :], TRI, start=True, stop=True)
                last.then_inc(m_r, 1)

            def chunk_b(k, u, i, projected):
                I = QT * k + i
                first = u == 0 and i == 0
                Y = psY[i % 2]
                if i == 1:
                    pe.wait_ge(m_sz, QT * projected)
                pe.wait_ge(m_mt, I + 1)
                pe.wait_ge(m_xd, I + 1)
                for h in range(HEADS):
                    last = pe.matmul(Y[:, h * HD:(h + 1) * HD], MT[i % 2][:, h, :], XD[i % 2][:, h * HD:(h + 1) * HD],
                                     start=True, stop=True)
                wait(pe, m_s, I)
                if not first:
                    last = pe.matmul(Y[:, 256:512], XC[u][:, 3, i * P:(i + 1) * P], S, start=True, stop=True)
                last.then_inc(m_y, 1)
                pe.wait_ge(m_c3, k + 1)
                pe.matmul(psS[:, 0:256], XT[i % 2][:, 256:384], XW[i % 2], start=True, stop=True).then_inc(m_st, 1)

            def turn_g(k, i):
                I = QT * k + i
                pe.wait_ge(m_gy, I + 1)
                for b in range(2):
                    last = pe.transpose(psT[:, (i % 2) * 256 + b * P:(i % 2) * 256 + (b + 1) * P],
                                        GY[i % 2][:, b * P:(b + 1) * P], IDENT)
                last.then_inc(m_gt, 1)

            def out_proj(k, i):
                I = QT * k + i
                if i == 0:
                    wait(pe, m_h, k)
                pe.wait_ge(m_gc, I + 1)
                for b in range(2):
                    last = pe.matmul(psO[:, i * P:(i + 1) * P], GTr[i % 2][:, b * P:(b + 1) * P],
                                     wm("wout")[:, b * P:(b + 1) * P], start=(b == 0), stop=(b == 1))
                last.then_inc(m_o, 1)

            def scan(k, u, prep):
                chunk_a(k, u, 0)
                for i in range(QT):
                    if i < QT - 1:
                        chunk_a(k, u, i + 1)
                    if i >= 1:
                        turn_g(k, i - 1)
                    chunk_b(k, u, i, k + 2 if prep else k + 1)
                    if i >= 1:
                        out_proj(k, i - 1)
                turn_g(k, QT - 1)
                out_proj(k, QT - 1)
                if prep:
                    sums(k + 1, 1 - u, QT * k + QT)

            def mlp(k, u, projected):
                pe.wait_ge(m_hn, k + 1)
                for i in range(QT):
                    last = pe.transpose(psT[:, i * P:(i + 1) * P], HN[:, i, :], IDENT)
                last.then_inc(m_hT, 1)
                pe.wait_ge(m_ht, k + 1)
                pe.wait_ge(m_sz, QT * projected)
                for b in range(4):
                    wait(pe, m_sg, QT * k + b)
                    pe.matmul(psA[:, :], wm("gate")[:, b * P:(b + 1) * P], HT, start=True, stop=True).then_inc(m_ga, 1)
                    wait(pe, m_at, QT * k + b)
                    pe.matmul(psB[:, :], wm("up")[:, b * P:(b + 1) * P], HT, start=True, stop=True).then_inc(m_up, 1)
                pe.wait_ge(m_at, QT * k + QT)
                wait(pe, m_fx, k)
                for i in range(QT):
                    for b in range(4):
                        last = pe.matmul(psR[:, i * P:(i + 1) * P], AT[:, b, i * P:(i + 1) * P],
                                         wm("down")[:, b * P:(b + 1) * P], start=(b == 0), stop=(b == 3))
                last.then_inc(m_dn, 1)

            for f in range(2):
                for g in range(GROUPS):
                    route(2 * f + g)
                if f == 0:
                    pe.wait_ge(s_w1, DMAS * 3)
                for g in range(GROUPS):
                    experts(2 * f + g, g)
                if f == 0:
                    pe.wait_ge(s_wmam, DMAS)
                    pe.wait_ge(m_set, 1)
                    project(0, 0)
                    sums(0, 0, 0)
                    project(1, 1)
                    scan(0, 0, True)
                    with pe.Fori(0, QUADS // 2 - 1) as b:
                        for u in (1, 0):
                            k = 2 * b + (2 - u)
                            project(k + 1, 1 - u)
                            scan(k, u, True)
                            mlp(k - 1, 1 - u, k + 2)
                    k = QUADS - 1
                    scan(k, 1, False)
                    mlp(k - 1, 0, k + 1)
                    mlp(k, 1, k + 1)

        @block.vector
        def _(dve):
            own = Steps(dve, o_dve)
            link = own.link

            def stats(t0, n):
                with dve.Fori(0, n // 4) as a:
                    for i in range(4):
                        t = t0 + 4 * a + i
                        last = dve.bn_stats(st6[:, ds(t, 1), :], X[:, ds(t, 1), :])
                    own.enter(a, 1)
                    own.mark(last)
                    own.leave(n // 4)
                dve.wait_ge(o_dve, own.base + own.n)

            def root(v, y, w):
                link(dve.tensor_single_scalar(y.bitcast(I32), v.bitcast(I32), 1, ALU.arith_shift_right))
                link(dve.tensor_scalar(y.bitcast(I32), y.bitcast(I32), -1.0, MAGIC, ALU.mult, ALU.add))
                for _ in range(3):
                    link(dve.tensor_tensor(w, y, y, ALU.mult))
                    link(dve.scalar_tensor_tensor(w, w, -0.5, v, ALU.mult, ALU.mult))
                    link(dve.scalar_tensor_tensor(y, w, 1.5, y, ALU.add, ALU.mult))

            def moments(t0, n):
                m, v, w = mean[:, t0:t0 + n], va2[:, 0, t0:t0 + n], nw[:, 0:n]
                m0, m1, q0, q1 = (st6[:, t0:t0 + n, c] for c in (1, 4, 2, 5))
                link(dve.tensor_tensor(m, m0, m1, ALU.add))
                link(dve.tensor_scalar(m, m, 0.5, None, ALU.mult))
                link(dve.tensor_tensor(w, m0, m1, ALU.subtract))
                link(dve.tensor_tensor(w, w, w, ALU.mult))
                link(dve.tensor_tensor(v, q0, q1, ALU.add))
                link(dve.tensor_scalar(v, v, 1.0 / P, LN_EPS, ALU.mult, ALU.add))
                link(dve.scalar_tensor_tensor(v, w, 0.25, v, ALU.mult, ALU.add))

            def route(c, g):
                t0, q0 = g * GT, c * GT // 4
                stats(t0, GT)
                moments(t0, GT)
                root(va2[:, 0, t0:t0 + GT], rs2[:, 0, t0:t0 + GT], nw[:, 0:GT])
                start = own.base + own.n
                with dve.Fori(0, GT // 8) as mm:
                    own.enter(mm, 2)
                    for u in range(2):
                        m = 2 * mm + u
                        t = t0 + 4 * m
                        dve.wait_ge(xn_kept, q0 + 2 * mm)
                        dve.wait_ge(xn_transposed, q0 + 2 * mm)
                        link(dve.tensor_tensor(xq[u], X[:, ds(t, 4), :], bc(mean[:, ds(t, 4)], P), ALU.subtract))
                        dve.tensor_tensor(xq[u], xq[u], bc(rs2[:, 0, ds(t, 4)], P), ALU.mult).then_inc(xn_ready, 1)
                    own.leave(GT // 8)
                L, Pr, T, O1, A, O2, C0, C1 = R
                row = lambda i: rb[:, i, :]
                dve.wait_ge(logits_done, q0 + GT // 4)
                link(dve.tensor_tensor(L, psL[:, 0:GT * NE].rearrange("p (a b) -> p a b", b=NE), rep(sm("bg"), GT), ALU.add))
                link(dve.tensor_reduce(row(0), L, AX, ALU.max))
                dve.tensor_tensor(L, L, bc(row(0), NE), ALU.subtract).then_inc(shifted, 1)
                dve.wait_ge(exped, c + 1)
                link(dve.tensor_reduce(row(1), Pr, AX, ALU.add))
                link(dve.reciprocal(row(2), row(1)))
                link(dve.tensor_tensor(Pr, Pr, bc(row(2), NE), ALU.mult))
                for w, (src, oh) in enumerate(((Pr, O1), (A, O2))):
                    link(dve.tensor_reduce(row(3 + w), src, AX, ALU.max))
                    link(dve.tensor_tensor(T, src, bc(row(3 + w), NE), ALU.is_equal))
                    link(dve.tensor_tensor(T, T, rep(E8, GT), ALU.mult))
                    link(dve.tensor_reduce(row(7), T, AX, ALU.min))
                    link(dve.tensor_tensor(oh, rep(E8, GT), bc(row(7), NE), ALU.is_equal))
                    if w == 0:
                        link(dve.scalar_tensor_tensor(A, oh, -2.0, Pr, ALU.mult, ALU.add))
                dve.tensor_tensor(row(5), row(4), row(3), ALU.subtract).then_inc(gap_ready, 1)
                dve.tensor_tensor(A, O1, O2, ALU.add).then_inc(chosen, 1)
                dve.wait_ge(gap_exped, c + 1)
                link(dve.tensor_scalar(row(8), row(6), 1.0, None, ALU.add))
                link(dve.reciprocal(row(9), row(8)))
                link(dve.tensor_scalar(wtop[g][:, 0, :], row(9), 0.5, None, ALU.mult))
                link(dve.tensor_tensor(wtop[g][:, 1, :], wtop[g][:, 0, :], row(6), ALU.mult))
                dve.wait_ge(counted, c + 1)
                cnt = psC[:, 256:512].rearrange("p (a b) -> p a b", b=NE)
                link(dve.tensor_copy(C0, cnt))
                a, b = C0, C1
                s = 1
                while s < GT:
                    own.mark(dve.tensor_copy(b[:, 0:s, :], a[:, 0:s, :]))
                    link(dve.tensor_tensor(b[:, s:GT, :], a[:, s:GT, :], a[:, 0:GT - s, :], ALU.add))
                    a, b = b, a
                    s *= 2
                tot, nt, inc, inc2, base = (tb[:, i, :] for i in range(5))
                nti = tb[:, 5, :].bitcast(I32)
                link(dve.tensor_scalar(tot, a[:, GT - 1, :], float(SLOTS - 1), None, ALU.add))
                link(dve.tensor_copy(nti, tot))
                link(dve.tensor_single_scalar(nti, nti, SLOTS.bit_length() - 1, ALU.arith_shift_right))
                link(dve.tensor_copy(nt, nti))
                link(dve.tensor_copy(inc, nt))
                s = 1
                while s < NE:
                    own.mark(dve.tensor_copy(inc2[:, 0:s], inc[:, 0:s]))
                    link(dve.tensor_tensor(inc2[:, s:NE], inc[:, s:NE], inc[:, 0:NE - s], ALU.add))
                    inc, inc2 = inc2, inc
                    s *= 2
                link(dve.tensor_tensor(base, inc, nt, ALU.subtract))
                link(dve.tensor_scalar(base, base, float(SLOTS), None, ALU.mult))
                link(dve.tensor_tensor(L, a, cnt, ALU.subtract))
                link(dve.tensor_tensor(L, L, psC[:, 0:256].rearrange("p (a b) -> p a b", b=NE), ALU.add))
                link(dve.tensor_tensor(L, L, rep(base, GT), ALU.add))
                for w, oh in enumerate((O1, O2)):
                    link(dve.tensor_tensor(T, oh, L, ALU.mult))
                    link(dve.tensor_reduce(row(10 + w), T, AX, ALU.add))
                dve.tensor_copy(pos[g][:, :, :], rb[:, 10:12, :]).then_inc(placed, 1)
                link(dve.tensor_tensor(jb[:, :, :], bc(JJ, NE), rep(inc, NT), ALU.is_ge))
                link(dve.tensor_reduce(jf[:, :], jb[:, :, :], AX, ALU.add))
                link(dve.tensor_scalar(jf[:, :], jf[:, :], float(NE - 1), None, ALU.min))
                dve.tensor_copy(eid[g][:, :], jf[:, :]).then_inc(tiles_known, 1)

            def weights(c, e, j, par):
                wait(dve, hidden_done, c * NT + j - 1)
                wait(dve, relu_act, c * NT + j - 1)
                wait(dve, relu_dve, c * NT + j - 1)
                dve.tensor_copy(w1c[par], W1[:, ds(e, 1), :]).then_inc(w1_ready, 1)

            def relu(c, j, par):
                dve.wait_ge(w1_ready, c * NT + j + 1)
                dve.wait_ge(hidden_done, c * NT + j + 1)
                for h in (2, 3):
                    last = dve.tensor_scalar(Hh[par][:, h, :], psHid[par][1][:, (h % 2) * 256:(h % 2) * 256 + 256],
                                             w1c[par][:, HID + h:HID + h + 1], 0.0, ALU.add, ALU.max)
                last.then_inc(relu_dve, 1)

            def rows(c, e, j, jj, r):
                dve.wait_ge(rows_done, c * NT + j + 1)
                wait(dve, slots_out[r], DMAS * (of_ring[r] * c + jj))
                dve.tensor_tensor(Yb[r], psOut[r % 2][:, 0:256].rearrange("p (a b) -> p a b", a=2),
                                  B2[:, ds(e, 1), :].to_broadcast([P, 2, P]), ALU.add).then_inc(rows_ready, 1)

            def experts(c, g):
                dve.wait_ge(tiles_known, c + 1)
                e = load_ids(EngineType.DVE, g, 0, 2)
                weights(c, e[0], 0, 0)
                weights(c, e[1], 1, 1)
                relu(c, 0, 0)
                with dve.Fori(0, TURNS) as jj:
                    e = load_ids(EngineType.DVE, g, TR * jj, TR + 2)
                    for u in range(TR):
                        j = TR * jj + u
                        weights(c, e[u + 2], j + 2, u % 2)
                        relu(c, j + 1, (u + 1) % 2)
                        rows(c, e[u], j, jj, u)
                e = load_ids(EngineType.DVE, g, NT - 3, 3)
                weights(c, e[2], NT - 1, (NT - 1) % 2)
                relu(c, NT - 2, (NT - 2) % 2)
                rows(c, e[0], NT - 3, TURNS, 0)
                relu(c, NT - 1, (NT - 1) % 2)
                rows(c, e[1], NT - 2, TURNS, 1)
                rows(c, e[2], NT - 1, TURNS, 2)

            def combine(c, g):
                for q in range(GT // GTILES):
                    dve.wait_ge(gathered[g][q], 2 * DMAS * GTILES * (c // GROUPS + 1))
                    with dve.Fori(0, GTILES // 4) as tt:
                        own.enter(tt, 4)
                        for s in range(4):
                            t = GTILES * q + 4 * tt + s
                            xrow = X[:, ds(g * GT + t, 1), :]
                            own.mark(dve.scalar_tensor_tensor(xrow, GB[g][:, ds(t, 1), 0, :], wtop[g][:, 0, ds(t, 1)],
                                                              xrow, ALU.mult, ALU.add))
                        dve.wait_ge(o_dve, own.base + own.n)
                        for s in range(4):
                            t = GTILES * q + 4 * tt + s
                            xrow = X[:, ds(g * GT + t, 1), :]
                            dve.scalar_tensor_tensor(xrow, GB[g][:, ds(t, 1), 1, :], wtop[g][:, 1, ds(t, 1)], xrow,
                                                     ALU.mult, ALU.add).then_inc(combined, 1)
                        own.leave(GTILES // 4)

            def norm(k, u):
                wait(dve, m_unT, k)
                for dst, r in ((U[u], 0), (UN, 1)):
                    for i in range(QT):
                        t = QT * k + i
                        last = dve.tensor_scalar(dst[:, i:i + 1, :], X[:, ds(t, 1), :], mean[:, ds(t, 1)],
                                                 rs2[:, r, ds(t, 1)], ALU.subtract, ALU.mult)
                last.then_inc(m_un, 1)

            def conv(k, u):
                for b in CONV_DVE:
                    dve.wait_ge(m_xr, QT * k + b + 1)
                    wait(dve, m_xc, QT * k)
                    if u == 1:
                        link(dve.tensor_copy(XR[1][:, b, 0:3], XR[0][:, b, QT * P:QT * P + 3]))
                    w = sm("convw")[:, 4 * b:4 * b + 4]
                    link(dve.tensor_scalar(CV[:, b, :], XR[u][:, b, 0:512], w[:, 0:1], None, ALU.mult))
                    for t in (1, 2):
                        link(dve.scalar_tensor_tensor(CV[:, b, :], XR[u][:, b, t:t + 512], w[:, t:t + 1],
                                                      CV[:, b, :], ALU.mult, ALU.add))
                    dve.scalar_tensor_tensor(CV[:, b, :], XR[u][:, b, 3:515], w[:, 3:4],
                                             CV[:, b, :], ALU.mult, ALU.add).then_inc(m_cvd, 1)

            def heads(ap):
                return ap.rearrange("p (h d) -> p h d", h=HEADS)

            def steps_r(k):
                dve.wait_ge(m_ee, k + 1)
                link(dve.tensor_scalar(RD, EE, 2.0, None, ALU.add))
                dve.reciprocal(RD, RD).then_inc(m_rd, 1)

            def sums(k):
                dve.wait_ge(m_col, k + 1)
                link(dve.tensor_copy(C3[:, 0:32], psS[:, 256:288]))
                dve.tensor_tensor(C3[:, 32:48], C3[:, 16:32], C3[:, 0:16], ALU.subtract).then_inc(m_c3, 1)

            def mask(k, u, i):
                I = QT * k + i
                dve.wait_ge(m_r, I + 1)
                dve.tensor_tensor(RM[i % 2], psR[:, :].rearrange("p (h l) -> p h l", h=HEADS), rep(MINM, HEADS),
                                  ALU.min).then_inc(m_rm, 1)
                dve.wait_ge(m_xt, I + 1)
                c = slice(4 * i, 4 * i + 4)
                dve.tensor_tensor(heads(XD[i % 2]), heads(XT[i % 2][:, 0:256]), bc(DT[u][:, c], HD), ALU.mult)
                dve.tensor_tensor(heads(XW[i % 2]), heads(XT[i % 2][:, 0:256]), bc(DTW[u][:, c], HD), ALU.mult
                                  ).then_inc(m_xd, 1)

            def weigh(k, i):
                I = QT * k + i
                dve.wait_ge(m_ex, I + 1)
                dve.tensor_tensor(MT[i % 2], EX[i % 2], rep(XT[i % 2][:, 384:512], HEADS), ALU.mult
                                  ).then_inc(m_mt, 1)

            def scan(k, u, prep):
                dve.wait_ge(m_e3, k + 1)
                link(dve.tensor_tensor(DTW[u], DT[u], E3[u][:, 32:48], ALU.mult))
                mask(k, u, 0)
                weigh(k, 0)
                for i in range(QT):
                    I = QT * k + i
                    first = u == 0 and i == 0
                    c = slice(4 * i, 4 * i + 4)
                    Y = psY[i % 2]
                    if i < QT - 1:
                        mask(k, u, i + 1)
                    dve.wait_ge(m_st, I + 1)
                    if first:
                        dve.tensor_copy(S, psS[:, 0:256]).then_inc(m_s, 1)
                    else:
                        dve.wait_ge(m_s, I)
                        link(dve.tensor_tensor(heads(S), heads(S), bc(E3[u][:, 16 + 4 * i:20 + 4 * i], HD), ALU.mult))
                        dve.tensor_tensor(S, S, psS[:, 0:256], ALU.add).then_inc(m_s, 1)
                    dve.wait_ge(m_y, I + 1)
                    dve.wait_ge(m_dx, I + 1)
                    wait(dve, m_gy, I)
                    if first:
                        link(dve.tensor_tensor(YY, Y[:, 0:256], DX[i % 2], ALU.add))
                    else:
                        link(dve.tensor_tensor(heads(YY), heads(Y[:, 256:512]), bc(E3[u][:, c], HD), ALU.mult))
                        link(dve.tensor_tensor(YY, YY, Y[:, 0:256], ALU.add))
                        link(dve.tensor_tensor(YY, YY, DX[i % 2], ALU.add))
                    wait(dve, m_gt, I - 1)
                    wait(dve, m_sq, I - 1)
                    dve.tensor_tensor(GY[i % 2], YY, SZ[u][:, i, :], ALU.mult).then_inc(m_gy, 1)
                    if i < QT - 1:
                        weigh(k, i + 1)
                    if prep and i == 0:
                        steps_r(k + 1)
                if prep:
                    sums(k + 1)

            def seed(which, width):
                link(dve.tensor_scalar(NV[which], SQ[which], 1.0 / width, RMS_EPS, ALU.mult, ALU.add))
                y = NY[which].bitcast(I32)
                link(dve.tensor_single_scalar(y, NV[which].bitcast(I32), 1, ALU.arith_shift_right))
                dve.tensor_scalar(y, y, -1.0, MAGIC, ALU.mult, ALU.add).then_inc(m_seed, 1)

            def seed_g(k):
                dve.wait_ge(m_sq, QT * k + QT)
                seed(0, 256)

            def seed_h(k):
                dve.wait_ge(m_sqh, QT * k + QT)
                seed(1, P)

            def join(k, u):
                dve.wait_ge(m_nw, 2 * k + 1)
                dve.wait_ge(m_o, QT * k + QT)
                dve.wait_ge(m_un, k + 1)
                for i in range(QT):
                    last = dve.scalar_tensor_tensor(HH[u][:, i, :], psO[:, i * P:(i + 1) * P], NY[0][:, i:i + 1],
                                                    U[u][:, i, :], ALU.mult, ALU.add)
                last.then_inc(m_h, 1)

            def mlp(k, u):
                wait(dve, m_dn, k)
                for b in range(4):
                    dve.wait_ge(m_sg, QT * k + b + 1)
                    dve.wait_ge(m_up, QT * k + b + 1)
                    dve.tensor_tensor(AT[:, b, :], psB[:, :], SG[b % 2], ALU.mult).then_inc(m_at, 1)
                dve.wait_ge(m_dn, k + 1)
                dve.wait_ge(m_xh, k + 1)
                dve.tensor_tensor(X[:, ds(QT * k, QT), :], psR[:, :].rearrange("p (a b) -> p a b", a=QT), XH, ALU.add
                                  ).then_inc(m_fx, 1)

            dve.wait_ge(s_cst, DMAS)
            dve.wait_ge(s_small, DMAS)
            for f in range(2):
                for g in range(GROUPS):
                    if f == 0:
                        dve.wait_ge(s_x, DMAS * (g + 1))
                    route(2 * f + g, g)
                dve.wait_ge(s_w1, DMAS * 3)
                for g in range(GROUPS):
                    experts(2 * f + g, g)
                for g in range(GROUPS):
                    combine(2 * f + g, g)
                if f == 0:
                    dve.wait_ge(combined, TILES)
                    stats(0, TILES)
                    moments(0, TILES)
                    link(dve.tensor_scalar(nw[:, 0:TILES], va2[:, 0, :], -LN_EPS, None, ALU.add))
                    link(dve.scalar_tensor_tensor(va2[:, 1, :], va2[:, 0, :], RMS_EPS, nw[:, 0:TILES], ALU.mult, ALU.add))
                    root(va2[:, :, :].rearrange("p a b -> p (a b)"), rs2[:, :, :].rearrange("p a b -> p (a b)"), nw[:, :])
                    link(dve.memset(XR[0][:, :, 0:3], 0.0))
                    dve.wait_ge(s_wmam, DMAS)
                    for b in range(2):
                        w = wm("wout")[:, b * P:(b + 1) * P]
                        link(dve.tensor_scalar(w, w, sm("ssm")[:, b:b + 1], None, ALU.mult))
                    dve.wait_ge(m_alog, 1)
                    dve.tensor_scalar(ANEG, ANEG, -1.0, None, ALU.mult).then_inc(m_set, 1)
                    norm(0, 0)
                    norm(1, 1)
                    conv(0, 0)
                    steps_r(0)
                    sums(0)
                    scan(0, 0, True)
                    seed_g(0)
                    join(0, 0)
                    conv(1, 1)
                    seed_h(0)
                    with dve.Fori(0, QUADS // 2 - 1) as b:
                        own.enter(b, DVE_PER)
                        for u in (1, 0):
                            k = 2 * b + (2 - u)
                            norm(k + 1, 1 - u)
                            scan(k, u, True)
                            seed_g(k)
                            mlp(k - 1, 1 - u)
                            join(k, u)
                            conv(k + 1, 1 - u)
                            seed_h(k)
                        own.leave(QUADS // 2 - 1)
                    k = QUADS - 1
                    scan(k, 1, False)
                    seed_g(k)
                    mlp(k - 1, 0)
                    join(k, 1)
                    seed_h(k)
                    mlp(k, 1)


def kernel(L0_attn_x, L0_attn_prenorm_w, L0_attn_postnorm_w, L0_attn_in_proj_w, L0_attn_conv_w, L0_attn_conv_b,
           L0_attn_dt_bias, L0_attn_A_log, L0_attn_D_param, L0_attn_ssm_norm_w, L0_attn_out_proj_w, L0_attn_gate_w,
           L0_attn_up_w, L0_attn_down_w, L0_ffn_W1, L0_ffn_b1, L0_ffn_W2, L0_ffn_b2, L0_ffn_Wg, L0_ffn_bg):
    import numpy as np
    import concourse.bacc as bacc
    from concourse.bass_utils import run_bass_kernel_spmd

    f = np.float32
    p = np.arange(P)
    cst = np.zeros((P, C_END), f)
    cst[:, C_ID:C_ID + P] = np.eye(P)
    cst[:, C_TRI:C_TRI + P] = p[:, None] <= p[None, :]
    cst[:, C_LOW:C_LOW + P] = p[:, None] > p[None, :]
    cst[:, C_UP:C_UP + P] = p[:, None] < p[None, :]
    cst[:, C_ONE:C_ONE + P] = 1.0
    cst[:, C_MIN:C_MIN + P] = np.where(p[:, None] <= p[None, :], 0.0, NEG)
    cst[:, C_E8:C_E8 + NE] = np.arange(NE) - NE
    cst[:, C_J:C_J + NT] = np.arange(NT)

    def rows(a):
        a = np.asarray(a)
        return np.broadcast_to(a.reshape(1, -1), (P, a.size))

    def cols(a, n):
        return np.asarray(a).reshape(n, P).T

    small = np.concatenate([
        np.asarray(L0_ffn_Wg), rows(L0_ffn_bg), rows(L0_attn_dt_bias), rows(L0_attn_A_log), rows(L0_attn_D_param),
        np.asarray(L0_attn_conv_w).reshape(4, P, 4).transpose(1, 0, 2).reshape(P, 16), cols(L0_attn_conv_b, 4),
        cols(L0_attn_prenorm_w, 1), cols(L0_attn_postnorm_w, 1), cols(L0_attn_ssm_norm_w, 2)], axis=1)
    win = np.asarray(L0_attn_in_proj_w).T
    wmam = np.concatenate([
        win[:, 256:768], win[:, 0:256], win[:, 768:772],
        np.asarray(L0_attn_out_proj_w).reshape(P, 2, P).transpose(2, 1, 0).reshape(P, 256),
        np.asarray(L0_attn_gate_w).T, np.asarray(L0_attn_up_w).T,
        np.asarray(L0_attn_down_w).reshape(P, 4, P).transpose(2, 1, 0).reshape(P, 512)], axis=1)
    w1p = np.concatenate([np.asarray(L0_ffn_W1).transpose(1, 0, 2),
                          np.asarray(L0_ffn_b1).reshape(NE, HB, P).transpose(2, 0, 1)], axis=2)
    w2p = np.asarray(L0_ffn_W2).reshape(NE, HB, P, P).transpose(2, 0, 1, 3)
    b2p = np.broadcast_to(np.asarray(L0_ffn_b2).reshape(1, NE, P), (P, NE, P))
    arrays = {"x": np.asarray(L0_attn_x), "cst": cst, "small": small, "wmam": wmam, "w1p": w1p, "w2p": w2p, "b2p": b2p}
    nc = bacc.Bacc("TRN2", target_bir_lowering=False, num_devices=1)
    args, given = [], {}
    for name, a in arrays.items():
        given[name] = np.ascontiguousarray(a)
        args.append(nc.dram_tensor(name, a.shape, mybir.dt.from_np(a.dtype), kind="ExternalInput").ap())
    args.append(nc.dram_tensor("out", (SEQS, SEQ, P), F32, kind="ExternalOutput").ap())
    macaron(nc, *args)
    r = run_bass_kernel_spmd(nc, [given], core_ids=[0])
    return r.results[0]["out"]
```

```python
from contextlib import ExitStack

import concourse.bass as bass
from concourse import mybir

F32 = mybir.dt.float32
I32 = mybir.dt.int32
ALU = mybir.AluOpType
EngineType = mybir.EngineType
ACT = mybir.ActivationFunctionType
AX = mybir.AxisListType.X
ds = bass.ds

P = 128
SEQS, SEQ = 8, 1024
TILES = SEQS * SEQ // P
NE, HID = 8, 512
HB = HID // P
GROUPS = 2
GT = TILES // GROUPS
SLOTS = 256
TR = 4
GTILES = 8
NT = (2 * GT * P + NE * (SLOTS - 1)) // SLOTS
HEADS, HD = 4, 64
QT = 4
QUADS = TILES // QT
CONV_DVE, CONV_PE = (2, 0, 1), 3
NEG = -1.0e30
MAGIC = float(0x5F3759DF)
POOL_PER, DVE_PER = 84, 53
LN_EPS, RMS_EPS = 1e-5, 1e-6

C_ID, C_TRI, C_LOW, C_UP, C_ONE, C_MIN, C_E8, C_J = 0, 128, 256, 384, 512, 640, 768, 776
C_END = 776 + 40
SM = {}
_at = 0
for _n, _w in (("wg", 8), ("bg", 8), ("dtb", 4), ("alog", 4), ("dcol", 2), ("convw", 16), ("convb", 4),
               ("pre", 1), ("post", 1), ("ssm", 2)):
    SM[_n] = (_at, _at + _w)
    _at += _w
SM_END = _at
WM = {}
_at = 0
for _n, _w in (("wx", 512), ("wz", 260), ("wout", 256), ("gate", 512), ("up", 512), ("down", 512)):
    WM[_n] = (_at, _at + _w)
    _at += _w
WM_END = _at


class Steps:

    def __init__(self, eng, sem, tick=None):
        self.eng, self.sem, self.tick, self.base, self.n = eng, sem, tick, 0, 0

    def mark(self, ins):
        ins.then_inc(self.sem, 1)
        self.n += 1

    def link(self, ins):
        self.mark(ins)
        self.eng.wait_ge(self.sem, self.base + self.n)
        if self.tick is not None:
            self.eng.sem_inc(self.tick, 1)

    def enter(self, i, per):
        self.start, self.per = self.base + self.n, per
        self.base, self.n = self.start + i * per, 0

    def leave(self, turns):
        assert self.n == self.per, (self.n, self.per)
        self.base, self.n = self.start + turns * self.per, 0


def wait(eng, sem, value):
    if isinstance(value, int) and value <= 0:
        return
    eng.wait_ge(sem, value)


def bc(ap, n):
    return ap.unsqueeze(2).to_broadcast([ap.shape[0], ap.shape[1], n])


def rep(ap, n):
    return ap.unsqueeze(1).to_broadcast([ap.shape[0], n, ap.shape[1]])


def macaron(nc, x, cst, small, wmam, w1p, w2p, b2p, out):
    ctx = ExitStack()
    with ctx:
        def sb(name, shape, dt=F32):
            return ctx.enter_context(nc.sbuf_tensor(name, shape, dt))

        def ps(name):
            return ctx.enter_context(nc.psum_tensor(name, [P, 512], F32))

        def sem(name):
            return ctx.enter_context(nc.semaphore(name))

        xs = [nc.dram_tensor(f"xs{g}", (NT * SLOTS, P), F32, kind="Internal").ap() for g in range(GROUPS)]
        ys = [nc.dram_tensor(f"ys{g}", (NT * SLOTS, P), F32, kind="Internal").ap() for g in range(GROUPS)]
        x_v = x.rearrange("b (t p) c -> p (b t) c", p=P)
        out_v = out.rearrange("b (t p) c -> p (b t) c", p=P)

        X = sb("X", [P, TILES, P])
        CST = sb("CST", [P, C_END])
        SMALL = sb("SMALL", [P, SM_END])
        WMAM = sb("WMAM", [P, WM_END])
        W1 = sb("W1", [P, NE, HID + HB])
        W2 = sb("W2", [P, NE, HB, P])
        B2 = sb("B2", [P, NE, P])
        IDENT, TRI, LOW, UP, ONE, MINM = (CST[:, c:c + P] for c in (C_ID, C_TRI, C_LOW, C_UP, C_ONE, C_MIN))
        E8, JJ = CST[:, C_E8:C_E8 + NE], CST[:, C_J:C_J + NT]

        def sm(name):
            return SMALL[:, SM[name][0]:SM[name][1]]

        def wm(name):
            return WMAM[:, WM[name][0]:WM[name][1]]

        arena = sb("arena", [P, 30000])
        used = {"f": 0, "m": 0}

        def at(which, shape):
            n = 1
            for s in shape:
                n *= s
            a = arena[:, used[which]:used[which] + n]
            used[which] += n
            assert used[which] <= 30000
            if len(shape) == 2:
                a = a.rearrange("p (a b) -> p a b", a=shape[0])
            if len(shape) == 3:
                a = a.rearrange("p (a b c) -> p a b c", a=shape[0], b=shape[1])
            return a

        XN = at("f", [TILES, P])
        xq = [at("f", [4, P]) for _ in range(2)]
        xnT = [at("f", [4 * P]) for _ in range(2)]
        w1c = [at("f", [HID + HB]) for _ in range(2)]
        xt = [at("f", [2, P]) for _ in range(TR)]
        xT = [at("f", [SLOTS]) for _ in range(2)]
        Hh = [at("f", [HB, SLOTS]) for _ in range(2)]
        Yb = [at("f", [2, P]) for _ in range(TR)]
        R = [at("f", [GT, NE]) for _ in range(8)]
        GB = [at("f", [GT, 2, P]), XN.rearrange("p (a b) c -> p a b c", b=2)]

        st6 = sb("st6", [P, TILES, 6])
        mean = sb("mean", [P, TILES])
        rs2 = sb("rs2", [P, 2, TILES])
        va2 = sb("va2", [P, 2, TILES])
        nw = sb("nw", [P, 2 * TILES])
        rb = sb("rb", [P, 12, GT])
        tb = sb("tb", [P, 8, NE])
        wtop = [sb(f"wtop{g}", [P, 2, GT]) for g in range(GROUPS)]
        pos = [sb(f"pos{g}", [P, 2, GT], I32) for g in range(GROUPS)]
        jb = sb("jb", [P, NT, NE])
        jf = sb("jf", [P, NT])
        eid = [sb(f"eid{g}", [P, NT], I32) for g in range(GROUPS)]
        zeros = sb("zeros", [P, P])

        XR = [at("m", [4, 3 + QT * P]) for _ in range(2)]
        CV = at("m", [4, QT * P])
        CT = at("m", [4, P])
        XC = [at("m", [4, QT * P]) for _ in range(2)]
        U = at("m", [QT, P])
        DG = at("m", [2, P])
        UN = at("m", [QT, P])
        UT = at("m", [QT * P])
        SZ = [at("m", [QT, 256]) for _ in range(2)]
        SLH = [at("m", [HEADS, P]) for _ in range(2)]
        RM = [at("m", [HEADS, P]) for _ in range(2)]
        EX = [at("m", [HEADS, P]) for _ in range(QT)]
        MT = [at("m", [HEADS, P]) for _ in range(2)]
        XT = [at("m", [512]) for _ in range(2)]
        XD = [at("m", [256]) for _ in range(2)]
        XW = [at("m", [256]) for _ in range(2)]
        S = at("m", [256])
        YY = at("m", [256])
        GY = [at("m", [256]) for _ in range(2)]
        GTr = [at("m", [256]) for _ in range(2)]
        JK = at("m", [256])
        JH = at("m", [P])
        HH = at("m", [QT, P])
        HN = at("m", [QT, P])
        HT = at("m", [QT * P])
        SG = [at("m", [QT * P]) for _ in range(2)]
        AT = at("m", [4, QT * P])
        XH = at("m", [QT, P])
        DTR = [at("m", [16]) for _ in range(2)]
        V = at("m", [16])
        VA = at("m", [16])
        EE = at("m", [16])
        RD = at("m", [16])
        SS_ = at("m", [16])
        S2 = at("m", [16])
        PO = at("m", [16])
        DT = [at("m", [16]) for _ in range(2)]
        DA = [at("m", [16]) for _ in range(2)]
        C3 = at("m", [48])
        E3 = [at("m", [48]) for _ in range(2)]
        DTW = [at("m", [16]) for _ in range(2)]
        SQ = [at("m", [4]) for _ in range(2)]
        NV = [at("m", [4]) for _ in range(2)]
        NY = [at("m", [4]) for _ in range(2)]
        NW = [at("m", [4]) for _ in range(2)]
        ANEG = at("m", [4])

        BANK = [ps(f"bank{i}") for i in range(8)]
        psT, psA, psB, psX, psR, psY, psS, psO = BANK
        psTr = [BANK[0], BANK[1]]
        psL = BANK[2]
        psC = BANK[3]
        psHid = [[BANK[2], BANK[3]], [BANK[4], BANK[5]]]
        psOut = [BANK[6], BANK[7]]

        s_cst, s_small, s_wmam, s_w1, s_x, s_out = (sem(n) for n in ("s_cst", "s_small", "s_wmam", "s_w1", "s_x", "s_out"))
        s_zero = sem("s_zero")
        zero_ready = sem("zero_ready")
        pool_tick = sem("pool_tick")
        o_dve, o_pool = sem("o_dve"), sem("o_pool")
        xn_ready, xn_transposed, xnt_ready, xn_kept, logits_done = (
            sem(n) for n in ("xn_ready", "xn_transposed", "xnt_ready", "xn_kept", "logits_done"))
        shifted, exped, chosen, counted, placed, gap_ready, gap_exped, tiles_known = (
            sem(n) for n in ("shifted", "exped", "chosen", "counted", "placed", "gap_ready", "gap_exped", "tiles_known"))
        scattered = [sem(f"scattered{c}") for c in range(2 * GROUPS)]
        slots_in = [sem(f"slots_in{i}") for i in range(TR)]
        slots_out = [sem(f"slots_out{i}") for i in range(TR)]
        slots_turned, slots_ready, w1_ready, hidden_done, relu_act, relu_dve, rows_done, rows_ready = (
            sem(n) for n in ("slots_turned", "slots_ready", "w1_ready", "hidden_done", "relu_act", "relu_dve",
                             "rows_done", "rows_ready"))
        gathered = [[sem(f"gathered{g}_{i}") for i in range(GT // GTILES)] for g in range(GROUPS)]
        combined = sem("combined")
        (m_un, m_unT, m_ut, m_ip, m_xr, m_z, m_sz, m_cvd, m_cvp, m_xc, m_va, m_ee, m_rd, m_da, m_col, m_c3, m_e3,
         m_sl, m_tx, m_r, m_xt, m_rm, m_ex, m_xd, m_mt, m_y, m_st, m_s, m_u, m_gy, m_gt, m_gc, m_o, m_sq, m_seed,
         m_nw, m_h, m_hn, m_hT, m_ht, m_ga, m_up, m_sg, m_at, m_dn, m_xh, m_fx, m_set, m_sqh, m_alog) = (
            sem("m_" + n) for n in
            ("un unT ut ip xr z sz cvd cvp xc va ee rd da col c3 e3 sl tx r xt rm ex xd mt y st s u gy gt gc o sq seed"
             " nw h hn hT ht ga up sg at dn xh fx set sqh alog").split())

        block = ctx.enter_context(nc.Block())
        def load_ids(engine, g, j, n):
            return nc.values_load_multi_w_load_instructions(eid[g][0:1, ds(j, n)], engines=[engine],
                                                            min_val=0, max_val=NE - 1)[1]

        CALLS = [(f, g) for f in range(2) for g in range(GROUPS)]
        DMAS = 16
        TURNS = (NT - 3) // TR
        of_ring = [(NT - i + TR - 1) // TR for i in range(TR)]

        @block.sync
        def _(sp):
            sp.dma_start(CST[:, :], cst).then_inc(s_cst, DMAS)
            sp.dma_start(SMALL[:, :], small).then_inc(s_small, DMAS)
            for g in range(GROUPS):
                sp.dma_start(X[:, g * GT:(g + 1) * GT, :], x_v[:, g * GT:(g + 1) * GT, :]).then_inc(s_x, DMAS)
                sp.wait_ge(s_x, DMAS * (g + 1))
            sp.dma_start(W1[:, :, :], w1p).then_inc(s_w1, DMAS)
            sp.dma_start(W2[:, :, :, :], w2p).then_inc(s_w1, DMAS)
            sp.dma_start(B2[:, :, :], b2p).then_inc(s_w1, DMAS)
            sp.wait_ge(zero_ready, 1)
            for g in range(GROUPS):
                sp.dma_start(xs[g].rearrange("(p a) c -> p a c", p=P), rep(zeros[:, :], NT * SLOTS // P)
                             ).then_inc(s_zero, DMAS)
            sp.dma_start(WMAM[:, :], wmam).then_inc(s_wmam, DMAS)

            def slots_load(c, g, j, par):
                wait(sp, slots_turned, c * NT + j - TR + 1)
                sp.dma_start(xt[par], xs[g][ds(j * SLOTS, SLOTS), :].rearrange("(a p) c -> p a c", p=P)
                             ).then_inc(slots_in[par], DMAS)

            def slots_store(c, g, j, par):
                sp.wait_ge(rows_ready, c * NT + j + 1)
                sp.dma_start(ys[g][ds(j * SLOTS, SLOTS), :].rearrange("(a p) c -> p a c", p=P), Yb[par]
                             ).then_inc(slots_out[par], DMAS)

            for c, (f, g) in enumerate(CALLS):
                sp.wait_ge(scattered[c], DMAS * 2 * GT)
                if f == 1 and g == 0:
                    sp.wait_ge(m_fx, QUADS)
                for u in range(TR):
                    slots_load(c, g, u, u)
                with sp.Fori(0, TURNS - 1) as jj:
                    for u in range(TR):
                        slots_load(c, g, TR * jj + u + TR, u)
                        slots_store(c, g, TR * jj + u, u)
                for j in range(TR * (TURNS - 1), NT):
                    if j + TR < NT:
                        slots_load(c, g, j + TR, j % TR)
                    slots_store(c, g, j, j % TR)
                if g == GROUPS - 1 and f == 1:
                    for t in range(0, TILES, GTILES):
                        sp.wait_ge(combined, TILES + t + GTILES)
                        sp.dma_start(out_v[:, t:t + GTILES, :], X[:, t:t + GTILES, :]).then_inc(s_out, DMAS)
            sp.wait_ge(s_out, DMAS * TILES // GTILES)

        @block.gpsimd
        def _(pool):
            own = Steps(pool, o_pool, pool_tick)
            pool.memset(zeros[:, :], 0.0).then_inc(zero_ready, 1)

            def scatter(c, g):
                pool.wait_ge(placed, c + 1)
                pool.wait_ge(xn_kept, (c + 1) * GT // 4)
                pool.wait_ge(s_zero, DMAS * GROUPS)
                for t in range(GT):
                    for w in range(2):
                        pool.indirect_dma_start(
                            out=xs[g], out_offset=bass.IndirectOffsetOnAxis(ap=pos[g][:, w, t:t + 1], axis=0),
                            in_=XN[:, g * GT + t, :], in_offset=None).then_inc(scattered[c], DMAS)

            def gather(c, g):
                for u in range(TR):
                    pool.wait_ge(slots_out[u], DMAS * of_ring[u] * (c + 1))
                if g == GROUPS - 1:
                    pool.wait_ge(scattered[c], DMAS * 2 * GT)
                    pool.wait_ge(scattered[c - 1], DMAS * 2 * GT)
                for t in range(GT):
                    for w in range(2):
                        pool.indirect_dma_start(
                            out=GB[g][:, t, w, :], out_offset=None, in_=ys[g],
                            in_offset=bass.IndirectOffsetOnAxis(ap=pos[g][:, w, t:t + 1], axis=0)
                        ).then_inc(gathered[g][t // GTILES], DMAS)

            def hold(sem, value):
                if isinstance(value, int) and value <= 0:
                    return
                pool.wait_ge(sem, value)
                pool.sem_inc(pool_tick, 1)

            def softplus_a(k, u):
                hold(m_sz, QT * k + QT)
                hold(m_da, k)
                own.link(pool.tensor_tensor(V.rearrange("p (a b) -> p a b", a=QT),
                                            DTR[u].rearrange("p (a b) -> p a b", a=QT), rep(sm("dtb"), QT), ALU.add))
                own.link(pool.tensor_scalar(VA, V, 0.0, None, ALU.min))
                own.link(pool.tensor_scalar(V, V, 0.0, None, ALU.max))
                pool.tensor_tensor(VA, VA, V, ALU.subtract).then_inc(m_va, 1)

            def softplus_b(k, u):
                hold(m_rd, k + 1)
                own.link(pool.tensor_tensor(SS_, EE, RD, ALU.mult))
                own.link(pool.tensor_tensor(S2, SS_, SS_, ALU.mult))
                own.link(pool.tensor_scalar(PO, S2, 2.0 / 15, 2.0 / 13, ALU.mult, ALU.add))
                for d in (11, 9, 7, 5, 3, 1):
                    own.link(pool.tensor_tensor(PO, PO, S2, ALU.mult))
                    own.link(pool.tensor_scalar(PO, PO, 1.0, 2.0 / d, ALU.mult, ALU.add))
                own.link(pool.tensor_tensor(PO, PO, SS_, ALU.mult))
                own.link(pool.tensor_tensor(DT[u], PO, V, ALU.add))
                pool.tensor_tensor(DA[u].rearrange("p (a b) -> p a b", a=QT),
                                   DT[u].rearrange("p (a b) -> p a b", a=QT), rep(ANEG, QT), ALU.mult
                                   ).then_inc(m_da, 1)

            def newton(n, u):
                hold(m_seed, n)
                for it in range(3):
                    own.link(pool.tensor_tensor(NW[u], NY[u], NY[u], ALU.mult))
                    own.link(pool.tensor_tensor(NW[u], NW[u], NV[u], ALU.mult))
                    own.link(pool.tensor_scalar(NW[u], NW[u], -0.5, 1.5, ALU.mult, ALU.add))
                    last = pool.tensor_tensor(NY[u], NY[u], NW[u], ALU.mult)
                    if it < 2:
                        own.link(last)
                last.then_inc(m_nw, 1)

            def decay(k, u, i):
                hold(m_da, k + 1)
                hold(m_r, QT * k + i - 1)
                pool.tensor_tensor(SLH[i % 2], rep(LOW, HEADS), bc(DA[u][:, 4 * i:4 * i + 4], P), ALU.mult
                                   ).then_inc(m_sl, 1)

            def residual(k):
                hold(m_h, k + 1)
                hold(m_fx, k)
                pool.tensor_tensor(XH, X[:, ds(QT * k, QT), :], HH, ALU.add).then_inc(m_xh, 1)

            def norm_h(k):
                hold(m_nw, 2 * k + 2)
                hold(m_hT, k)
                pool.tensor_tensor(HN, HH, bc(NY[1], P), ALU.mult).then_inc(m_hn, 1)

            def step(k, u, ahead, now, back):
                if back:
                    newton(2 * k - 1, 0)
                    newton(2 * k, 1)
                if ahead:
                    softplus_a(k + 1, 1 - u)
                if back:
                    norm_h(k - 1)
                    residual(k - 1)
                if ahead:
                    softplus_b(k + 1, 1 - u)
                    for i in range(QT):
                        decay(k + 1, 1 - u, i)

            for f in range(2):
                for g in range(GROUPS):
                    scatter(2 * f + g, g)
                for g in range(GROUPS):
                    gather(2 * f + g, g)
                if f == 0:
                    pool.wait_ge(m_set, 1)
                    step(-1, 1, True, False, False)
                    step(0, 0, True, True, False)
                    with pool.Fori(0, QUADS // 2 - 1) as b:
                        own.enter(b, POOL_PER)
                        for u in (1, 0):
                            step(2 * b + (2 - u), u, True, True, True)
                        own.leave(QUADS // 2 - 1)
                    step(QUADS - 1, 1, False, True, True)
                    step(QUADS, 0, False, False, True)

        @block.scalar
        def _(act):
            def route(c, g):
                q0 = c * GT // 4
                with act.Fori(0, GT // 8) as mm:
                    for u in range(2):
                        m = 2 * mm + u
                        act.wait_ge(xn_transposed, q0 + m + 1)
                        act.wait_ge(logits_done, q0 + 2 * mm)
                        act.activation(xnT[u], psTr[u][:, :], ACT.Copy).then_inc(xnt_ready, 1)
                        act.activation(XN[:, ds(g * GT + 4 * m, 4), :], xq[u], ACT.Copy).then_inc(xn_kept, 1)
                act.wait_ge(shifted, c + 1)
                act.activation(R[1], R[0], ACT.Exp).then_inc(exped, 1)
                act.wait_ge(gap_ready, c + 1)
                act.activation(rb[:, 6, :], rb[:, 5, :], ACT.Exp).then_inc(gap_exped, 1)

            def slots_T(c, j, par):
                act.wait_ge(slots_turned, c * NT + j + 1)
                wait(act, hidden_done, c * NT + j - 1)
                act.activation(xT[par], psTr[par][:, 0:256], ACT.Copy).then_inc(slots_ready, 1)

            def relu(c, j, par):
                act.wait_ge(hidden_done, c * NT + j + 1)
                for h in range(2):
                    last = act.activation(Hh[par][:, h, :], psHid[par][h // 2][:, (h % 2) * 256:(h % 2) * 256 + 256],
                                          ACT.Relu, bias=w1c[par][:, HID + h:HID + h + 1])
                last.then_inc(relu_act, 1)

            def experts(c):
                slots_T(c, 0, 0)
                with act.Fori(0, (NT - 1) // 2) as jj:
                    for u in range(2):
                        j = 2 * jj + u
                        relu(c, j, u)
                        slots_T(c, j + 1, 1 - u)
                relu(c, NT - 1, 0)

            def un_T(k):
                act.wait_ge(m_unT, k + 1)
                wait(act, m_z, QT * k)
                act.activation(UT, psA[:, :], ACT.Copy, scale=sm("pre")).then_inc(m_ut, 1)

            def xr(k, u, b):
                act.wait_ge(m_ip, QT * k + b + 1)
                wait(act, m_cvd, len(CONV_DVE) * (k if u == 0 else k - 1))
                wait(act, m_cvp, k if u == 0 else k - 1)
                if u == 1 and b == 0:
                    act.activation(XR[1][:, :, 0:3], XR[0][:, :, QT * P:QT * P + 3], ACT.Copy)
                act.activation(XR[u][:, b, 3:515], (psB, psA)[b % 2][:, :], ACT.Copy).then_inc(m_xr, 1)

            def sz(k, u, i):
                act.wait_ge(m_z, QT * k + i + 1)
                wait(act, m_gy, QT * (k - 1))
                act.activation(DTR[u][:, 4 * i:4 * i + 4], (psB, psA)[i % 2][:, 256:260], ACT.Copy)
                act.activation(SZ[u][:, i, :], (psB, psA)[i % 2][:, 0:256], ACT.Silu).then_inc(m_sz, 1)

            def xt_(k, i):
                I = QT * k + i
                act.wait_ge(m_tx, I + 1)
                wait(act, m_st, I - 1)
                wait(act, m_xd, I - 1)
                wait(act, m_mt, I - 1)
                act.activation(XT[i % 2], psX[:, :], ACT.Copy).then_inc(m_xt, 1)

            def exp_r(k, i):
                act.wait_ge(m_rm, QT * k + i + 1)
                wait(act, m_mt, QT * (k - 1) + i + 1)
                act.activation(EX[i], RM[i % 2], ACT.Exp).then_inc(m_ex, 1)

            def square(k, i):
                I = QT * k + i
                act.wait_ge(m_gy, I + 1)
                wait(act, m_sq, I)
                if i == 0:
                    wait(act, m_seed, 2 * k - 1)
                act.activation(JK, GY[i % 2], ACT.Square, accum_out=SQ[0][:, i:i + 1]).then_inc(m_sq, 1)
                act.wait_ge(m_gt, I + 1)
                wait(act, m_o, I - 1)
                act.activation(GTr[i % 2], psT[:, (i % 2) * 256:(i % 2) * 256 + 256], ACT.Copy).then_inc(m_gc, 1)

            def exp_a(k):
                act.wait_ge(m_va, k + 1)
                act.activation(EE, VA, ACT.Exp).then_inc(m_ee, 1)

            def exp_b(k, u):
                act.wait_ge(m_c3, k + 1)
                act.activation(E3[u], C3, ACT.Exp).then_inc(m_e3, 1)

            def h_T(k):
                act.wait_ge(m_hT, k + 1)
                wait(act, m_up, QT * k)
                act.activation(HT, psB[:, :], ACT.Copy, scale=sm("post")).then_inc(m_ht, 1)

            def gate(k, b):
                act.wait_ge(m_ga, QT * k + b + 1)
                if b >= 2:
                    act.wait_ge(m_at, QT * k + b - 1)
                act.activation(SG[b % 2], psA[:, :], ACT.Silu).then_inc(m_sg, 1)

            def square_h(k):
                act.wait_ge(m_h, k + 1)
                wait(act, m_seed, 2 * k)
                for i in range(QT):
                    wait(act, m_sqh, QT * k + i)
                    act.activation(JH, HH[:, i, :], ACT.Square, accum_out=SQ[1][:, i:i + 1]).then_inc(m_sqh, 1)

            def conv_silu(k, u, b):
                if b in CONV_DVE:
                    act.wait_ge(m_cvd, len(CONV_DVE) * k + CONV_DVE.index(b) + 1)
                    taps = CV[:, b, :]
                else:
                    act.wait_ge(m_cvp, k + 1)
                    taps = psR[:, :]
                wait(act, m_y, QT * (k - 1))
                act.activation(XC[u][:, b, :], taps, ACT.Silu, bias=sm("convb")[:, b:b + 1]).then_inc(m_xc, 1)

            def step(k, u, ahead, now, back):
                n, v = k + 1, 1 - u
                if now:
                    xt_(k, 0)
                if ahead:
                    un_T(n)
                if back:
                    square(k - 1, QT - 1)
                if now:
                    xt_(k, 1)
                if ahead:
                    for b in range(4):
                        xr(n, v, b)
                if now:
                    square(k, 0)
                if back:
                    square_h(k - 1)
                if ahead:
                    sz(n, v, 0)
                    sz(n, v, 1)
                if now:
                    xt_(k, 2)
                if ahead:
                    sz(n, v, 2)
                    sz(n, v, 3)
                if now:
                    square(k, 1)
                if ahead:
                    exp_a(n)
                if now:
                    xt_(k, 3)
                if back:
                    h_T(k - 1)
                if ahead:
                    conv_silu(n, v, CONV_PE)
                    conv_silu(n, v, CONV_DVE[0])
                if back:
                    gate(k - 1, 0)
                if ahead:
                    conv_silu(n, v, CONV_DVE[1])
                if now:
                    square(k, 2)
                if back:
                    gate(k - 1, 1)
                    gate(k - 1, 2)
                if ahead:
                    conv_silu(n, v, CONV_DVE[2])
                if back:
                    gate(k - 1, 3)
                if ahead:
                    exp_b(n, v)
                    for i in range(QT):
                        exp_r(n, i)

            for f in range(2):
                for g in range(GROUPS):
                    route(2 * f + g, g)
                for g in range(GROUPS):
                    experts(2 * f + g)
                if f == 0:
                    act.wait_ge(s_small, DMAS)
                    act.wait_ge(combined, TILES)
                    act.activation(ANEG, sm("alog"), ACT.Exp).then_inc(m_alog, 1)
                    step(-1, 1, True, False, False)
                    step(0, 0, True, True, False)
                    with act.Fori(0, QUADS // 2 - 1) as b:
                        for u in (1, 0):
                            step(2 * b + (2 - u), u, True, True, True)
                    step(QUADS - 1, 1, False, True, True)
                    step(QUADS, 0, False, False, True)

        @block.tensor
        def _(pe):
            pe.wait_ge(s_cst, DMAS)
            pe.wait_ge(s_small, DMAS)

            def route(c):
                q0 = c * GT // 4
                with pe.Fori(0, GT // 8) as mm:
                    for u in range(2):
                        m = 2 * mm + u
                        pe.wait_ge(xn_ready, q0 + m + 1)
                        for i in range(4):
                            last = pe.transpose(psTr[u][:, i * P:(i + 1) * P], xq[u][:, i, :], IDENT)
                        last.then_inc(xn_transposed, 1)
                        pe.wait_ge(xnt_ready, q0 + m + 1)
                        for i in range(4):
                            last = pe.matmul(psL[:, ds((4 * m + i) * NE, NE)], xnT[u][:, i * P:(i + 1) * P], sm("wg"),
                                             start=True, stop=True)
                        last.then_inc(logits_done, 1)
                pe.wait_ge(chosen, c + 1)
                oh = R[4].rearrange("p a b -> p (a b)")
                pe.matmul(psC[:, 0:256], UP, oh, start=True, stop=True)
                pe.matmul(psC[:, 256:512], ONE, oh, start=True, stop=True).then_inc(counted, 1)

            def turn(c, j, jj, r):
                par = r % 2
                pe.wait_ge(slots_in[r], DMAS * (of_ring[r] * c + jj + 1))
                for a in range(2):
                    last = pe.transpose(psTr[par][:, a * P:(a + 1) * P], xt[r][:, a, :], IDENT)
                last.then_inc(slots_turned, 1)

            def up_proj(c, j, par):
                pe.wait_ge(slots_ready, c * NT + j + 1)
                pe.wait_ge(w1_ready, c * NT + j + 1)
                for h in range(HB):
                    last = pe.matmul(psHid[par][h // 2][:, (h % 2) * 256:(h % 2) * 256 + 256],
                                     w1c[par][:, h * P:(h + 1) * P], xT[par], start=True, stop=True)
                last.then_inc(hidden_done, 1)

            def down_proj(c, e, j, par):
                pe.wait_ge(relu_act, c * NT + j + 1)
                pe.wait_ge(relu_dve, c * NT + j + 1)
                for a in range(2):
                    for h in range(HB):
                        last = pe.matmul(psOut[par][:, a * P:(a + 1) * P],
                                         Hh[par][:, h, a * P:(a + 1) * P], W2[:, ds(e, 1), h, :],
                                         start=(h == 0), stop=(h == HB - 1))
                last.then_inc(rows_done, 1)
                wait(pe, rows_ready, c * NT + j)

            def experts(c, g):
                pe.wait_ge(tiles_known, c + 1)
                turn(c, 0, 0, 0)
                up_proj(c, 0, 0)
                turn(c, 1, 0, 1)
                with pe.Fori(0, TURNS) as jj:
                    e = load_ids(EngineType.PE, g, TR * jj, TR)
                    for u in range(TR):
                        j = TR * jj + u
                        up_proj(c, j + 1, (u + 1) % 2)
                        turn(c, j + 2, jj + (u + 2) // TR, (u + 2) % TR)
                        down_proj(c, e[u], j, u % 2)
                e = load_ids(EngineType.PE, g, NT - 3, 3)
                up_proj(c, NT - 2, (NT - 2) % 2)
                turn(c, NT - 1, (NT - 1) // TR, (NT - 1) % TR)
                down_proj(c, e[0], NT - 3, (NT - 3) % 2)
                up_proj(c, NT - 1, (NT - 1) % 2)
                down_proj(c, e[1], NT - 2, (NT - 2) % 2)
                down_proj(c, e[2], NT - 1, (NT - 1) % 2)

            def turn_un(k):
                pe.wait_ge(m_un, k + 1)
                wait(pe, m_sz, QT * k)
                wait(pe, m_sg, QT * (k - 2))
                for i in range(QT):
                    last = pe.transpose(psA[:, i * P:(i + 1) * P], UN[:, i, :], IDENT)
                last.then_inc(m_unT, 1)

            def in_proj(k, b):
                if b == 0:
                    pe.wait_ge(m_ut, k + 1)
                    wait(pe, m_fx, k - 2)
                if b >= 2:
                    pe.wait_ge(m_xr, QT * k + b - 1)
                pe.matmul((psB, psA)[b % 2][:, :], wm("wx")[:, b * P:(b + 1) * P], UT, start=True, stop=True
                          ).then_inc(m_ip, 1)

            def z_proj(k, i):
                if i < 2:
                    pe.wait_ge(m_xr, QT * k + 3 + i)
                else:
                    pe.wait_ge(m_sz, QT * k + i - 1)
                pe.matmul((psB, psA)[i % 2][:, 0:260], UT[:, i * P:(i + 1) * P], wm("wz"), start=True, stop=True
                          ).then_inc(m_z, 1)

            def sums(k, u):
                pe.wait_ge(m_da, k + 1)
                wait(pe, m_s, QT * k)
                pe.matmul(psS[:, 256:272], TRI, DA[u], start=True, stop=True)
                pe.matmul(psS[:, 272:288], ONE, DA[u], start=True, stop=True).then_inc(m_col, 1)

            def conv(k, u):
                pe.wait_ge(m_xr, QT * k + QT)
                wait(pe, m_rm, QT * k)
                for t in range(4):
                    last = pe.matmul(psR[:, :], CT[:, t, :], XR[u][:, CONV_PE, t:t + 512], start=(t == 0), stop=(t == 3))
                last.then_inc(m_cvp, 1)

            def decay(k, i):
                pe.wait_ge(m_sl, QT * k + i + 1)
                if i == 0:
                    pe.wait_ge(m_xc, QT * k + 1)
                elif i == 1:
                    wait(pe, m_xt, QT * k)
                else:
                    pe.wait_ge(m_rm, QT * k + (1, 3)[i - 2])
                R = psX if i == 1 else psR
                for h in range(HEADS):
                    last = pe.matmul(R[:, h * P:(h + 1) * P], SLH[i % 2][:, h, :], TRI, start=True, stop=True)
                last.then_inc(m_r, 1)

            def chunk_a(k, u, i):
                I = QT * k + i
                if i == 0:
                    pe.wait_ge(m_xc, QT * k + QT)
                    pe.wait_ge(m_rm, QT * k + 2)
                wait(pe, m_xt, I)
                for b in range(3):
                    last = pe.transpose(psX[:, b * P:(b + 1) * P], XC[u][:, b, i * P:(i + 1) * P], IDENT)
                pe.matmul(psX[:, 384:512], XC[u][:, 2, i * P:(i + 1) * P],
                          XC[u][:, 3, i * P:(i + 1) * P], start=True, stop=True).then_inc(m_tx, 1)

            def chunk_b(k, u, i):
                I = QT * k + i
                first = u == 0 and i == 0
                wait(pe, m_gy, I)
                for b in range(2):
                    pe.matmul(psY[:, b * P:(b + 1) * P], XC[u][:, b, i * P:(i + 1) * P], DG[:, b, :],
                              start=(b == 0), stop=False)
                pe.wait_ge(m_xd, I + 1)
                pe.wait_ge(m_mt, I + 1)
                for h in range(HEADS):
                    last = pe.matmul(psY[:, h * HD:(h + 1) * HD], MT[i % 2][:, h, :], XD[i % 2][:, h * HD:(h + 1) * HD],
                                     start=False, stop=(h == HEADS - 1))
                wait(pe, m_s, I)
                if not first:
                    last = pe.matmul(psY[:, 256:512], XC[u][:, 3, i * P:(i + 1) * P], S, start=True, stop=True)
                last.then_inc(m_y, 1)
                pe.wait_ge(m_c3, k + 1)
                pe.matmul(psS[:, 0:256], XT[i % 2][:, 256:384], XW[i % 2], start=True, stop=True).then_inc(m_st, 1)

            def turn_g(k, i):
                I = QT * k + i
                pe.wait_ge(m_gy, I + 1)
                wait(pe, m_gc, I)
                for b in range(2):
                    last = pe.transpose(psT[:, (i % 2) * 256 + b * P:(i % 2) * 256 + (b + 1) * P],
                                        GY[i % 2][:, b * P:(b + 1) * P], IDENT)
                last.then_inc(m_gt, 1)

            def out_proj(k, i):
                I = QT * k + i
                if i == 0:
                    wait(pe, m_h, k)
                pe.wait_ge(m_gc, I + 1)
                for b in range(2):
                    last = pe.matmul(psO[:, i * P:(i + 1) * P], GTr[i % 2][:, b * P:(b + 1) * P],
                                     wm("wout")[:, b * P:(b + 1) * P], start=(b == 0), stop=(b == 1))
                last.then_inc(m_o, 1)

            def turn_h(k):
                pe.wait_ge(m_hn, k + 1)
                pe.wait_ge(m_sz, m_sz_all(k))
                wait(pe, m_fx, k)
                for i in range(QT):
                    last = pe.transpose(psB[:, i * P:(i + 1) * P], HN[:, i, :], IDENT)
                last.then_inc(m_hT, 1)

            def m_sz_all(k):
                return QT * (k + 3) if not isinstance(k, int) or k + 3 <= QUADS else QT * QUADS

            def gate_up(k, b):
                if b == 0:
                    pe.wait_ge(m_ht, k + 1)
                wait(pe, m_sg, QT * k + b)
                pe.matmul(psA[:, :], wm("gate")[:, b * P:(b + 1) * P], HT, start=True, stop=True).then_inc(m_ga, 1)
                wait(pe, m_at, QT * k + b)
                pe.matmul(psB[:, :], wm("up")[:, b * P:(b + 1) * P], HT, start=True, stop=True).then_inc(m_up, 1)

            def down(k):
                pe.wait_ge(m_at, QT * k + QT)
                for i in range(QT):
                    for b in range(4):
                        last = pe.matmul(psB[:, i * P:(i + 1) * P], AT[:, b, i * P:(i + 1) * P],
                                         wm("down")[:, b * P:(b + 1) * P], start=(b == 0), stop=(b == 3))
                last.then_inc(m_dn, 1)

            def step(k, u, ahead, now, back):
                n, v = k + 1, 1 - u
                if now:
                    chunk_a(k, u, 0)
                if back:
                    turn_g(k - 1, QT - 1)
                if ahead:
                    turn_un(n)
                if now:
                    chunk_a(k, u, 1)
                    chunk_b(k, u, 0)
                if ahead:
                    in_proj(n, 0)
                if back:
                    out_proj(k - 1, QT - 1)
                if ahead:
                    in_proj(n, 1)
                    in_proj(n, 2)
                if now:
                    turn_g(k, 0)
                if ahead:
                    in_proj(n, 3)
                if now:
                    chunk_b(k, u, 1)
                    chunk_a(k, u, 2)
                if ahead:
                    z_proj(n, 0)
                    z_proj(n, 1)
                if now:
                    out_proj(k, 0)
                if ahead:
                    z_proj(n, 2)
                    z_proj(n, 3)
                if now:
                    turn_g(k, 1)
                    chunk_b(k, u, 2)
                    chunk_a(k, u, 3)
                    out_proj(k, 1)
                if back:
                    turn_h(k - 1)
                if ahead:
                    conv(n, v)
                if back:
                    gate_up(k - 1, 0)
                if now:
                    turn_g(k, 2)
                    chunk_b(k, u, 3)
                if back:
                    gate_up(k - 1, 1)
                if now:
                    out_proj(k, 2)
                if back:
                    gate_up(k - 1, 2)
                if ahead:
                    sums(n, v)
                    decay(n, 0)
                if back:
                    gate_up(k - 1, 3)
                if ahead:
                    decay(n, 1)
                if back:
                    down(k - 1)
                if ahead:
                    decay(n, 2)
                    decay(n, 3)

            for f in range(2):
                for g in range(GROUPS):
                    route(2 * f + g)
                if f == 0:
                    pe.wait_ge(s_w1, DMAS * 3)
                for g in range(GROUPS):
                    experts(2 * f + g, g)
                if f == 0:
                    pe.wait_ge(s_wmam, DMAS)
                    pe.wait_ge(m_set, 1)
                    step(-1, 1, True, False, False)
                    step(0, 0, True, True, False)
                    with pe.Fori(0, QUADS // 2 - 1) as b:
                        for u in (1, 0):
                            step(2 * b + (2 - u), u, True, True, True)
                    step(QUADS - 1, 1, False, True, True)
                    step(QUADS, 0, False, False, True)

        @block.vector
        def _(dve):
            own = Steps(dve, o_dve)
            link = own.link

            def stats(t0, n):
                with dve.Fori(0, n // 4) as a:
                    for i in range(4):
                        t = t0 + 4 * a + i
                        last = dve.bn_stats(st6[:, ds(t, 1), :], X[:, ds(t, 1), :])
                    own.enter(a, 1)
                    own.mark(last)
                    own.leave(n // 4)
                dve.wait_ge(o_dve, own.base + own.n)

            def root(v, y, w):
                link(dve.tensor_single_scalar(y.bitcast(I32), v.bitcast(I32), 1, ALU.arith_shift_right))
                link(dve.tensor_scalar(y.bitcast(I32), y.bitcast(I32), -1.0, MAGIC, ALU.mult, ALU.add))
                for _ in range(3):
                    link(dve.tensor_tensor(w, y, y, ALU.mult))
                    link(dve.scalar_tensor_tensor(w, w, -0.5, v, ALU.mult, ALU.mult))
                    link(dve.scalar_tensor_tensor(y, w, 1.5, y, ALU.add, ALU.mult))

            def moments(t0, n):
                m, v, w = mean[:, t0:t0 + n], va2[:, 0, t0:t0 + n], nw[:, 0:n]
                m0, m1, q0, q1 = (st6[:, t0:t0 + n, c] for c in (1, 4, 2, 5))
                link(dve.tensor_tensor(m, m0, m1, ALU.add))
                link(dve.tensor_scalar(m, m, 0.5, None, ALU.mult))
                link(dve.tensor_tensor(w, m0, m1, ALU.subtract))
                link(dve.tensor_tensor(w, w, w, ALU.mult))
                link(dve.tensor_tensor(v, q0, q1, ALU.add))
                link(dve.tensor_scalar(v, v, 1.0 / P, LN_EPS, ALU.mult, ALU.add))
                link(dve.scalar_tensor_tensor(v, w, 0.25, v, ALU.mult, ALU.add))

            def route(c, g):
                t0, q0 = g * GT, c * GT // 4
                stats(t0, GT)
                moments(t0, GT)
                root(va2[:, 0, t0:t0 + GT], rs2[:, 0, t0:t0 + GT], nw[:, 0:GT])
                start = own.base + own.n
                with dve.Fori(0, GT // 8) as mm:
                    own.enter(mm, 2)
                    for u in range(2):
                        m = 2 * mm + u
                        t = t0 + 4 * m
                        dve.wait_ge(xn_kept, q0 + 2 * mm)
                        dve.wait_ge(xn_transposed, q0 + 2 * mm)
                        link(dve.tensor_tensor(xq[u], X[:, ds(t, 4), :], bc(mean[:, ds(t, 4)], P), ALU.subtract))
                        dve.tensor_tensor(xq[u], xq[u], bc(rs2[:, 0, ds(t, 4)], P), ALU.mult).then_inc(xn_ready, 1)
                    own.leave(GT // 8)
                L, Pr, T, O1, A, O2, C0, C1 = R
                row = lambda i: rb[:, i, :]
                dve.wait_ge(logits_done, q0 + GT // 4)
                link(dve.tensor_tensor(L, psL[:, 0:GT * NE].rearrange("p (a b) -> p a b", b=NE), rep(sm("bg"), GT), ALU.add))
                link(dve.tensor_reduce(row(0), L, AX, ALU.max))
                dve.tensor_tensor(L, L, bc(row(0), NE), ALU.subtract).then_inc(shifted, 1)
                dve.wait_ge(exped, c + 1)
                link(dve.tensor_reduce(row(1), Pr, AX, ALU.add))
                link(dve.reciprocal(row(2), row(1)))
                link(dve.tensor_tensor(Pr, Pr, bc(row(2), NE), ALU.mult))
                for w, (src, oh) in enumerate(((Pr, O1), (A, O2))):
                    link(dve.tensor_reduce(row(3 + w), src, AX, ALU.max))
                    link(dve.tensor_tensor(T, src, bc(row(3 + w), NE), ALU.is_equal))
                    link(dve.tensor_tensor(T, T, rep(E8, GT), ALU.mult))
                    link(dve.tensor_reduce(row(7), T, AX, ALU.min))
                    link(dve.tensor_tensor(oh, rep(E8, GT), bc(row(7), NE), ALU.is_equal))
                    if w == 0:
                        link(dve.scalar_tensor_tensor(A, oh, -2.0, Pr, ALU.mult, ALU.add))
                dve.tensor_tensor(row(5), row(4), row(3), ALU.subtract).then_inc(gap_ready, 1)
                dve.tensor_tensor(A, O1, O2, ALU.add).then_inc(chosen, 1)
                dve.wait_ge(gap_exped, c + 1)
                link(dve.tensor_scalar(row(8), row(6), 1.0, None, ALU.add))
                link(dve.reciprocal(row(9), row(8)))
                link(dve.tensor_scalar(wtop[g][:, 0, :], row(9), 0.5, None, ALU.mult))
                link(dve.tensor_tensor(wtop[g][:, 1, :], wtop[g][:, 0, :], row(6), ALU.mult))
                dve.wait_ge(counted, c + 1)
                cnt = psC[:, 256:512].rearrange("p (a b) -> p a b", b=NE)
                link(dve.tensor_copy(C0, cnt))
                a, b = C0, C1
                s = 1
                while s < GT:
                    own.mark(dve.tensor_copy(b[:, 0:s, :], a[:, 0:s, :]))
                    link(dve.tensor_tensor(b[:, s:GT, :], a[:, s:GT, :], a[:, 0:GT - s, :], ALU.add))
                    a, b = b, a
                    s *= 2
                tot, nt, inc, inc2, base = (tb[:, i, :] for i in range(5))
                nti = tb[:, 5, :].bitcast(I32)
                link(dve.tensor_scalar(tot, a[:, GT - 1, :], float(SLOTS - 1), None, ALU.add))
                link(dve.tensor_copy(nti, tot))
                link(dve.tensor_single_scalar(nti, nti, SLOTS.bit_length() - 1, ALU.arith_shift_right))
                link(dve.tensor_copy(nt, nti))
                link(dve.tensor_copy(inc, nt))
                s = 1
                while s < NE:
                    own.mark(dve.tensor_copy(inc2[:, 0:s], inc[:, 0:s]))
                    link(dve.tensor_tensor(inc2[:, s:NE], inc[:, s:NE], inc[:, 0:NE - s], ALU.add))
                    inc, inc2 = inc2, inc
                    s *= 2
                link(dve.tensor_tensor(base, inc, nt, ALU.subtract))
                link(dve.tensor_scalar(base, base, float(SLOTS), None, ALU.mult))
                link(dve.tensor_tensor(L, a, cnt, ALU.subtract))
                link(dve.tensor_tensor(L, L, psC[:, 0:256].rearrange("p (a b) -> p a b", b=NE), ALU.add))
                link(dve.tensor_tensor(L, L, rep(base, GT), ALU.add))
                for w, oh in enumerate((O1, O2)):
                    link(dve.tensor_tensor(T, oh, L, ALU.mult))
                    link(dve.tensor_reduce(row(10 + w), T, AX, ALU.add))
                dve.tensor_copy(pos[g][:, :, :], rb[:, 10:12, :]).then_inc(placed, 1)
                link(dve.tensor_tensor(jb[:, :, :], bc(JJ, NE), rep(inc, NT), ALU.is_ge))
                link(dve.tensor_reduce(jf[:, :], jb[:, :, :], AX, ALU.add))
                link(dve.tensor_scalar(jf[:, :], jf[:, :], float(NE - 1), None, ALU.min))
                dve.tensor_copy(eid[g][:, :], jf[:, :]).then_inc(tiles_known, 1)

            def weights(c, e, j, par):
                wait(dve, hidden_done, c * NT + j - 1)
                wait(dve, relu_act, c * NT + j - 1)
                wait(dve, relu_dve, c * NT + j - 1)
                dve.tensor_copy(w1c[par], W1[:, ds(e, 1), :]).then_inc(w1_ready, 1)

            def relu(c, j, par):
                dve.wait_ge(w1_ready, c * NT + j + 1)
                dve.wait_ge(hidden_done, c * NT + j + 1)
                for h in (2, 3):
                    last = dve.tensor_scalar(Hh[par][:, h, :], psHid[par][1][:, (h % 2) * 256:(h % 2) * 256 + 256],
                                             w1c[par][:, HID + h:HID + h + 1], 0.0, ALU.add, ALU.max)
                last.then_inc(relu_dve, 1)

            def rows(c, e, j, jj, r):
                dve.wait_ge(rows_done, c * NT + j + 1)
                wait(dve, slots_out[r], DMAS * (of_ring[r] * c + jj))
                dve.tensor_tensor(Yb[r], psOut[r % 2][:, 0:256].rearrange("p (a b) -> p a b", a=2),
                                  B2[:, ds(e, 1), :].to_broadcast([P, 2, P]), ALU.add).then_inc(rows_ready, 1)

            def experts(c, g):
                dve.wait_ge(tiles_known, c + 1)
                e = load_ids(EngineType.DVE, g, 0, 2)
                weights(c, e[0], 0, 0)
                weights(c, e[1], 1, 1)
                relu(c, 0, 0)
                with dve.Fori(0, TURNS) as jj:
                    e = load_ids(EngineType.DVE, g, TR * jj, TR + 2)
                    for u in range(TR):
                        j = TR * jj + u
                        weights(c, e[u + 2], j + 2, u % 2)
                        relu(c, j + 1, (u + 1) % 2)
                        rows(c, e[u], j, jj, u)
                e = load_ids(EngineType.DVE, g, NT - 3, 3)
                weights(c, e[2], NT - 1, (NT - 1) % 2)
                relu(c, NT - 2, (NT - 2) % 2)
                rows(c, e[0], NT - 3, TURNS, 0)
                relu(c, NT - 1, (NT - 1) % 2)
                rows(c, e[1], NT - 2, TURNS, 1)
                rows(c, e[2], NT - 1, TURNS, 2)

            def combine(c, g):
                for q in range(GT // GTILES):
                    dve.wait_ge(gathered[g][q], 2 * DMAS * GTILES * (c // GROUPS + 1))
                    with dve.Fori(0, GTILES // 4) as tt:
                        own.enter(tt, 4)
                        for s in range(4):
                            t = GTILES * q + 4 * tt + s
                            xrow = X[:, ds(g * GT + t, 1), :]
                            own.mark(dve.scalar_tensor_tensor(xrow, GB[g][:, ds(t, 1), 0, :], wtop[g][:, 0, ds(t, 1)],
                                                              xrow, ALU.mult, ALU.add))
                        dve.wait_ge(o_dve, own.base + own.n)
                        for s in range(4):
                            t = GTILES * q + 4 * tt + s
                            xrow = X[:, ds(g * GT + t, 1), :]
                            dve.scalar_tensor_tensor(xrow, GB[g][:, ds(t, 1), 1, :], wtop[g][:, 1, ds(t, 1)], xrow,
                                                     ALU.mult, ALU.add).then_inc(combined, 1)
                        own.leave(GTILES // 4)

            def norm(k, dst, r):
                for i in range(QT):
                    t = QT * k + i
                    last = dve.tensor_scalar(dst[:, i:i + 1, :], X[:, ds(t, 1), :], mean[:, ds(t, 1)],
                                             rs2[:, r, ds(t, 1)], ALU.subtract, ALU.mult)
                return last

            def norm_both(k):
                wait(dve, m_unT, k)
                norm(k, UN, 1).then_inc(m_un, 1)

            def norm_one(k):
                wait(dve, m_h, k)
                norm(k, U, 0).then_inc(m_u, 1)

            def conv(k, u, b):
                dve.wait_ge(m_xr, QT * k + b + 1)
                wait(dve, m_xc, QT * k)
                w = sm("convw")[:, 4 * b:4 * b + 4]
                link(dve.tensor_scalar(CV[:, b, :], XR[u][:, b, 0:512], w[:, 0:1], None, ALU.mult))
                for t in (1, 2):
                    link(dve.scalar_tensor_tensor(CV[:, b, :], XR[u][:, b, t:t + 512], w[:, t:t + 1],
                                                  CV[:, b, :], ALU.mult, ALU.add))
                dve.scalar_tensor_tensor(CV[:, b, :], XR[u][:, b, 3:515], w[:, 3:4],
                                         CV[:, b, :], ALU.mult, ALU.add).then_inc(m_cvd, 1)

            def heads(ap):
                return ap.rearrange("p (h d) -> p h d", h=HEADS)

            def steps_r(k):
                dve.wait_ge(m_ee, k + 1)
                link(dve.tensor_scalar(RD, EE, 2.0, None, ALU.add))
                dve.reciprocal(RD, RD).then_inc(m_rd, 1)

            def sums(k):
                dve.wait_ge(m_col, k + 1)
                link(dve.tensor_copy(C3[:, 0:32], psS[:, 256:288]))
                dve.tensor_tensor(C3[:, 32:48], C3[:, 16:32], C3[:, 0:16], ALU.subtract).then_inc(m_c3, 1)

            def decay(k, i):
                I = QT * k + i
                dve.wait_ge(m_r, I + 1)
                wait(dve, m_ex, I - 1)
                R = psX if i == 1 else psR
                dve.tensor_tensor(RM[i % 2], R[:, :].rearrange("p (h l) -> p h l", h=HEADS), rep(MINM, HEADS),
                                  ALU.min).then_inc(m_rm, 1)

            def weigh(k, u, i):
                I = QT * k + i
                dve.wait_ge(m_xt, I + 1)
                wait(dve, m_st, I - 1)
                c = slice(4 * i, 4 * i + 4)
                dve.tensor_tensor(heads(XD[i % 2]), heads(XT[i % 2][:, 0:256]), bc(DT[u][:, c], HD), ALU.mult)
                dve.tensor_tensor(heads(XW[i % 2]), heads(XT[i % 2][:, 0:256]), bc(DTW[u][:, c], HD), ALU.mult
                                  ).then_inc(m_xd, 1)
                dve.wait_ge(m_ex, I + 1)
                dve.tensor_tensor(MT[i % 2], EX[i], rep(XT[i % 2][:, 384:512], HEADS), ALU.mult
                                  ).then_inc(m_mt, 1)

            def rates(k, u):
                dve.wait_ge(m_e3, k + 1)
                link(dve.tensor_tensor(DTW[u], DT[u], E3[u][:, 32:48], ALU.mult))

            def output(k, u, i):
                I = QT * k + i
                first = u == 0 and i == 0
                c = slice(4 * i, 4 * i + 4)
                dve.wait_ge(m_st, I + 1)
                if first:
                    dve.tensor_copy(S, psS[:, 0:256]).then_inc(m_s, 1)
                else:
                    dve.wait_ge(m_s, I)
                    link(dve.tensor_tensor(heads(S), heads(S), bc(E3[u][:, 16 + 4 * i:20 + 4 * i], HD), ALU.mult))
                    dve.tensor_tensor(S, S, psS[:, 0:256], ALU.add).then_inc(m_s, 1)
                dve.wait_ge(m_y, I + 1)
                wait(dve, m_gy, I)
                y = psY[:, 0:256]
                if not first:
                    link(dve.tensor_tensor(heads(YY), heads(psY[:, 256:512]), bc(E3[u][:, c], HD), ALU.mult))
                    link(dve.tensor_tensor(YY, YY, y, ALU.add))
                    y = YY
                wait(dve, m_gt, I - 1)
                wait(dve, m_sq, I - 1)
                dve.tensor_tensor(GY[i % 2], y, SZ[u][:, i, :], ALU.mult).then_inc(m_gy, 1)

            def seed(which, width):
                link(dve.tensor_scalar(NV[which], SQ[which], 1.0 / width, RMS_EPS, ALU.mult, ALU.add))
                y = NY[which].bitcast(I32)
                link(dve.tensor_single_scalar(y, NV[which].bitcast(I32), 1, ALU.arith_shift_right))
                dve.tensor_scalar(y, y, -1.0, MAGIC, ALU.mult, ALU.add).then_inc(m_seed, 1)

            def seed_g(k):
                dve.wait_ge(m_sq, QT * k + QT)
                seed(0, 256)

            def seed_h(k):
                dve.wait_ge(m_sqh, QT * k + QT)
                seed(1, P)

            def join(k):
                dve.wait_ge(m_nw, 2 * k + 1)
                dve.wait_ge(m_o, QT * k + QT)
                dve.wait_ge(m_u, k + 1)
                for i in range(QT):
                    last = dve.scalar_tensor_tensor(HH[:, i, :], psO[:, i * P:(i + 1) * P], NY[0][:, i:i + 1],
                                                    U[:, i, :], ALU.mult, ALU.add)
                last.then_inc(m_h, 1)

            def gated(k, b):
                if b == 0:
                    wait(dve, m_dn, k)
                dve.wait_ge(m_sg, QT * k + b + 1)
                dve.wait_ge(m_up, QT * k + b + 1)
                dve.tensor_tensor(AT[:, b, :], psB[:, :], SG[b % 2], ALU.mult).then_inc(m_at, 1)

            def finish(k):
                dve.wait_ge(m_dn, k + 1)
                dve.wait_ge(m_xh, k + 1)
                dve.tensor_tensor(X[:, ds(QT * k, QT), :], psB[:, :].rearrange("p (a b) -> p a b", a=QT), XH, ALU.add
                                  ).then_inc(m_fx, 1)

            def step(k, u, ahead, now, back):
                n, v = k + 1, 1 - u
                if ahead:
                    norm_both(n)
                if now:
                    rates(k, u)
                    weigh(k, u, 0)
                if back:
                    seed_g(k - 1)
                if now:
                    output(k, u, 0)
                    weigh(k, u, 1)
                if back:
                    join(k - 1)
                if ahead:
                    conv(n, v, CONV_DVE[0])
                if back:
                    seed_h(k - 1)
                if now:
                    output(k, u, 1)
                    weigh(k, u, 2)
                if ahead:
                    conv(n, v, CONV_DVE[1])
                    steps_r(n)
                if now:
                    output(k, u, 2)
                    weigh(k, u, 3)
                if back:
                    gated(k - 1, 0)
                if ahead:
                    conv(n, v, CONV_DVE[2])
                if back:
                    gated(k - 1, 1)
                if now:
                    norm_one(k)
                    output(k, u, 3)
                if back:
                    gated(k - 1, 2)
                    gated(k - 1, 3)
                if ahead:
                    sums(n)
                    decay(n, 0)
                    decay(n, 1)
                if back:
                    finish(k - 1)
                if ahead:
                    decay(n, 2)
                    decay(n, 3)

            dve.wait_ge(s_cst, DMAS)
            dve.wait_ge(s_small, DMAS)
            for f in range(2):
                for g in range(GROUPS):
                    if f == 0:
                        dve.wait_ge(s_x, DMAS * (g + 1))
                    route(2 * f + g, g)
                dve.wait_ge(s_w1, DMAS * 3)
                for g in range(GROUPS):
                    experts(2 * f + g, g)
                for g in range(GROUPS):
                    combine(2 * f + g, g)
                if f == 0:
                    dve.wait_ge(combined, TILES)
                    stats(0, TILES)
                    moments(0, TILES)
                    link(dve.tensor_scalar(nw[:, 0:TILES], va2[:, 0, :], -LN_EPS, None, ALU.add))
                    link(dve.scalar_tensor_tensor(va2[:, 1, :], va2[:, 0, :], RMS_EPS, nw[:, 0:TILES], ALU.mult, ALU.add))
                    root(va2[:, :, :].rearrange("p a b -> p (a b)"), rs2[:, :, :].rearrange("p a b -> p (a b)"), nw[:, :])
                    link(dve.memset(XR[0][:, :, 0:3], 0.0))
                    dve.wait_ge(s_wmam, DMAS)
                    for b in range(2):
                        w = wm("wout")[:, b * P:(b + 1) * P]
                        link(dve.tensor_scalar(w, w, sm("ssm")[:, b:b + 1], None, ALU.mult))
                        link(dve.tensor_scalar(DG[:, b, :], IDENT, sm("dcol")[:, b:b + 1], None, ALU.mult))
                    for t in range(4):
                        w = 4 * CONV_PE + t
                        link(dve.tensor_scalar(CT[:, t, :], IDENT, sm("convw")[:, w:w + 1], None, ALU.mult))
                    dve.wait_ge(m_alog, 1)
                    dve.tensor_scalar(ANEG, ANEG, -1.0, None, ALU.mult).then_inc(m_set, 1)
                    step(-1, 1, True, False, False)
                    step(0, 0, True, True, False)
                    with dve.Fori(0, QUADS // 2 - 1) as b:
                        own.enter(b, DVE_PER)
                        for u in (1, 0):
                            step(2 * b + (2 - u), u, True, True, True)
                        own.leave(QUADS // 2 - 1)
                    step(QUADS - 1, 1, False, True, True)
                    step(QUADS, 0, False, False, True)


def kernel(L0_attn_x, L0_attn_prenorm_w, L0_attn_postnorm_w, L0_attn_in_proj_w, L0_attn_conv_w, L0_attn_conv_b,
           L0_attn_dt_bias, L0_attn_A_log, L0_attn_D_param, L0_attn_ssm_norm_w, L0_attn_out_proj_w, L0_attn_gate_w,
           L0_attn_up_w, L0_attn_down_w, L0_ffn_W1, L0_ffn_b1, L0_ffn_W2, L0_ffn_b2, L0_ffn_Wg, L0_ffn_bg):
    import numpy as np
    import concourse.bacc as bacc
    from concourse.bass_utils import run_bass_kernel_spmd

    f = np.float32
    p = np.arange(P)
    cst = np.zeros((P, C_END), f)
    cst[:, C_ID:C_ID + P] = np.eye(P)
    cst[:, C_TRI:C_TRI + P] = p[:, None] <= p[None, :]
    cst[:, C_LOW:C_LOW + P] = p[:, None] > p[None, :]
    cst[:, C_UP:C_UP + P] = p[:, None] < p[None, :]
    cst[:, C_ONE:C_ONE + P] = 1.0
    cst[:, C_MIN:C_MIN + P] = np.where(p[:, None] <= p[None, :], 0.0, NEG)
    cst[:, C_E8:C_E8 + NE] = np.arange(NE) - NE
    cst[:, C_J:C_J + NT] = np.arange(NT)

    def rows(a):
        a = np.asarray(a)
        return np.broadcast_to(a.reshape(1, -1), (P, a.size))

    def cols(a, n):
        return np.asarray(a).reshape(n, P).T

    small = np.concatenate([
        np.asarray(L0_ffn_Wg), rows(L0_ffn_bg), rows(L0_attn_dt_bias), rows(L0_attn_A_log),
        np.repeat(np.asarray(L0_attn_D_param), HD).reshape(2, P).T,
        np.asarray(L0_attn_conv_w).reshape(4, P, 4).transpose(1, 0, 2).reshape(P, 16), cols(L0_attn_conv_b, 4),
        cols(L0_attn_prenorm_w, 1), cols(L0_attn_postnorm_w, 1), cols(L0_attn_ssm_norm_w, 2)], axis=1)
    win = np.asarray(L0_attn_in_proj_w).T
    wmam = np.concatenate([
        win[:, 256:768], win[:, 0:256], win[:, 768:772],
        np.asarray(L0_attn_out_proj_w).reshape(P, 2, P).transpose(2, 1, 0).reshape(P, 256),
        np.asarray(L0_attn_gate_w).T, np.asarray(L0_attn_up_w).T,
        np.asarray(L0_attn_down_w).reshape(P, 4, P).transpose(2, 1, 0).reshape(P, 512)], axis=1)
    w1p = np.concatenate([np.asarray(L0_ffn_W1).transpose(1, 0, 2),
                          np.asarray(L0_ffn_b1).reshape(NE, HB, P).transpose(2, 0, 1)], axis=2)
    w2p = np.asarray(L0_ffn_W2).reshape(NE, HB, P, P).transpose(2, 0, 1, 3)
    b2p = np.broadcast_to(np.asarray(L0_ffn_b2).reshape(1, NE, P), (P, NE, P))
    arrays = {"x": np.asarray(L0_attn_x), "cst": cst, "small": small, "wmam": wmam, "w1p": w1p, "w2p": w2p, "b2p": b2p}
    nc = bacc.Bacc("TRN2", target_bir_lowering=False, num_devices=1)
    args, given = [], {}
    for name, a in arrays.items():
        given[name] = np.ascontiguousarray(a)
        args.append(nc.dram_tensor(name, a.shape, mybir.dt.from_np(a.dtype), kind="ExternalInput").ap())
    args.append(nc.dram_tensor("out", (SEQS, SEQ, P), F32, kind="ExternalOutput").ap())
    macaron(nc, *args)
    r = run_bass_kernel_spmd(nc, [given], core_ids=[0])
    return r.results[0]["out"]
```

```python
from contextlib import ExitStack

import concourse.bass as bass
from concourse import mybir

F32 = mybir.dt.float32
I32 = mybir.dt.int32
ALU = mybir.AluOpType
EngineType = mybir.EngineType
ACT = mybir.ActivationFunctionType
AX = mybir.AxisListType.X
ds = bass.ds

P = 128
SEQS, SEQ = 8, 1024
TILES = SEQS * SEQ // P
NE, HID = 8, 512
HB = HID // P
GROUPS = 2
GT = TILES // GROUPS
SLOTS = 256
TR = 4
GTILES = 4
RING = 2
LATE = 6
ARENA = 29500
OUT = 8
NT = (2 * GT * P + NE * (SLOTS - 1)) // SLOTS
HEADS, HD = 4, 64
QT = 4
QUADS = TILES // QT
CONV_DVE, CONV_PE = (2, 0, 1), 3
NEG = -1.0e30
MAGIC = float(0x5F3759DF)
POOL_PER, DVE_PER = 84, 55
LN_EPS, RMS_EPS = 1e-5, 1e-6

C_ID, C_TRI, C_LOW, C_UP, C_ONE, C_MIN, C_E8, C_J = 0, 128, 256, 384, 512, 640, 768, 776
C_END = C_J + NT
SM = {}
_at = 0
for _n, _w in (("wg", 8), ("bg", 8), ("dtb", 4), ("alog", 4), ("dcol", 2), ("convw", 16), ("convb", 4),
               ("pre", 1), ("post", 1), ("ssm", 2)):
    SM[_n] = (_at, _at + _w)
    _at += _w
SM_END = _at
WM = {}
_at = 0
for _n, _w in (("wx", 512), ("wz", 260), ("wout", 256), ("gate", 512), ("up", 512), ("down", 512)):
    WM[_n] = (_at, _at + _w)
    _at += _w
WM_END = _at


class Steps:

    def __init__(self, eng, sem, tick=None):
        self.eng, self.sem, self.tick, self.base, self.n = eng, sem, tick, 0, 0

    def mark(self, ins):
        ins.then_inc(self.sem, 1)
        self.n += 1

    def link(self, ins):
        self.mark(ins)
        self.eng.wait_ge(self.sem, self.base + self.n)
        if self.tick is not None:
            self.eng.sem_inc(self.tick, 1)

    def enter(self, i, per):
        self.start, self.per = self.base + self.n, per
        self.base, self.n = self.start + i * per, 0

    def leave(self, turns):
        assert self.n == self.per, (self.n, self.per)
        self.base, self.n = self.start + turns * self.per, 0


def wait(eng, sem, value):
    if isinstance(value, int) and value <= 0:
        return
    eng.wait_ge(sem, value)


def bc(ap, n):
    return ap.unsqueeze(2).to_broadcast([ap.shape[0], ap.shape[1], n])


def rep(ap, n):
    return ap.unsqueeze(1).to_broadcast([ap.shape[0], n, ap.shape[1]])


def macaron(nc, x, cst, small, wmam, w1p, w2p, b2p, out):
    ctx = ExitStack()
    with ctx:
        def sb(name, shape, dt=F32):
            return ctx.enter_context(nc.sbuf_tensor(name, shape, dt))

        def ps(name):
            return ctx.enter_context(nc.psum_tensor(name, [P, 512], F32))

        def sem(name):
            return ctx.enter_context(nc.semaphore(name))

        xs = [nc.dram_tensor(f"xs{g}", (NT * SLOTS, P), F32, kind="Internal").ap() for g in range(GROUPS)]
        ys = [nc.dram_tensor(f"ys{g}", (NT * SLOTS, P), F32, kind="Internal").ap() for g in range(GROUPS)]
        x_v = x.rearrange("b (t p) c -> p (b t) c", p=P)
        out_v = out.rearrange("b (t p) c -> p (b t) c", p=P)

        X = sb("X", [P, TILES, P])
        CST = sb("CST", [P, C_END])
        SMALL = sb("SMALL", [P, SM_END])
        WMAM = sb("WMAM", [P, WM_END])
        W1 = sb("W1", [P, NE, HID + HB])
        W2 = sb("W2", [P, NE, HB, P])
        B2 = sb("B2", [P, NE, P])
        IDENT, TRI, LOW, UP, ONE, MINM = (CST[:, c:c + P] for c in (C_ID, C_TRI, C_LOW, C_UP, C_ONE, C_MIN))
        E8, JJ = CST[:, C_E8:C_E8 + NE], CST[:, C_J:C_J + NT]

        def sm(name):
            return SMALL[:, SM[name][0]:SM[name][1]]

        def wm(name):
            return WMAM[:, WM[name][0]:WM[name][1]]

        arena = sb("arena", [P, ARENA])
        used = {"f": 0, "m": 0}

        def at(which, shape):
            n = 1
            for s in shape:
                n *= s
            a = arena[:, used[which]:used[which] + n]
            used[which] += n
            assert used[which] <= ARENA
            if len(shape) == 2:
                a = a.rearrange("p (a b) -> p a b", a=shape[0])
            if len(shape) == 3:
                a = a.rearrange("p (a b c) -> p a b c", a=shape[0], b=shape[1])
            return a

        XN = at("f", [TILES, P])
        xq = [at("f", [4, P]) for _ in range(2)]
        xnT = [at("f", [4 * P]) for _ in range(2)]
        w1c = [at("f", [HID + HB]) for _ in range(TR)]
        xt = [at("f", [2, P]) for _ in range(TR)]
        xT = [at("f", [SLOTS]) for _ in range(2)]
        Hh = [at("f", [HB, SLOTS]) for _ in range(2)]
        Yb = [at("f", [2, P]) for _ in range(TR)]
        R = [at("f", [GT, NE]) for _ in range(8)]
        jb = at("f", [NT, NE])
        GB = [at("f", [GT, 2, P]), XN.rearrange("p (a b) c -> p a b c", b=2)]

        st6 = sb("st6", [P, TILES, 6])
        mean = sb("mean", [P, TILES])
        rs2 = sb("rs2", [P, 2, TILES])
        va2 = sb("va2", [P, 2, TILES])
        nw = sb("nw", [P, 2 * TILES])
        rb = sb("rb", [P, 12, GT])
        tb = sb("tb", [P, 8, NE])
        wtop = [sb(f"wtop{g}", [P, 2, GT]) for g in range(GROUPS)]
        pos = [sb(f"pos{g}", [P, 2, GT], I32) for g in range(GROUPS)]
        jf = sb("jf", [P, NT])
        eid = [sb(f"eid{g}", [P, NT], I32) for g in range(GROUPS)]
        zeros = sb("zeros", [P, P])
        DG = sb("DG", [P, 2, P])
        CT = sb("CT", [P, 4, P])
        ANEG = sb("ANEG", [P, HEADS])

        XR = [at("m", [4, 3 + QT * P]) for _ in range(2)]
        CV = at("m", [len(CONV_DVE), QT * P])
        XC = [at("m", [4, QT * P]) for _ in range(2)]
        U = at("m", [QT, P])
        UN = at("m", [QT, P])
        UT = at("m", [QT * P])
        SZ = [at("m", [QT, 256]) for _ in range(2)]
        SLH = [at("m", [HEADS, P]) for _ in range(2)]
        RM = [at("m", [HEADS, P]) for _ in range(2)]
        EX = [at("m", [HEADS, P]) for _ in range(QT)]
        MT = [at("m", [HEADS, P]) for _ in range(2)]
        XT = [at("m", [512]) for _ in range(2)]
        XD = [at("m", [256]) for _ in range(2)]
        XW = [at("m", [256]) for _ in range(2)]
        S = at("m", [256])
        YY = at("m", [256])
        GY = [at("m", [256]) for _ in range(2)]
        GTr = [at("m", [256]) for _ in range(2)]
        JK = at("m", [256])
        JH = at("m", [P])
        HH = at("m", [QT, P])
        HN = at("m", [QT, P])
        HT = at("m", [QT * P])
        SG = [at("m", [QT * P]) for _ in range(2)]
        AT = at("m", [4, QT * P])
        DTR = [at("m", [16]) for _ in range(2)]
        V = at("m", [16])
        VA = at("m", [16])
        EE = at("m", [16])
        RD = at("m", [16])
        SS_ = at("m", [16])
        S2 = at("m", [16])
        PO = at("m", [16])
        DT = [at("m", [16]) for _ in range(2)]
        DA = [at("m", [16]) for _ in range(2)]
        C3 = at("m", [48])
        E3 = [at("m", [48]) for _ in range(2)]
        DTW = [at("m", [16]) for _ in range(2)]
        SQ = [at("m", [4]) for _ in range(2)]
        NV = [at("m", [4]) for _ in range(2)]
        NY = [at("m", [4]) for _ in range(2)]
        NW = [at("m", [4]) for _ in range(2)]
        GR = at("m", [RING * GTILES, 2, P])

        BANK = [ps(f"bank{i}") for i in range(8)]
        psT, psA, psB, psX, psR, psY, psS, psO = BANK
        psTr = [BANK[0], BANK[1]]
        psL = BANK[2]
        psC = BANK[3]
        psHid = [[BANK[2], BANK[3]], [BANK[4], BANK[5]]]
        psOut = [BANK[6], BANK[7]]

        s_cst, s_small, s_wmam, s_w1, s_out = (sem(n) for n in ("s_cst", "s_small", "s_wmam", "s_w1", "s_out"))
        s_x = [sem(f"s_x{i}") for i in range(2 * GROUPS)]
        s_zero = sem("s_zero")
        zero_ready = sem("zero_ready")
        pool_tick = sem("pool_tick")
        o_dve, o_pool = sem("o_dve"), sem("o_pool")
        xn_ready, xn_transposed, xnt_ready, xn_kept, logits_done = (
            sem(n) for n in ("xn_ready", "xn_transposed", "xnt_ready", "xn_kept", "logits_done"))
        shifted, exped, chosen, counted, placed, gap_ready, gap_exped, tiles_known = (
            sem(n) for n in ("shifted", "exped", "chosen", "counted", "placed", "gap_ready", "gap_exped", "tiles_known"))
        scattered = [sem(f"scattered{c}") for c in range(2 * GROUPS)]
        slots_in = [sem(f"slots_in{i}") for i in range(TR)]
        slots_out = [sem(f"slots_out{i}") for i in range(TR)]
        slots_turned, slots_ready, w1_ready, hidden_done, relu_act, relu_dve, rows_done, rows_ready = (
            sem(n) for n in ("slots_turned", "slots_ready", "w1_ready", "hidden_done", "relu_act", "relu_dve",
                             "rows_done", "rows_ready"))
        gathered = [sem("gathered_a")]
        gathered_last = [sem(f"gathered_b{i}") for i in range(GT // GTILES)]
        combined = sem("combined")
        (m_un, m_unT, m_ut, m_ip, m_xr, m_z, m_sz, m_cvd, m_cvp, m_xc, m_va, m_ee, m_rd, m_da, m_col, m_c3, m_e3,
         m_sl, m_tx, m_r, m_xt, m_rm, m_ex, m_xd, m_mt, m_y, m_st, m_s, m_u, m_gy, m_gt, m_gc, m_o, m_sq, m_seed,
         m_nw, m_h, m_hn, m_hT, m_ht, m_ga, m_up, m_sg, m_at, m_dn, m_xh, m_fx, m_set, m_sqh, m_alog) = (
            sem("m_" + n) for n in
            ("un unT ut ip xr z sz cvd cvp xc va ee rd da col c3 e3 sl tx r xt rm ex xd mt y st s u gy gt gc o sq seed"
             " nw h hn hT ht ga up sg at dn xh fx set sqh alog").split())

        block = ctx.enter_context(nc.Block())

        def last_rows(c, t):
            return GR[:, t % (RING * GTILES)] if c < GROUPS else GB[1][:, t]

        GATHERED_IN = {-2: (0,), -1: (1, 2), 0: (3,), 1: (4,), 2: (5,), 3: (6,), 4: (7,)}
        ADDED_IN = {-1: (0,), 0: (1, 2), 1: (3,), 2: (4,), 3: (5,), 4: (6,), 5: (7,)}

        def load_ids(engine, g, j, n):
            return nc.values_load_multi_w_load_instructions(eid[g][0:1, ds(j, n)], engines=[engine],
                                                            min_val=0, max_val=NE - 1)[1]

        CALLS = [(f, g) for f in range(2) for g in range(GROUPS)]
        DMAS = 16
        TURNS = (NT - 3) // TR
        PLAIN = TURNS - 4
        of_ring = [(NT - i + TR - 1) // TR for i in range(TR)]

        @block.sync
        def _(sp):
            for i in range(2 * GROUPS):
                h = slice(i * GT // 2, (i + 1) * GT // 2)
                sp.dma_start(X[:, h, :], x_v[:, h, :]).then_inc(s_x[i], DMAS)
                if i == 1:
                    sp.dma_start(CST[:, :], cst).then_inc(s_cst, DMAS)
                    sp.dma_start(SMALL[:, :], small).then_inc(s_small, DMAS)
            sp.dma_start(W1[:, :, :], w1p).then_inc(s_w1, DMAS)
            sp.dma_start(W2[:, :, :, :], w2p).then_inc(s_w1, DMAS)
            sp.dma_start(B2[:, :, :], b2p).then_inc(s_w1, DMAS)
            sp.wait_ge(zero_ready, 1)
            for g in range(GROUPS):
                sp.dma_start(xs[g].rearrange("(p a) c -> p a c", p=P), rep(zeros[:, :], NT * SLOTS // P)
                             ).then_inc(s_zero, DMAS)
            sp.dma_start(WMAM[:, :], wmam).then_inc(s_wmam, DMAS)

            def slots_load(c, g, j, par):
                wait(sp, slots_turned, c * NT + j - TR + 1)
                sp.dma_start(xt[par], xs[g][ds(j * SLOTS, SLOTS), :].rearrange("(a p) c -> p a c", p=P)
                             ).then_inc(slots_in[par], DMAS)

            def slots_store(c, g, j, par):
                sp.wait_ge(rows_ready, c * NT + j + 1)
                sp.dma_start(ys[g][ds(j * SLOTS, SLOTS), :].rearrange("(a p) c -> p a c", p=P), Yb[par]
                             ).then_inc(slots_out[par], DMAS)

            for c, (f, g) in enumerate(CALLS):
                sp.wait_ge(scattered[c], DMAS * 2 * GT)
                if f == 1 and g == 0:
                    sp.wait_ge(m_fx, QUADS)
                for u in range(TR):
                    slots_load(c, g, u, u)
                with sp.Fori(0, TURNS - 1) as jj:
                    for u in range(TR):
                        slots_load(c, g, TR * jj + u + TR, u)
                        slots_store(c, g, TR * jj + u, u)
                for j in range(TR * (TURNS - 1), NT):
                    if j + TR < NT:
                        slots_load(c, g, j + TR, j % TR)
                    slots_store(c, g, j, j % TR)
                if g == GROUPS - 1 and f == 1:
                    for t in range(0, TILES, OUT):
                        sp.wait_ge(combined, TILES + t + OUT)
                        sp.dma_start(out_v[:, t:t + OUT, :], X[:, t:t + OUT, :]).then_inc(s_out, DMAS)
            sp.wait_ge(s_out, DMAS * TILES // OUT)

        @block.gpsimd
        def _(pool):
            own = Steps(pool, o_pool, pool_tick)
            pool.memset(zeros[:, :], 0.0).then_inc(zero_ready, 1)

            def scatter(c, g):
                pool.wait_ge(placed, c + 1)
                pool.wait_ge(xn_kept, (c + 1) * GT // 4)
                pool.wait_ge(s_zero, DMAS * GROUPS)
                for t in range(GT):
                    for w in range(2):
                        pool.indirect_dma_start(
                            out=xs[g], out_offset=bass.IndirectOffsetOnAxis(ap=pos[g][:, w, t:t + 1], axis=0),
                            in_=XN[:, g * GT + t, :], in_offset=None).then_inc(scattered[c], DMAS)

            def gather(c, g):
                for u in range(TR):
                    pool.wait_ge(slots_out[u], DMAS * of_ring[u] * (c + 1))
                for t in range(GT):
                    for w in range(2):
                        pool.indirect_dma_start(
                            out=GB[g][:, t, w, :], out_offset=None, in_=ys[g],
                            in_offset=bass.IndirectOffsetOnAxis(ap=pos[g][:, w, t:t + 1], axis=0)
                        ).then_inc(gathered[g], DMAS)

            def gather_last(c, q):
                g = GROUPS - 1
                if q == 0:
                    for u in range(TR):
                        pool.wait_ge(slots_out[u], DMAS * of_ring[u] * (c + 1))
                    if c == 2 * GROUPS - 1:
                        for d in range(GROUPS, 2 * GROUPS):
                            pool.wait_ge(scattered[d], DMAS * 2 * GT)
                if c < GROUPS and q >= RING:
                    pool.wait_ge(combined, c * GT + GTILES * (q - RING + 1))
                for t in range(GTILES * q, GTILES * (q + 1)):
                    for w in range(2):
                        pool.indirect_dma_start(
                            out=last_rows(c, t)[:, w, :], out_offset=None, in_=ys[g],
                            in_offset=bass.IndirectOffsetOnAxis(ap=pos[g][:, w, t:t + 1], axis=0)
                        ).then_inc(gathered_last[q], DMAS)

            def hold(sem, value):
                if isinstance(value, int) and value <= 0:
                    return
                pool.wait_ge(sem, value)
                pool.sem_inc(pool_tick, 1)

            def softplus_a(k, u):
                hold(m_sz, QT * k + QT)
                hold(m_da, k)
                own.link(pool.tensor_tensor(V.rearrange("p (a b) -> p a b", a=QT),
                                            DTR[u].rearrange("p (a b) -> p a b", a=QT), rep(sm("dtb"), QT), ALU.add))
                own.link(pool.tensor_scalar(VA, V, 0.0, None, ALU.min))
                own.link(pool.tensor_scalar(V, V, 0.0, None, ALU.max))
                pool.tensor_tensor(VA, VA, V, ALU.subtract).then_inc(m_va, 1)

            def softplus_b(k, u):
                hold(m_rd, k + 1)
                own.link(pool.tensor_tensor(SS_, EE, RD, ALU.mult))
                own.link(pool.tensor_tensor(S2, SS_, SS_, ALU.mult))
                own.link(pool.tensor_scalar(PO, S2, 2.0 / 15, 2.0 / 13, ALU.mult, ALU.add))
                for d in (11, 9, 7, 5, 3, 1):
                    own.link(pool.tensor_tensor(PO, PO, S2, ALU.mult))
                    own.link(pool.tensor_scalar(PO, PO, 1.0, 2.0 / d, ALU.mult, ALU.add))
                own.link(pool.tensor_tensor(PO, PO, SS_, ALU.mult))
                own.link(pool.tensor_tensor(DT[u], PO, V, ALU.add))
                pool.tensor_tensor(DA[u].rearrange("p (a b) -> p a b", a=QT),
                                   DT[u].rearrange("p (a b) -> p a b", a=QT), rep(ANEG[:, :], QT), ALU.mult
                                   ).then_inc(m_da, 1)

            def newton(n, u):
                hold(m_seed, n)
                for it in range(3):
                    own.link(pool.tensor_tensor(NW[u], NY[u], NY[u], ALU.mult))
                    own.link(pool.tensor_tensor(NW[u], NW[u], NV[u], ALU.mult))
                    own.link(pool.tensor_scalar(NW[u], NW[u], -0.5, 1.5, ALU.mult, ALU.add))
                    last = pool.tensor_tensor(NY[u], NY[u], NW[u], ALU.mult)
                    if it < 2:
                        own.link(last)
                last.then_inc(m_nw, 1)

            def decay(k, u, i):
                hold(m_da, k + 1)
                hold(m_r, QT * k + i - 1)
                pool.tensor_tensor(SLH[i % 2], rep(LOW, HEADS), bc(DA[u][:, 4 * i:4 * i + 4], P), ALU.mult
                                   ).then_inc(m_sl, 1)

            def residual(k):
                hold(m_h, k + 1)
                hold(m_hn, k + 1)
                hold(m_sqh, QT * k + QT)
                pool.tensor_tensor(HH, X[:, ds(QT * k, QT), :], HH, ALU.add).then_inc(m_xh, 1)

            def norm_h(k):
                hold(m_nw, 2 * k + 2)
                hold(m_hT, k)
                pool.tensor_tensor(HN, HH, bc(NY[1], P), ALU.mult).then_inc(m_hn, 1)

            def step(k, u, ahead, now, back):
                if back:
                    newton(2 * k - 1, 0)
                    newton(2 * k, 1)
                if ahead:
                    softplus_a(k + 1, 1 - u)
                if back:
                    norm_h(k - 1)
                if ahead:
                    softplus_b(k + 1, 1 - u)
                    decay(k + 1, 1 - u, 0)
                    decay(k + 1, 1 - u, 1)
                if back:
                    residual(k - 1)
                if ahead:
                    decay(k + 1, 1 - u, 2)
                    decay(k + 1, 1 - u, 3)

            for f in range(2):
                for g in range(GROUPS):
                    scatter(2 * f + g, g)
                gather(2 * f, 0)
                if f == 1:
                    for q in range(GT // GTILES):
                        gather_last(2 * f + 1, q)
                if f == 0:
                    for k in range(-2, LATE + 1):
                        if k == -1:
                            pool.wait_ge(m_set, 1)
                        if k >= -1:
                            step(k, k % 2, True, k >= 0, k >= 1)
                        for q in GATHERED_IN.get(k, ()):
                            gather_last(1, q)
                    with pool.Fori(0, (QUADS - 2 - LATE) // 2) as b:
                        own.enter(b, POOL_PER)
                        for u in (1, 0):
                            step(2 * b + LATE + (2 - u), u, True, True, True)
                        own.leave((QUADS - 2 - LATE) // 2)
                    step(QUADS - 1, 1, False, True, True)
                    step(QUADS, 0, False, False, True)

        @block.scalar
        def _(act):
            def keep(c, g, m, u):
                q0 = c * GT // 4
                act.wait_ge(xn_transposed, q0 + m + 1)
                wait(act, logits_done, q0 + m - 1)
                act.activation(xnT[u], psTr[u][:, :], ACT.Copy).then_inc(xnt_ready, 1)
                act.activation(XN[:, ds(g * GT + 4 * m, 4), :], xq[u], ACT.Copy).then_inc(xn_kept, 1)

            def route(c, g):
                keep(c, g, 0, 0)
                keep(c, g, 1, 1)
                with act.Fori(0, GT // 8 - 1) as mm:
                    for u in range(2):
                        keep(c, g, 2 * mm + u + 2, u)
                act.wait_ge(shifted, c + 1)
                act.activation(R[1], R[0], ACT.Exp).then_inc(exped, 1)
                act.wait_ge(gap_ready, c + 1)
                act.activation(rb[:, 6, :], rb[:, 5, :], ACT.Exp).then_inc(gap_exped, 1)

            def slots_T(c, j, par):
                act.wait_ge(slots_turned, c * NT + j + 1)
                wait(act, hidden_done, c * NT + j - 1)
                act.activation(xT[par], psTr[par][:, 0:256], ACT.Copy).then_inc(slots_ready, 1)

            def weights(c, e, j, r):
                free = c * NT + j - TR + 1 if not isinstance(j, int) else c * NT
                wait(act, hidden_done, free)
                wait(act, relu_act, free)
                wait(act, relu_dve, free)
                act.activation(w1c[r], W1[:, ds(e, 1), :], ACT.Copy).then_inc(w1_ready, 1)

            def relu(c, j, r):
                par = r % 2
                act.wait_ge(w1_ready, c * NT + j + 1)
                act.wait_ge(hidden_done, c * NT + j + 1)
                for h in range(2):
                    last = act.activation(Hh[par][:, h, :], psHid[par][h // 2][:, (h % 2) * 256:(h % 2) * 256 + 256],
                                          ACT.Relu, bias=w1c[r][:, HID + h:HID + h + 1])
                last.then_inc(relu_act, 1)

            def experts(c, g):
                act.wait_ge(tiles_known, c + 1)
                act.wait_ge(s_w1, DMAS * 3)
                e = load_ids(EngineType.Activation, g, 0, 3)
                for j in range(3):
                    weights(c, e[j], j, j)
                slots_T(c, 0, 0)
                with act.Fori(0, TURNS) as jj:
                    for u in range(TR):
                        j = TR * jj + u
                        slots_T(c, j + 1, (u + 1) % 2)
                        relu(c, j, u)
                        if u == 0:
                            e = load_ids(EngineType.Activation, g, TR * jj + 3, TR)
                        weights(c, e[u], j + 3, (u + 3) % TR)
                for j in range(NT - 3, NT):
                    if j < NT - 1:
                        slots_T(c, j + 1, (j + 1) % 2)
                    relu(c, j, j % TR)

            def un_T(k):
                act.wait_ge(m_unT, k + 1)
                wait(act, m_z, QT * k)
                act.activation(UT, psA[:, :], ACT.Copy, scale=sm("pre")).then_inc(m_ut, 1)

            def xr(k, u, b):
                act.wait_ge(m_ip, QT * k + b + 1)
                wait(act, m_cvd, len(CONV_DVE) * (k if u == 0 else k - 1))
                wait(act, m_cvp, k if u == 0 else k - 1)
                if u == 1 and b == 0:
                    act.activation(XR[1][:, :, 0:3], XR[0][:, :, QT * P:QT * P + 3], ACT.Copy)
                act.activation(XR[u][:, b, 3:515], (psB, psA)[b % 2][:, :], ACT.Copy).then_inc(m_xr, 1)

            def sz(k, u, i):
                act.wait_ge(m_z, QT * k + i + 1)
                wait(act, m_gy, QT * (k - 1))
                act.activation(DTR[u][:, 4 * i:4 * i + 4], (psB, psA)[i % 2][:, 256:260], ACT.Copy)
                act.activation(SZ[u][:, i, :], (psB, psA)[i % 2][:, 0:256], ACT.Silu).then_inc(m_sz, 1)

            def xt_(k, i):
                I = QT * k + i
                act.wait_ge(m_tx, I + 1)
                wait(act, m_st, I - 1)
                wait(act, m_xd, I - 1)
                wait(act, m_mt, I - 1)
                act.activation(XT[i % 2], psX[:, :], ACT.Copy).then_inc(m_xt, 1)

            def exp_r(k, i):
                act.wait_ge(m_rm, QT * k + i + 1)
                wait(act, m_mt, QT * (k - 1) + i + 1)
                act.activation(EX[i], RM[i % 2], ACT.Exp).then_inc(m_ex, 1)

            def square(k, i):
                I = QT * k + i
                act.wait_ge(m_gy, I + 1)
                wait(act, m_sq, I)
                if i == 0:
                    wait(act, m_seed, 2 * k - 1)
                act.activation(JK, GY[i % 2], ACT.Square, accum_out=SQ[0][:, i:i + 1]).then_inc(m_sq, 1)
                act.wait_ge(m_gt, I + 1)
                wait(act, m_o, I - 1)
                act.activation(GTr[i % 2], psT[:, (i % 2) * 256:(i % 2) * 256 + 256], ACT.Copy).then_inc(m_gc, 1)

            def exp_a(k):
                act.wait_ge(m_va, k + 1)
                act.activation(EE, VA, ACT.Exp).then_inc(m_ee, 1)

            def exp_b(k, u):
                act.wait_ge(m_c3, k + 1)
                act.activation(E3[u], C3, ACT.Exp).then_inc(m_e3, 1)

            def h_T(k):
                act.wait_ge(m_hT, k + 1)
                wait(act, m_up, QT * k)
                act.activation(HT, psB[:, :], ACT.Copy, scale=sm("post")).then_inc(m_ht, 1)

            def gate(k, b):
                act.wait_ge(m_ga, QT * k + b + 1)
                if b >= 2:
                    act.wait_ge(m_at, QT * k + b - 1)
                act.activation(SG[b % 2], psA[:, :], ACT.Silu).then_inc(m_sg, 1)

            def square_h(k):
                act.wait_ge(m_h, k + 1)
                wait(act, m_seed, 2 * k)
                for i in range(QT):
                    wait(act, m_sqh, QT * k + i)
                    act.activation(JH, HH[:, i, :], ACT.Square, accum_out=SQ[1][:, i:i + 1]).then_inc(m_sqh, 1)

            def conv_silu(k, u, b):
                if b in CONV_DVE:
                    act.wait_ge(m_cvd, len(CONV_DVE) * k + CONV_DVE.index(b) + 1)
                    taps = CV[:, CONV_DVE.index(b), :]
                else:
                    act.wait_ge(m_cvp, k + 1)
                    taps = psR[:, :]
                wait(act, m_y, QT * (k - 1))
                act.activation(XC[u][:, b, :], taps, ACT.Silu, bias=sm("convb")[:, b:b + 1]).then_inc(m_xc, 1)

            def step(k, u, ahead, now, back):
                n, v = k + 1, 1 - u
                if now:
                    xt_(k, 0)
                if ahead:
                    un_T(n)
                if back:
                    square(k - 1, QT - 1)
                if now:
                    xt_(k, 1)
                if ahead:
                    for b in range(4):
                        xr(n, v, b)
                if now:
                    square(k, 0)
                if back:
                    square_h(k - 1)
                if now:
                    xt_(k, 2)
                if ahead:
                    sz(n, v, 0)
                    sz(n, v, 1)
                    sz(n, v, 2)
                    sz(n, v, 3)
                if now:
                    square(k, 1)
                if ahead:
                    exp_a(n)
                if now:
                    xt_(k, 3)
                if back:
                    h_T(k - 1)
                if ahead:
                    conv_silu(n, v, CONV_PE)
                    conv_silu(n, v, CONV_DVE[0])
                if back:
                    gate(k - 1, 0)
                if ahead:
                    conv_silu(n, v, CONV_DVE[1])
                if now:
                    square(k, 2)
                if back:
                    gate(k - 1, 1)
                    gate(k - 1, 2)
                if ahead:
                    conv_silu(n, v, CONV_DVE[2])
                if back:
                    gate(k - 1, 3)
                if ahead:
                    exp_b(n, v)
                    for i in range(QT):
                        exp_r(n, i)

            act.wait_ge(s_small, DMAS)
            act.activation(ANEG[:, :], sm("alog"), ACT.Exp).then_inc(m_alog, 1)
            for f in range(2):
                for g in range(GROUPS):
                    route(2 * f + g, g)
                for g in range(GROUPS):
                    experts(2 * f + g, g)
                if f == 0:
                    for k in range(-1, LATE + 1):
                        step(k, k % 2, True, k >= 0, k >= 1)
                    with act.Fori(0, (QUADS - 2 - LATE) // 2) as b:
                        for u in (1, 0):
                            step(2 * b + LATE + (2 - u), u, True, True, True)
                    step(QUADS - 1, 1, False, True, True)
                    step(QUADS, 0, False, False, True)

        @block.tensor
        def _(pe):
            pe.wait_ge(s_cst, DMAS)
            pe.wait_ge(s_small, DMAS)

            def turn_xn(c, m, u):
                pe.wait_ge(xn_ready, c * GT // 4 + m + 1)
                for i in range(4):
                    last = pe.transpose(psTr[u][:, i * P:(i + 1) * P], xq[u][:, i, :], IDENT)
                last.then_inc(xn_transposed, 1)

            def logits(c, m, u):
                pe.wait_ge(xnt_ready, c * GT // 4 + m + 1)
                for i in range(4):
                    last = pe.matmul(psL[:, ds((4 * m + i) * NE, NE)], xnT[u][:, i * P:(i + 1) * P], sm("wg"),
                                     start=True, stop=True)
                last.then_inc(logits_done, 1)

            def route(c):
                turn_xn(c, 0, 0)
                with pe.Fori(0, GT // 8 - 1) as mm:
                    for u in range(2):
                        m = 2 * mm + u
                        turn_xn(c, m + 1, 1 - u)
                        logits(c, m, u)
                turn_xn(c, GT // 4 - 1, 1)
                logits(c, GT // 4 - 2, 0)
                logits(c, GT // 4 - 1, 1)
                pe.wait_ge(chosen, c + 1)
                oh = R[4].rearrange("p a b -> p (a b)")
                pe.matmul(psC[:, 0:256], UP, oh, start=True, stop=True)
                pe.matmul(psC[:, 256:512], ONE, oh, start=True, stop=True).then_inc(counted, 1)

            def turn(c, j, jj, r):
                par = r % 2
                pe.wait_ge(slots_in[r], DMAS * (of_ring[r] * c + jj + 1))
                for a in range(2):
                    last = pe.transpose(psTr[par][:, a * P:(a + 1) * P], xt[r][:, a, :], IDENT)
                last.then_inc(slots_turned, 1)

            def up_proj(c, j, r):
                par = r % 2
                pe.wait_ge(slots_ready, c * NT + j + 1)
                pe.wait_ge(w1_ready, c * NT + j + 1)
                for h in range(HB):
                    last = pe.matmul(psHid[par][h // 2][:, (h % 2) * 256:(h % 2) * 256 + 256],
                                     w1c[r][:, h * P:(h + 1) * P], xT[par], start=True, stop=True)
                last.then_inc(hidden_done, 1)

            def down_proj(c, e, j, par):
                pe.wait_ge(relu_act, c * NT + j + 1)
                pe.wait_ge(relu_dve, c * NT + j + 1)
                for a in range(2):
                    for h in range(HB):
                        last = pe.matmul(psOut[par][:, a * P:(a + 1) * P],
                                         Hh[par][:, h, a * P:(a + 1) * P], W2[:, ds(e, 1), h, :],
                                         start=(h == 0), stop=(h == HB - 1))
                last.then_inc(rows_done, 1)
                wait(pe, rows_ready, c * NT + j)

            def experts(c, g):
                pe.wait_ge(tiles_known, (c // GROUPS + 1) * GROUPS)
                turn(c, 0, 0, 0)
                up_proj(c, 0, 0)
                turn(c, 1, 0, 1)
                with pe.Fori(0, TURNS) as jj:
                    for u in range(TR):
                        j = TR * jj + u
                        up_proj(c, j + 1, (u + 1) % TR)
                        if u == 0:
                            e = load_ids(EngineType.PE, g, TR * jj, TR)
                        turn(c, j + 2, jj + (u + 2) // TR, (u + 2) % TR)
                        down_proj(c, e[u], j, u % 2)
                e = load_ids(EngineType.PE, g, NT - 3, 3)
                up_proj(c, NT - 2, (NT - 2) % TR)
                turn(c, NT - 1, (NT - 1) // TR, (NT - 1) % TR)
                down_proj(c, e[0], NT - 3, (NT - 3) % 2)
                up_proj(c, NT - 1, (NT - 1) % TR)
                down_proj(c, e[1], NT - 2, (NT - 2) % 2)
                down_proj(c, e[2], NT - 1, (NT - 1) % 2)

            def turn_un(k):
                pe.wait_ge(m_un, k + 1)
                wait(pe, m_sz, QT * k)
                wait(pe, m_sg, QT * (k - 2))
                for i in range(QT):
                    last = pe.transpose(psA[:, i * P:(i + 1) * P], UN[:, i, :], IDENT)
                last.then_inc(m_unT, 1)

            def in_proj(k, b):
                if b == 0:
                    pe.wait_ge(m_ut, k + 1)
                    wait(pe, m_fx, k - 2)
                if b >= 2:
                    pe.wait_ge(m_xr, QT * k + b - 1)
                pe.matmul((psB, psA)[b % 2][:, :], wm("wx")[:, b * P:(b + 1) * P], UT, start=True, stop=True
                          ).then_inc(m_ip, 1)

            def z_proj(k, i):
                if i < 2:
                    pe.wait_ge(m_xr, QT * k + 3 + i)
                else:
                    pe.wait_ge(m_sz, QT * k + i - 1)
                pe.matmul((psB, psA)[i % 2][:, 0:260], UT[:, i * P:(i + 1) * P], wm("wz"), start=True, stop=True
                          ).then_inc(m_z, 1)

            def sums(k, u):
                pe.wait_ge(m_da, k + 1)
                wait(pe, m_s, QT * k)
                pe.matmul(psS[:, 256:272], TRI, DA[u], start=True, stop=True)
                pe.matmul(psS[:, 272:288], ONE, DA[u], start=True, stop=True).then_inc(m_col, 1)

            def conv(k, u, taps):
                pe.wait_ge(m_xr, QT * k + QT)
                wait(pe, m_rm, QT * k)
                for t in taps:
                    last = pe.matmul(psR[:, :], CT[:, t, :], XR[u][:, CONV_PE, t:t + 512], start=(t == 0), stop=(t == 3))
                if t == 3:
                    last.then_inc(m_cvp, 1)

            def decay(k, i):
                pe.wait_ge(m_sl, QT * k + i + 1)
                if i == 0:
                    pe.wait_ge(m_xc, QT * k + 1)
                elif i == 1:
                    wait(pe, m_xt, QT * k)
                else:
                    pe.wait_ge(m_rm, QT * k + i - 1)
                R = (psR, psX)[i % 2]
                for h in range(HEADS):
                    last = pe.matmul(R[:, h * P:(h + 1) * P], SLH[i % 2][:, h, :], TRI, start=True, stop=True)
                last.then_inc(m_r, 1)

            def chunk_a(k, u, i):
                I = QT * k + i
                if i == 0:
                    pe.wait_ge(m_xc, QT * k + QT)
                    pe.wait_ge(m_rm, QT * k + QT)
                wait(pe, m_xt, I)
                for b in range(3):
                    last = pe.transpose(psX[:, b * P:(b + 1) * P], XC[u][:, b, i * P:(i + 1) * P], IDENT)
                pe.matmul(psX[:, 384:512], XC[u][:, 2, i * P:(i + 1) * P],
                          XC[u][:, 3, i * P:(i + 1) * P], start=True, stop=True).then_inc(m_tx, 1)

            def chunk_b(k, u, i):
                I = QT * k + i
                first = u == 0 and i == 0
                wait(pe, m_gy, I)
                for b in range(2):
                    pe.matmul(psY[:, b * P:(b + 1) * P], XC[u][:, b, i * P:(i + 1) * P], DG[:, b, :],
                              start=(b == 0), stop=False)
                pe.wait_ge(m_xd, I + 1)
                pe.wait_ge(m_mt, I + 1)
                for h in range(HEADS):
                    last = pe.matmul(psY[:, h * HD:(h + 1) * HD], MT[i % 2][:, h, :], XD[i % 2][:, h * HD:(h + 1) * HD],
                                     start=False, stop=(h == HEADS - 1))
                wait(pe, m_s, I)
                if not first:
                    last = pe.matmul(psY[:, 256:512], XC[u][:, 3, i * P:(i + 1) * P], S, start=True, stop=True)
                last.then_inc(m_y, 1)
                pe.wait_ge(m_c3, k + 1)
                pe.matmul(psS[:, 0:256], XT[i % 2][:, 256:384], XW[i % 2], start=True, stop=True).then_inc(m_st, 1)

            def turn_g(k, i):
                I = QT * k + i
                pe.wait_ge(m_gy, I + 1)
                wait(pe, m_gc, I)
                for b in range(2):
                    last = pe.transpose(psT[:, (i % 2) * 256 + b * P:(i % 2) * 256 + (b + 1) * P],
                                        GY[i % 2][:, b * P:(b + 1) * P], IDENT)
                last.then_inc(m_gt, 1)

            def out_proj(k, i):
                I = QT * k + i
                if i == 0:
                    wait(pe, m_h, k)
                pe.wait_ge(m_gc, I + 1)
                for b in range(2):
                    last = pe.matmul(psO[:, i * P:(i + 1) * P], GTr[i % 2][:, b * P:(b + 1) * P],
                                     wm("wout")[:, b * P:(b + 1) * P], start=(b == 0), stop=(b == 1))
                last.then_inc(m_o, 1)

            def turn_h(k):
                pe.wait_ge(m_hn, k + 1)
                pe.wait_ge(m_sz, QT * min(k + 3, QUADS) if isinstance(k, int) else QT * (k + 3))
                wait(pe, m_fx, k)
                for i in range(QT):
                    last = pe.transpose(psB[:, i * P:(i + 1) * P], HN[:, i, :], IDENT)
                last.then_inc(m_hT, 1)

            def gate_up(k, b):
                if b == 0:
                    pe.wait_ge(m_ht, k + 1)
                wait(pe, m_sg, QT * k + b)
                pe.matmul(psA[:, :], wm("gate")[:, b * P:(b + 1) * P], HT, start=True, stop=True).then_inc(m_ga, 1)
                wait(pe, m_at, QT * k + b)
                pe.matmul(psB[:, :], wm("up")[:, b * P:(b + 1) * P], HT, start=True, stop=True).then_inc(m_up, 1)

            def down(k):
                pe.wait_ge(m_at, QT * k + QT)
                for i in range(QT):
                    for b in range(4):
                        last = pe.matmul(psB[:, i * P:(i + 1) * P], AT[:, b, i * P:(i + 1) * P],
                                         wm("down")[:, b * P:(b + 1) * P], start=(b == 0), stop=(b == 3))
                last.then_inc(m_dn, 1)

            def step(k, u, ahead, now, back):
                n, v = k + 1, 1 - u
                if back:
                    turn_g(k - 1, QT - 1)
                if now:
                    chunk_a(k, u, 0)
                if ahead:
                    turn_un(n)
                if now:
                    chunk_a(k, u, 1)
                    chunk_b(k, u, 0)
                if ahead:
                    in_proj(n, 0)
                if back:
                    out_proj(k - 1, QT - 1)
                if ahead:
                    in_proj(n, 1)
                    in_proj(n, 2)
                if now:
                    turn_g(k, 0)
                if ahead:
                    in_proj(n, 3)
                if now:
                    chunk_b(k, u, 1)
                    chunk_a(k, u, 2)
                if ahead:
                    z_proj(n, 0)
                    z_proj(n, 1)
                if now:
                    out_proj(k, 0)
                if ahead:
                    conv(n, v, (0, 1))
                    z_proj(n, 2)
                    z_proj(n, 3)
                if now:
                    turn_g(k, 1)
                    chunk_b(k, u, 2)
                    chunk_a(k, u, 3)
                    out_proj(k, 1)
                if back:
                    turn_h(k - 1)
                if ahead:
                    conv(n, v, (2, 3))
                if back:
                    gate_up(k - 1, 0)
                if now:
                    turn_g(k, 2)
                    chunk_b(k, u, 3)
                if back:
                    gate_up(k - 1, 1)
                if now:
                    out_proj(k, 2)
                if back:
                    gate_up(k - 1, 2)
                if ahead:
                    sums(n, v)
                    decay(n, 0)
                    decay(n, 1)
                if back:
                    gate_up(k - 1, 3)
                if ahead:
                    decay(n, 2)
                    decay(n, 3)
                if back:
                    down(k - 1)

            for f in range(2):
                for g in range(GROUPS):
                    route(2 * f + g)
                if f == 0:
                    pe.wait_ge(s_w1, DMAS * 3)
                for g in range(GROUPS):
                    experts(2 * f + g, g)
                if f == 0:
                    pe.wait_ge(s_wmam, DMAS)
                    pe.wait_ge(m_set, 1)
                    for k in range(-1, LATE + 1):
                        step(k, k % 2, True, k >= 0, k >= 1)
                    with pe.Fori(0, (QUADS - 2 - LATE) // 2) as b:
                        for u in (1, 0):
                            step(2 * b + LATE + (2 - u), u, True, True, True)
                    step(QUADS - 1, 1, False, True, True)
                    step(QUADS, 0, False, False, True)

        @block.vector
        def _(dve):
            own = Steps(dve, o_dve)
            link = own.link

            def stats(t0, n):
                for i in range(n):
                    last = dve.bn_stats(st6[:, ds(t0 + i, 1), :], X[:, ds(t0 + i, 1), :])
                link(last)

            def root(v, y, w):
                link(dve.tensor_single_scalar(y.bitcast(I32), v.bitcast(I32), 1, ALU.arith_shift_right))
                link(dve.tensor_scalar(y.bitcast(I32), y.bitcast(I32), -1.0, MAGIC, ALU.mult, ALU.add))
                for _ in range(3):
                    link(dve.tensor_tensor(w, y, y, ALU.mult))
                    link(dve.scalar_tensor_tensor(w, w, -0.5, v, ALU.mult, ALU.mult))
                    link(dve.scalar_tensor_tensor(y, w, 1.5, y, ALU.add, ALU.mult))

            def moments(t0, n):
                m, v, w = mean[:, t0:t0 + n], va2[:, 0, t0:t0 + n], nw[:, 0:n]
                m0, m1, q0, q1 = (st6[:, t0:t0 + n, c] for c in (1, 4, 2, 5))
                link(dve.tensor_tensor(m, m0, m1, ALU.add))
                link(dve.tensor_scalar(m, m, 0.5, None, ALU.mult))
                link(dve.tensor_tensor(w, m0, m1, ALU.subtract))
                link(dve.tensor_tensor(w, w, w, ALU.mult))
                link(dve.tensor_tensor(v, q0, q1, ALU.add))
                link(dve.tensor_scalar(v, v, 1.0 / P, LN_EPS, ALU.mult, ALU.add))
                link(dve.scalar_tensor_tensor(v, w, 0.25, v, ALU.mult, ALU.add))

            def normalise(c, t0, m, u):
                q0, t = c * GT // 4, t0 + 4 * m
                wait(dve, xn_kept, q0 + m - 1)
                wait(dve, xn_transposed, q0 + m - 1)
                link(dve.tensor_tensor(xq[u], X[:, ds(t, 4), :], bc(mean[:, ds(t, 4)], P), ALU.subtract))
                dve.tensor_tensor(xq[u], xq[u], bc(rs2[:, 0, ds(t, 4)], P), ALU.mult).then_inc(xn_ready, 1)

            def layer_norm(c, g):
                t0 = g * GT
                if c < GROUPS:
                    for h in range(2):
                        dve.wait_ge(s_x[2 * g + h], DMAS)
                        stats(t0 + h * GT // 2, GT // 2)
                moments(t0, GT)
                root(va2[:, 0, t0:t0 + GT], rs2[:, 0, t0:t0 + GT], nw[:, 0:GT])

            def route(c, g):
                t0, q0 = g * GT, c * GT // 4
                if c != GROUPS:
                    layer_norm(c, g)
                normalise(c, t0, 0, 0)
                normalise(c, t0, 1, 1)
                with dve.Fori(0, GT // 8 - 1) as mm:
                    own.enter(mm, 2)
                    for u in range(2):
                        normalise(c, t0, 2 * mm + u + 2, u)
                    own.leave(GT // 8 - 1)
                L, Pr, T, O1, A, O2, C0, C1 = R
                row = lambda i: rb[:, i, :]
                dve.wait_ge(s_cst, DMAS)
                dve.wait_ge(s_small, DMAS)
                dve.wait_ge(logits_done, q0 + GT // 4)
                link(dve.tensor_tensor(L, psL[:, 0:GT * NE].rearrange("p (a b) -> p a b", b=NE), rep(sm("bg"), GT), ALU.add))
                link(dve.tensor_reduce(row(0), L, AX, ALU.max))
                dve.tensor_tensor(L, L, bc(row(0), NE), ALU.subtract).then_inc(shifted, 1)
                dve.wait_ge(exped, c + 1)
                link(dve.tensor_reduce(row(1), Pr, AX, ALU.add))
                link(dve.reciprocal(row(2), row(1)))
                link(dve.tensor_tensor(Pr, Pr, bc(row(2), NE), ALU.mult))
                for w, (src, oh) in enumerate(((Pr, O1), (A, O2))):
                    link(dve.tensor_reduce(row(3 + w), src, AX, ALU.max))
                    link(dve.tensor_tensor(T, src, bc(row(3 + w), NE), ALU.is_equal))
                    link(dve.tensor_tensor(T, T, rep(E8, GT), ALU.mult))
                    link(dve.tensor_reduce(row(7), T, AX, ALU.min))
                    link(dve.tensor_tensor(oh, rep(E8, GT), bc(row(7), NE), ALU.is_equal))
                    if w == 0:
                        link(dve.scalar_tensor_tensor(A, oh, -2.0, Pr, ALU.mult, ALU.add))
                dve.tensor_tensor(row(5), row(4), row(3), ALU.subtract).then_inc(gap_ready, 1)
                dve.tensor_tensor(A, O1, O2, ALU.add).then_inc(chosen, 1)
                dve.wait_ge(gap_exped, c + 1)
                link(dve.tensor_scalar(row(8), row(6), 1.0, None, ALU.add))
                link(dve.reciprocal(row(9), row(8)))
                link(dve.tensor_scalar(wtop[g][:, 0, :], row(9), 0.5, None, ALU.mult))
                link(dve.tensor_tensor(wtop[g][:, 1, :], wtop[g][:, 0, :], row(6), ALU.mult))
                dve.wait_ge(counted, c + 1)
                cnt = psC[:, 256:512].rearrange("p (a b) -> p a b", b=NE)
                link(dve.tensor_copy(C0, cnt))
                a, b = C0, C1
                s = 1
                while s < GT:
                    own.mark(dve.tensor_copy(b[:, 0:s, :], a[:, 0:s, :]))
                    link(dve.tensor_tensor(b[:, s:GT, :], a[:, s:GT, :], a[:, 0:GT - s, :], ALU.add))
                    a, b = b, a
                    s *= 2
                tot, nt, inc, inc2, base = (tb[:, i, :] for i in range(5))
                nti = tb[:, 5, :].bitcast(I32)
                link(dve.tensor_scalar(tot, a[:, GT - 1, :], float(SLOTS - 1), None, ALU.add))
                link(dve.tensor_copy(nti, tot))
                link(dve.tensor_single_scalar(nti, nti, SLOTS.bit_length() - 1, ALU.arith_shift_right))
                link(dve.tensor_copy(nt, nti))
                link(dve.tensor_copy(inc, nt))
                s = 1
                while s < NE:
                    own.mark(dve.tensor_copy(inc2[:, 0:s], inc[:, 0:s]))
                    link(dve.tensor_tensor(inc2[:, s:NE], inc[:, s:NE], inc[:, 0:NE - s], ALU.add))
                    inc, inc2 = inc2, inc
                    s *= 2
                link(dve.tensor_tensor(base, inc, nt, ALU.subtract))
                link(dve.tensor_scalar(base, base, float(SLOTS), None, ALU.mult))
                link(dve.tensor_tensor(L, a, cnt, ALU.subtract))
                link(dve.tensor_tensor(L, L, psC[:, 0:256].rearrange("p (a b) -> p a b", b=NE), ALU.add))
                link(dve.tensor_tensor(L, L, rep(base, GT), ALU.add))
                for w, oh in enumerate((O1, O2)):
                    link(dve.tensor_tensor(T, oh, L, ALU.mult))
                    link(dve.tensor_reduce(row(10 + w), T, AX, ALU.add))
                dve.tensor_copy(pos[g][:, :, :], rb[:, 10:12, :]).then_inc(placed, 1)
                link(dve.tensor_tensor(jb[:, :, :], bc(JJ, NE), rep(inc, NT), ALU.is_ge))
                link(dve.tensor_reduce(jf[:, :], jb[:, :, :], AX, ALU.add))
                link(dve.tensor_scalar(jf[:, :], jf[:, :], float(NE - 1), None, ALU.min))
                dve.tensor_copy(eid[g][:, :], jf[:, :]).then_inc(tiles_known, 1)

            def relu(c, j, r):
                par = r % 2
                dve.wait_ge(w1_ready, c * NT + j + 1)
                dve.wait_ge(hidden_done, c * NT + j + 1)
                for h in (2, 3):
                    last = dve.tensor_scalar(Hh[par][:, h, :], psHid[par][1][:, (h % 2) * 256:(h % 2) * 256 + 256],
                                             w1c[r][:, HID + h:HID + h + 1], 0.0, ALU.add, ALU.max)
                last.then_inc(relu_dve, 1)

            def rows(c, e, j, jj, r):
                dve.wait_ge(rows_done, c * NT + j + 1)
                wait(dve, slots_out[r], DMAS * (of_ring[r] * c + jj))
                dve.tensor_tensor(Yb[r], psOut[r % 2][:, 0:256].rearrange("p (a b) -> p a b", a=2),
                                  B2[:, ds(e, 1), :].to_broadcast([P, 2, P]), ALU.add).then_inc(rows_ready, 1)

            def experts(c, g):
                dve.wait_ge(tiles_known, c + 1)
                relu(c, 0, 0)
                if g == 0:
                    turns(c, g, 0, TURNS, False)
                else:
                    turns(c, g, 0, PLAIN, False)
                    dve.wait_ge(gathered[0], 2 * DMAS * GT * (c // GROUPS + 1))
                    turns(c, g, PLAIN, TURNS, True)
                e = load_ids(EngineType.DVE, g, NT - 3, 3)
                relu(c, NT - 2, (NT - 2) % TR)
                rows(c, e[0], NT - 3, TURNS, 0)
                if c == GROUPS - 1:
                    norms_of(0)
                relu(c, NT - 1, (NT - 1) % TR)
                if c == GROUPS - 1:
                    norms_root(0, 0)
                rows(c, e[1], NT - 2, TURNS, 1)
                if c == GROUPS - 1:
                    norms_root(0, 1)
                rows(c, e[2], NT - 1, TURNS, 2)

            def turns(c, g, first, end, adding):
                each = GT // (TURNS - PLAIN) // TR
                with dve.Fori(first, end) as jj:
                    if adding:
                        own.enter(jj - first, TR * (each + (c < GROUPS)))
                    for u in range(TR):
                        j = TR * jj + u
                        relu(c, j + 1, (u + 1) % TR)
                        if u == 0:
                            e = load_ids(EngineType.DVE, g, TR * jj, TR)
                        rows(c, e[u], j, jj, u)
                        if adding:
                            t = (jj - first) * (TR * each) + each * u
                            add_rows(c - 1, 0, lambda t: GB[0][:, ds(t, 1)].rearrange("p a w c -> p (a w) c"),
                                     [t + i for i in range(each)])
                    if adding:
                        own.leave(end - first)

            def add_rows(c, g, rows_of, ts):
                for t in ts:
                    xrow = X[:, ds(g * GT + t, 1), :]
                    own.mark(dve.scalar_tensor_tensor(xrow, rows_of(t)[:, 0:1, :], wtop[g][:, 0, ds(t, 1)], xrow,
                                                      ALU.mult, ALU.add))
                dve.wait_ge(o_dve, own.base + own.n)
                for t in ts:
                    xrow = X[:, ds(g * GT + t, 1), :]
                    dve.scalar_tensor_tensor(xrow, rows_of(t)[:, 1:2, :], wtop[g][:, 1, ds(t, 1)], xrow,
                                             ALU.mult, ALU.add).then_inc(combined, 1)
                if c < GROUPS:
                    dve.wait_ge(combined, c * GT + ts[-1] + 1)
                    stats(g * GT + ts[0], len(ts))

            def add_last(c, *parts):
                for q in parts:
                    dve.wait_ge(gathered_last[q], 2 * DMAS * GTILES * (c // GROUPS + 1))
                    add_rows(c, GROUPS - 1, lambda t: last_rows(c, t), range(GTILES * q, GTILES * (q + 1)))

            def norms_of(t0):
                moments(t0, GT)
                v, w = va2[:, :, t0:t0 + GT], nw[:, :].rearrange("p (a b) -> p a b", a=2)[:, :, 0:GT]
                link(dve.tensor_scalar(w[:, 0, :], v[:, 0, :], -LN_EPS, None, ALU.add))
                link(dve.scalar_tensor_tensor(v[:, 1, :], v[:, 0, :], RMS_EPS, w[:, 0, :], ALU.mult, ALU.add))

            def norms_root(t0, i):
                root(va2[:, i, t0:t0 + GT], rs2[:, i, t0:t0 + GT], nw[:, 0:GT])

            def norm(k, dst, r):
                for i in range(QT):
                    t = QT * k + i
                    last = dve.tensor_scalar(dst[:, i:i + 1, :], X[:, ds(t, 1), :], mean[:, ds(t, 1)],
                                             rs2[:, r, ds(t, 1)], ALU.subtract, ALU.mult)
                return last

            def norm_both(k):
                wait(dve, m_unT, k)
                norm(k, UN, 1).then_inc(m_un, 1)

            def norm_one(k):
                wait(dve, m_h, k)
                norm(k, U, 0).then_inc(m_u, 1)

            def conv(k, u, b):
                c = CONV_DVE.index(b)
                dve.wait_ge(m_xr, QT * k + b + 1)
                wait(dve, m_xc, QT * k)
                w = sm("convw")[:, 4 * b:4 * b + 4]
                link(dve.tensor_scalar(CV[:, c, :], XR[u][:, b, 0:512], w[:, 0:1], None, ALU.mult))
                for t in (1, 2):
                    link(dve.scalar_tensor_tensor(CV[:, c, :], XR[u][:, b, t:t + 512], w[:, t:t + 1],
                                                  CV[:, c, :], ALU.mult, ALU.add))
                dve.scalar_tensor_tensor(CV[:, c, :], XR[u][:, b, 3:515], w[:, 3:4],
                                         CV[:, c, :], ALU.mult, ALU.add).then_inc(m_cvd, 1)

            def heads(ap):
                return ap.rearrange("p (h d) -> p h d", h=HEADS)

            def steps_r(k):
                dve.wait_ge(m_ee, k + 1)
                link(dve.tensor_scalar(RD, EE, 2.0, None, ALU.add))
                dve.reciprocal(RD, RD).then_inc(m_rd, 1)

            def sums(k):
                dve.wait_ge(m_col, k + 1)
                link(dve.tensor_copy(C3[:, 0:32], psS[:, 256:288]))
                dve.tensor_tensor(C3[:, 32:48], C3[:, 16:32], C3[:, 0:16], ALU.subtract).then_inc(m_c3, 1)

            def decay(k, i):
                I = QT * k + i
                dve.wait_ge(m_r, I + 1)
                wait(dve, m_ex, I - 1)
                R = (psR, psX)[i % 2]
                dve.tensor_tensor(RM[i % 2], R[:, :].rearrange("p (h l) -> p h l", h=HEADS), rep(MINM, HEADS),
                                  ALU.min).then_inc(m_rm, 1)

            def weigh(k, u, i):
                I = QT * k + i
                dve.wait_ge(m_xt, I + 1)
                wait(dve, m_st, I - 1)
                c = slice(4 * i, 4 * i + 4)
                dve.tensor_tensor(heads(XD[i % 2]), heads(XT[i % 2][:, 0:256]), bc(DT[u][:, c], HD), ALU.mult)
                dve.tensor_tensor(heads(XW[i % 2]), heads(XT[i % 2][:, 0:256]), bc(DTW[u][:, c], HD), ALU.mult
                                  ).then_inc(m_xd, 1)
                dve.wait_ge(m_ex, I + 1)
                dve.tensor_tensor(MT[i % 2], EX[i], rep(XT[i % 2][:, 384:512], HEADS), ALU.mult
                                  ).then_inc(m_mt, 1)

            def rates(k, u):
                dve.wait_ge(m_e3, k + 1)
                link(dve.tensor_tensor(DTW[u], DT[u], E3[u][:, 32:48], ALU.mult))

            def output(k, u, i):
                I = QT * k + i
                first = u == 0 and i == 0
                c = slice(4 * i, 4 * i + 4)
                dve.wait_ge(m_st, I + 1)
                if first:
                    dve.tensor_copy(S, psS[:, 0:256]).then_inc(m_s, 1)
                else:
                    dve.wait_ge(m_s, I)
                    link(dve.tensor_tensor(heads(S), heads(S), bc(E3[u][:, 16 + 4 * i:20 + 4 * i], HD), ALU.mult))
                    dve.tensor_tensor(S, S, psS[:, 0:256], ALU.add).then_inc(m_s, 1)
                dve.wait_ge(m_y, I + 1)
                wait(dve, m_gy, I)
                y = psY[:, 0:256]
                if not first:
                    link(dve.tensor_tensor(heads(YY), heads(psY[:, 256:512]), bc(E3[u][:, c], HD), ALU.mult))
                    link(dve.tensor_tensor(YY, YY, y, ALU.add))
                    y = YY
                wait(dve, m_gt, I - 1)
                wait(dve, m_sq, I - 1)
                dve.tensor_tensor(GY[i % 2], y, SZ[u][:, i, :], ALU.mult).then_inc(m_gy, 1)

            def seed(which, width):
                link(dve.tensor_scalar(NV[which], SQ[which], 1.0 / width, RMS_EPS, ALU.mult, ALU.add))
                y = NY[which].bitcast(I32)
                link(dve.tensor_single_scalar(y, NV[which].bitcast(I32), 1, ALU.arith_shift_right))
                dve.tensor_scalar(y, y, -1.0, MAGIC, ALU.mult, ALU.add).then_inc(m_seed, 1)

            def seed_g(k):
                dve.wait_ge(m_sq, QT * k + QT)
                seed(0, 256)

            def seed_h(k):
                dve.wait_ge(m_sqh, QT * k + QT)
                seed(1, P)

            def join(k):
                dve.wait_ge(m_nw, 2 * k + 1)
                dve.wait_ge(m_o, QT * k + QT)
                dve.wait_ge(m_u, k + 1)
                for i in range(QT):
                    last = dve.scalar_tensor_tensor(HH[:, i, :], psO[:, i * P:(i + 1) * P], NY[0][:, i:i + 1],
                                                    U[:, i, :], ALU.mult, ALU.add)
                last.then_inc(m_h, 1)

            def gated(k, b):
                if b == 0:
                    wait(dve, m_dn, k)
                dve.wait_ge(m_sg, QT * k + b + 1)
                dve.wait_ge(m_up, QT * k + b + 1)
                dve.tensor_tensor(AT[:, b, :], psB[:, :], SG[b % 2], ALU.mult).then_inc(m_at, 1)

            def finish(k):
                dve.wait_ge(m_dn, k + 1)
                dve.wait_ge(m_xh, k + 1)
                dve.tensor_tensor(X[:, ds(QT * k, QT), :], psB[:, :].rearrange("p (a b) -> p a b", a=QT), HH, ALU.add
                                  ).then_inc(m_fx, 1)

            def finished_stats(k):
                dve.wait_ge(m_fx, k + 1)
                stats(QT * k, QT)

            def step(k, u, ahead, now, back):
                n, v = k + 1, 1 - u
                if ahead:
                    norm_both(n)
                if isinstance(k, int) and k == -1:
                    for i in range(TR):
                        dve.wait_ge(slots_out[i], DMAS * of_ring[i] * GROUPS)
                before = back and not (isinstance(k, int) and k < 2)
                if now:
                    rates(k, u)
                if before:
                    finish(k - 2)
                if now:
                    weigh(k, u, 0)
                if before:
                    finished_stats(k - 2)
                if back:
                    seed_g(k - 1)
                if now:
                    output(k, u, 0)
                    weigh(k, u, 1)
                if back:
                    join(k - 1)
                if ahead:
                    conv(n, v, CONV_DVE[0])
                if back:
                    seed_h(k - 1)
                if now:
                    output(k, u, 1)
                    weigh(k, u, 2)
                if ahead:
                    conv(n, v, CONV_DVE[1])
                    steps_r(n)
                if now:
                    output(k, u, 2)
                    weigh(k, u, 3)
                if isinstance(k, int) and k <= LATE:
                    add_last(1, *ADDED_IN.get(k, ()))
                if back:
                    gated(k - 1, 0)
                if ahead:
                    conv(n, v, CONV_DVE[2])
                if back:
                    gated(k - 1, 1)
                if now:
                    output(k, u, 3)
                if back:
                    gated(k - 1, 2)
                if ahead:
                    sums(n)
                    decay(n, 0)
                    decay(n, 1)
                if back:
                    gated(k - 1, 3)
                if ahead:
                    decay(n, 2)
                    decay(n, 3)
                if now:
                    norm_one(k)

            for f in range(2):
                for g in range(GROUPS):
                    route(2 * f + g, g)
                if f == 0:
                    dve.wait_ge(s_wmam, DMAS)
                    for b in range(2):
                        w = wm("wout")[:, b * P:(b + 1) * P]
                        link(dve.tensor_scalar(w, w, sm("ssm")[:, b:b + 1], None, ALU.mult))
                        link(dve.tensor_scalar(DG[:, b, :], IDENT, sm("dcol")[:, b:b + 1], None, ALU.mult))
                    for t in range(4):
                        w = 4 * CONV_PE + t
                        link(dve.tensor_scalar(CT[:, t, :], IDENT, sm("convw")[:, w:w + 1], None, ALU.mult))
                    dve.wait_ge(m_alog, 1)
                    dve.tensor_scalar(ANEG[:, :], ANEG[:, :], -1.0, None, ALU.mult).then_inc(m_set, 1)
                dve.wait_ge(s_w1, DMAS * 3)
                for g in range(GROUPS):
                    experts(2 * f + g, g)
                if f == 1:
                    add_last(2 * f + 1, *range(GT // GTILES))
                if f == 0:
                    link(dve.memset(XR[0][:, :, 0:3], 0.0))
                    for k in range(-1, LATE + 1):
                        step(k, k % 2, True, k >= 0, k >= 1)
                    norms_of(GT)
                    norms_root(GT, 0)
                    norms_root(GT, 1)
                    with dve.Fori(0, (QUADS - 2 - LATE) // 2) as b:
                        own.enter(b, DVE_PER)
                        for u in (1, 0):
                            step(2 * b + LATE + (2 - u), u, True, True, True)
                        own.leave((QUADS - 2 - LATE) // 2)
                    step(QUADS - 1, 1, False, True, True)
                    layer_norm(GROUPS, 0)
                    step(QUADS, 0, False, False, True)
                    finish(QUADS - 1)
                    finished_stats(QUADS - 1)


def kernel(L0_attn_x, L0_attn_prenorm_w, L0_attn_postnorm_w, L0_attn_in_proj_w, L0_attn_conv_w, L0_attn_conv_b,
           L0_attn_dt_bias, L0_attn_A_log, L0_attn_D_param, L0_attn_ssm_norm_w, L0_attn_out_proj_w, L0_attn_gate_w,
           L0_attn_up_w, L0_attn_down_w, L0_ffn_W1, L0_ffn_b1, L0_ffn_W2, L0_ffn_b2, L0_ffn_Wg, L0_ffn_bg):
    import numpy as np
    import concourse.bacc as bacc
    from concourse.bass_utils import run_bass_kernel_spmd

    f = np.float32
    p = np.arange(P)
    cst = np.zeros((P, C_END), f)
    cst[:, C_ID:C_ID + P] = np.eye(P)
    cst[:, C_TRI:C_TRI + P] = p[:, None] <= p[None, :]
    cst[:, C_LOW:C_LOW + P] = p[:, None] > p[None, :]
    cst[:, C_UP:C_UP + P] = p[:, None] < p[None, :]
    cst[:, C_ONE:C_ONE + P] = 1.0
    cst[:, C_MIN:C_MIN + P] = np.where(p[:, None] <= p[None, :], 0.0, NEG)
    cst[:, C_E8:C_E8 + NE] = np.arange(NE) - NE
    cst[:, C_J:C_J + NT] = np.arange(NT)

    def rows(a):
        a = np.asarray(a)
        return np.broadcast_to(a.reshape(1, -1), (P, a.size))

    def cols(a, n):
        return np.asarray(a).reshape(n, P).T

    small = np.concatenate([
        np.asarray(L0_ffn_Wg), rows(L0_ffn_bg), rows(L0_attn_dt_bias), rows(L0_attn_A_log),
        np.repeat(np.asarray(L0_attn_D_param), HD).reshape(2, P).T,
        np.asarray(L0_attn_conv_w).reshape(4, P, 4).transpose(1, 0, 2).reshape(P, 16), cols(L0_attn_conv_b, 4),
        cols(L0_attn_prenorm_w, 1), cols(L0_attn_postnorm_w, 1), cols(L0_attn_ssm_norm_w, 2)], axis=1)
    win = np.asarray(L0_attn_in_proj_w).T
    wmam = np.concatenate([
        win[:, 256:768], win[:, 0:256], win[:, 768:772],
        np.asarray(L0_attn_out_proj_w).reshape(P, 2, P).transpose(2, 1, 0).reshape(P, 256),
        np.asarray(L0_attn_gate_w).T, np.asarray(L0_attn_up_w).T,
        np.asarray(L0_attn_down_w).reshape(P, 4, P).transpose(2, 1, 0).reshape(P, 512)], axis=1)
    w1p = np.concatenate([np.asarray(L0_ffn_W1).transpose(1, 0, 2),
                          np.asarray(L0_ffn_b1).reshape(NE, HB, P).transpose(2, 0, 1)], axis=2)
    w2p = np.asarray(L0_ffn_W2).reshape(NE, HB, P, P).transpose(2, 0, 1, 3)
    b2p = np.broadcast_to(np.asarray(L0_ffn_b2).reshape(1, NE, P), (P, NE, P))
    arrays = {"x": np.asarray(L0_attn_x), "cst": cst, "small": small, "wmam": wmam, "w1p": w1p, "w2p": w2p, "b2p": b2p}
    nc = bacc.Bacc("TRN2", target_bir_lowering=False, num_devices=1)
    args, given = [], {}
    for name, a in arrays.items():
        given[name] = np.ascontiguousarray(a)
        args.append(nc.dram_tensor(name, a.shape, mybir.dt.from_np(a.dtype), kind="ExternalInput").ap())
    args.append(nc.dram_tensor("out", (SEQS, SEQ, P), F32, kind="ExternalOutput").ap())
    macaron(nc, *args)
    r = run_bass_kernel_spmd(nc, [given], core_ids=[0])
    return r.results[0]["out"]
```
